# Optimizing a Trainium2 kernel written in Bass

```python
import numpy as np
import jax
import jax.numpy as jnp

def _softmax(x, axis=-1):
    return jax.nn.softmax(x, axis=axis)

def _gelu(x):
    return jax.nn.gelu(x, approximate=True)

def _silu(x):
    return jax.nn.silu(x)

def _sigmoid(x):
    return jax.nn.sigmoid(x)

def _layernorm(x, axis=-1, eps=1e-05):
    m = jnp.mean(x, axis=axis, keepdims=True)
    v = jnp.var(x, axis=axis, keepdims=True)
    return (x - m) / jnp.sqrt(v + eps)

def _scatter_add(tgt, idx, src, axis=0):
    return tgt.at[idx].add(src)

def _segment_sum(src, seg, n):
    return jax.ops.segment_sum(src, seg, n)
kernel_name = 'mk_flamingo_gated_d2_seqx_r4_0006f3'

def setup_inputs(seed: int=0):
    np.random.seed(seed)
    _w = jnp.asarray

    def _rec_inputs():
        import jax
        import jax.numpy as jnp
        _rk = jax.random.key(seed)
        x = 0.0001212 + 1 * jax.random.normal(jax.random.fold_in(_rk, 1), (16, 256, 512), jnp.float32)
        _lenS = 256 - jax.random.randint(jax.random.fold_in(_rk, 7), (16,), 0, max(1, 256 // 4) + 1, jnp.int32)
        _lenS2 = 256 - jax.random.randint(jax.random.fold_in(_rk, 8), (16,), 0, max(1, 256 // 4) + 1, jnp.int32)
        _ctx_2048P = jax.random.normal(jax.random.fold_in(_rk, 11), (16, 16, 512), jnp.float32)
        _ctx_2048c = jax.random.dirichlet(jax.random.fold_in(_rk, 511), 0.3 * jnp.ones((16,), jnp.float32), (16, 256))
        _ctx_2048t = jnp.einsum('bsk,bkd->bsd', _ctx_2048c, _ctx_2048P)
        _ctx_2048t = _ctx_2048t * jax.lax.rsqrt(jnp.mean(jnp.square(_ctx_2048t)) + 1e-12) * 0.953939
        ctx_2048 = 0.000173663 + 1.0001 * (_ctx_2048t + 0.3 * jax.random.normal(jax.random.fold_in(_rk, 611), (16, 256, 512), jnp.float32))
        _g = jax.random.normal(jax.random.fold_in(_rk, 9001), (2, 2), jnp.float32)
        _g = jnp.sign(_g) * jnp.maximum(jnp.abs(_g), 1.0) + (_g == 0) * 1.0
        g_xattn = _g[0]
        g_ffn = _g[1]
        return (x, ctx_2048, g_xattn, g_ffn)
    x, ctx_2048, g_xattn, g_ffn = _rec_inputs()

    def _L0_xattn_setup():
        import jax, jax.numpy as jnp
        import numpy as np
        B_DIM, T_DIM, C_DIM = (16, 256, 512)

        def _wkv(w, u, k, v):
            Bn, Tn, Cn = k.shape
            NEG_INF = jnp.float32(-1e+38)

            def step(carry, kv_t):
                p, q, o = carry
                kt, vt = kv_t
                no = jnp.maximum(o, u + kt)
                A = jnp.exp(o - no)
                E = jnp.exp(u + kt - no)
                y = (A * p + E * vt) / (A * q + E)
                no2 = jnp.maximum(w + o, kt)
                A2 = jnp.exp(w + o - no2)
                E2 = jnp.exp(kt - no2)
                return ((A2 * p + E2 * vt, A2 * q + E2, no2), y)
            init = (jnp.zeros((Bn, Cn), k.dtype), jnp.zeros((Bn, Cn), k.dtype), jnp.full((Bn, Cn), NEG_INF, k.dtype))
            kT = jnp.moveaxis(k, 1, 0)
            vT = jnp.moveaxis(v, 1, 0)
            _, yT = jax.lax.scan(step, init, (kT, vT))
            return jnp.moveaxis(yT, 0, 1)
        key = jax.random.key(seed)
        k1, k2, k3, k4 = jax.random.split(key, 4)
        w = -jnp.exp(jax.random.normal(k1, (C_DIM,), jnp.float32))
        u = jax.random.normal(k2, (C_DIM,), jnp.float32)
        k = jax.random.normal(k3, (B_DIM, T_DIM, C_DIM), jnp.float32)
        v = jax.random.normal(k4, (B_DIM, T_DIM, C_DIM), jnp.float32)
        return {'B': B_DIM, 'T': T_DIM, 'C': C_DIM, 'w': w, 'u': u, 'k': k, 'v': v}
    _L0_xattn_all = _L0_xattn_setup()
    _L0_xattn_in = {k: v for k, v in _L0_xattn_all.items() if k in ('w', 'u')}
    del _L0_xattn_all

    def _L0_ffn_setup():
        import jax, jax.numpy as jnp
        import numpy as np
        N_EXPERTS = 8
        TOP_K = 2
        C = 512
        H = 256
        HS = 512
        B, T = (1, 128)
        SCALE = 0.02
        key = jax.random.key(seed)
        ks = jax.random.split(key, 10)
        x = jax.random.normal(ks[0], (B, T, C), dtype=jnp.float32)
        gate_w = jax.random.normal(ks[1], (N_EXPERTS, C), dtype=jnp.float32) * SCALE
        w_gate = jax.random.normal(ks[2], (N_EXPERTS, H, C), dtype=jnp.float32) * SCALE
        w_up = jax.random.normal(ks[3], (N_EXPERTS, H, C), dtype=jnp.float32) * SCALE
        w_down = jax.random.normal(ks[4], (N_EXPERTS, C, H), dtype=jnp.float32) * SCALE
        sh_gate = jax.random.normal(ks[5], (HS, C), dtype=jnp.float32) * SCALE
        sh_up = jax.random.normal(ks[6], (HS, C), dtype=jnp.float32) * SCALE
        sh_down = jax.random.normal(ks[7], (C, HS), dtype=jnp.float32) * SCALE
        se_gate_w = jax.random.normal(ks[8], (1, C), dtype=jnp.float32) * SCALE
        return {'x': x, 'gate_w': gate_w, 'w_gate': w_gate, 'w_up': w_up, 'w_down': w_down, 'sh_gate': sh_gate, 'sh_up': sh_up, 'sh_down': sh_down, 'se_gate_w': se_gate_w}
    _L0_ffn_all = _L0_ffn_setup()
    _L0_ffn_in = {k: v for k, v in _L0_ffn_all.items() if k in ('gate_w', 'w_gate', 'w_up', 'w_down', 'sh_gate', 'sh_up', 'sh_down', 'se_gate_w')}
    del _L0_ffn_all

    def _L1_xattn_setup():
        import jax, jax.numpy as jnp
        import numpy as np
        HIDDEN = 512
        NUM_HEADS = 16
        HEAD_DIM = HIDDEN // NUM_HEADS
        CHUNK = 256
        SCALE = HEAD_DIM ** (-0.5)

        def _chunked_causal_attention(q, k, v):
            B, H, S, D = q.shape
            n_chunks = S // CHUNK
            kc = k.reshape(B, H, n_chunks, CHUNK, D).transpose(2, 0, 1, 3, 4)
            vc = v.reshape(B, H, n_chunks, CHUNK, D).transpose(2, 0, 1, 3, 4)
            j0s = jnp.arange(n_chunks) * CHUNK
            q_idx = jnp.arange(S)[:, None]
            k_off = jnp.arange(CHUNK)[None, :]
            out0 = jnp.zeros_like(q)
            m0 = jnp.full((B, H, S, 1), -jnp.inf, dtype=q.dtype)
            s0 = jnp.zeros((B, H, S, 1), dtype=q.dtype)

            def step(carry, inputs):
                out, m, s = carry
                kj, vj, j0 = inputs
                scores = jnp.einsum('bhqd,bhkd->bhqk', q, kj) * SCALE
                causal = j0 + k_off > q_idx
                scores = jnp.where(causal[None, None], -jnp.inf, scores)
                chunk_max = scores.max(axis=-1, keepdims=True)
                new_m = jnp.maximum(m, chunk_max)
                exp_old = jnp.exp(m - new_m)
                exp_c = jnp.exp(scores - new_m)
                new_s = s * exp_old + exp_c.sum(axis=-1, keepdims=True)
                out = out * (s / new_s) * exp_old + jnp.einsum('bhqk,bhkd->bhqd', exp_c / new_s, vj)
                return ((out, new_m, new_s), None)
            (out, _, _), _ = jax.lax.scan(step, (out0, m0, s0), (kc, vc, j0s))
            return out
        key = jax.random.key(seed)
        kq, kk, kv = jax.random.split(key, 3)
        B, S = (2, 1024)
        return {'query': jax.random.normal(kq, (B, S, HIDDEN), dtype=jnp.float32), 'key': jax.random.normal(kk, (B, S, HIDDEN), dtype=jnp.float32), 'value': jax.random.normal(kv, (B, S, HIDDEN), dtype=jnp.float32)}
    _L1_xattn_all = _L1_xattn_setup()
    _L1_xattn_in = {k: v for k, v in _L1_xattn_all.items() if k in ()}
    del _L1_xattn_all

    def _L1_ffn_setup():
        import jax, jax.numpy as jnp
        import numpy as np
        E, K, H, I = (64, 6, 512, 352)
        NS = 2
        IS = NS * I
        CAP = 64
        T_TOKENS = (1, 256)
        SCALE = 0.02

        def _moe_infer(x, gate_w, w_gate, w_up, w_down):
            T = x.shape[0]
            TK = T * K
            logits = x @ gate_w.T
            scores = jax.nn.softmax(logits, axis=-1)
            topk_w, topk_i = jax.lax.top_k(scores, K)
            flat_i = topk_i.reshape(-1)
            flat_w = topk_w.reshape(-1)
            token_ids = jnp.arange(TK, dtype=jnp.int32) // K
            order = jnp.argsort(flat_i)
            sorted_e = flat_i[order]
            counts = jnp.bincount(flat_i, length=E)
            starts = jnp.concatenate([jnp.zeros((1,), counts.dtype), jnp.cumsum(counts)[:-1]])
            pos_sorted = jnp.arange(TK) - starts[sorted_e]
            pos = jnp.zeros((TK,), jnp.int32).at[order].set(pos_sorted.astype(jnp.int32))
            valid = pos < CAP
            slot = jnp.where(valid, pos, CAP)
            buf = jnp.zeros((E, CAP + 1, H), x.dtype).at[flat_i, slot].set(x[token_ids])
            g = jnp.einsum('ech,ehi->eci', buf, w_gate)
            u = jnp.einsum('ech,ehi->eci', buf, w_up)
            y = jnp.einsum('eci,eih->ech', jax.nn.silu(g) * u, w_down)
            out_slots = y[flat_i, slot] * (flat_w * valid)[:, None]
            return out_slots.reshape(T, K, H).sum(axis=1)
        key = jax.random.key(seed)
        ks = jax.random.split(key, 8)
        f32 = jnp.float32
        return {'hidden_states': jax.random.normal(ks[0], (*T_TOKENS, H), f32), 'gate_w': jax.random.normal(ks[1], (E, H), f32) * SCALE, 'w_gate': jax.random.normal(ks[2], (E, H, I), f32) * SCALE, 'w_up': jax.random.normal(ks[3], (E, H, I), f32) * SCALE, 'w_down': jax.random.normal(ks[4], (E, I, H), f32) * SCALE, 'sw_gate': jax.random.normal(ks[5], (H, IS), f32) * SCALE, 'sw_up': jax.random.normal(ks[6], (H, IS), f32) * SCALE, 'sw_down': jax.random.normal(ks[7], (IS, H), f32) * SCALE}
    _L1_ffn_all = _L1_ffn_setup()
    _L1_ffn_in = {k: v for k, v in _L1_ffn_all.items() if k in ('gate_w', 'w_gate', 'w_up', 'w_down', 'sw_gate', 'sw_up', 'sw_down')}
    del _L1_ffn_all
    return {'x': x, 'ctx_2048': ctx_2048, 'g_xattn': g_xattn, 'g_ffn': g_ffn, 'L0_xattn_w': _L0_xattn_in['w'], 'L0_xattn_u': _L0_xattn_in['u'], 'L0_ffn_gate_w': _L0_ffn_in['gate_w'], 'L0_ffn_w_gate': _L0_ffn_in['w_gate'], 'L0_ffn_w_up': _L0_ffn_in['w_up'], 'L0_ffn_w_down': _L0_ffn_in['w_down'], 'L0_ffn_sh_gate': _L0_ffn_in['sh_gate'], 'L0_ffn_sh_up': _L0_ffn_in['sh_up'], 'L0_ffn_sh_down': _L0_ffn_in['sh_down'], 'L0_ffn_se_gate_w': _L0_ffn_in['se_gate_w'], 'L1_ffn_gate_w': _L1_ffn_in['gate_w'], 'L1_ffn_w_gate': _L1_ffn_in['w_gate'], 'L1_ffn_w_up': _L1_ffn_in['w_up'], 'L1_ffn_w_down': _L1_ffn_in['w_down'], 'L1_ffn_sw_gate': _L1_ffn_in['sw_gate'], 'L1_ffn_sw_up': _L1_ffn_in['sw_up'], 'L1_ffn_sw_down': _L1_ffn_in['sw_down']}

def reference(x, ctx_2048, g_xattn, g_ffn, L0_xattn_w, L0_xattn_u, L0_ffn_gate_w, L0_ffn_w_gate, L0_ffn_w_up, L0_ffn_w_down, L0_ffn_sh_gate, L0_ffn_sh_up, L0_ffn_sh_down, L0_ffn_se_gate_w, L1_ffn_gate_w, L1_ffn_w_gate, L1_ffn_w_up, L1_ffn_w_down, L1_ffn_sw_gate, L1_ffn_sw_up, L1_ffn_sw_down):
    import jax
    import jax.numpy as jnp

    def _L0_xattn_ref(B, T, C, w, u, k, v):
        import jax, jax.numpy as jnp
        import numpy as np
        B_DIM, T_DIM, C_DIM = (16, 256, 512)

        def _wkv(w, u, k, v):
            Bn, Tn, Cn = k.shape
            NEG_INF = jnp.float32(-1e+38)

            def step(carry, kv_t):
                p, q, o = carry
                kt, vt = kv_t
                no = jnp.maximum(o, u + kt)
                A = jnp.exp(o - no)
                E = jnp.exp(u + kt - no)
                y = (A * p + E * vt) / (A * q + E)
                no2 = jnp.maximum(w + o, kt)
                A2 = jnp.exp(w + o - no2)
                E2 = jnp.exp(kt - no2)
                return ((A2 * p + E2 * vt, A2 * q + E2, no2), y)
            init = (jnp.zeros((Bn, Cn), k.dtype), jnp.zeros((Bn, Cn), k.dtype), jnp.full((Bn, Cn), NEG_INF, k.dtype))
            kT = jnp.moveaxis(k, 1, 0)
            vT = jnp.moveaxis(v, 1, 0)
            _, yT = jax.lax.scan(step, init, (kT, vT))
            return jnp.moveaxis(yT, 0, 1)
        return _wkv(w, u, k, v)

    def _L0_ffn_ref(x, gate_w, w_gate, w_up, w_down, sh_gate, sh_up, sh_down, se_gate_w):
        import jax, jax.numpy as jnp
        import numpy as np
        N_EXPERTS = 8
        TOP_K = 2
        C = 512
        H = 256
        HS = 512
        B, T = (1, 128)
        SCALE = 0.02
        Bb, Tt, Cc = x.shape
        xf = x.reshape(-1, Cc)
        scores = xf @ gate_w.T
        ew, ei = jax.lax.top_k(scores, TOP_K)
        ew = jax.nn.softmax(ew, axis=-1)
        x1 = jax.nn.silu(jnp.einsum('td,ehd->teh', xf, w_gate))
        x3 = jnp.einsum('td,ehd->teh', xf, w_up)
        expert_out = jnp.einsum('teh,edh->ted', x1 * x3, w_down)
        onehot = jax.nn.one_hot(ei, N_EXPERTS, dtype=ew.dtype)
        comb = jnp.einsum('ta,tae->te', ew, onehot)
        routed = jnp.einsum('te,ted->td', comb, expert_out)
        shared = jax.nn.silu(xf @ sh_gate.T) * (xf @ sh_up.T) @ sh_down.T
        sgate = jax.nn.sigmoid(xf @ se_gate_w.T)
        return (routed + sgate * shared).reshape(Bb, Tt, Cc)

    def _L1_xattn_ref(query, key, value):
        import jax, jax.numpy as jnp
        import numpy as np
        HIDDEN = 512
        NUM_HEADS = 16
        HEAD_DIM = HIDDEN // NUM_HEADS
        CHUNK = 256
        SCALE = HEAD_DIM ** (-0.5)

        def _chunked_causal_attention(q, k, v):
            B, H, S, D = q.shape
            n_chunks = S // CHUNK
            kc = k.reshape(B, H, n_chunks, CHUNK, D).transpose(2, 0, 1, 3, 4)
            vc = v.reshape(B, H, n_chunks, CHUNK, D).transpose(2, 0, 1, 3, 4)
            j0s = jnp.arange(n_chunks) * CHUNK
            q_idx = jnp.arange(S)[:, None]
            k_off = jnp.arange(CHUNK)[None, :]
            out0 = jnp.zeros_like(q)
            m0 = jnp.full((B, H, S, 1), -jnp.inf, dtype=q.dtype)
            s0 = jnp.zeros((B, H, S, 1), dtype=q.dtype)

            def step(carry, inputs):
                out, m, s = carry
                kj, vj, j0 = inputs
                scores = jnp.einsum('bhqd,bhkd->bhqk', q, kj) * SCALE
                causal = j0 + k_off > q_idx
                scores = jnp.where(causal[None, None], -jnp.inf, scores)
                chunk_max = scores.max(axis=-1, keepdims=True)
                new_m = jnp.maximum(m, chunk_max)
                exp_old = jnp.exp(m - new_m)
                exp_c = jnp.exp(scores - new_m)
                new_s = s * exp_old + exp_c.sum(axis=-1, keepdims=True)
                out = out * (s / new_s) * exp_old + jnp.einsum('bhqk,bhkd->bhqd', exp_c / new_s, vj)
                return ((out, new_m, new_s), None)
            (out, _, _), _ = jax.lax.scan(step, (out0, m0, s0), (kc, vc, j0s))
            return out
        B, S, _ = query.shape
        q = query.reshape(B, S, NUM_HEADS, HEAD_DIM).transpose(0, 2, 1, 3)
        k = key.reshape(B, S, NUM_HEADS, HEAD_DIM).transpose(0, 2, 1, 3)
        v = value.reshape(B, S, NUM_HEADS, HEAD_DIM).transpose(0, 2, 1, 3)
        out = _chunked_causal_attention(q, k, v)
        return out.transpose(0, 2, 1, 3).reshape(B, S, HIDDEN)

    def _L1_ffn_ref(hidden_states, gate_w, w_gate, w_up, w_down, sw_gate, sw_up, sw_down):
        import jax, jax.numpy as jnp
        import numpy as np
        E, K, H, I = (64, 6, 512, 352)
        NS = 2
        IS = NS * I
        CAP = 64
        T_TOKENS = (1, 256)
        SCALE = 0.02

        def _moe_infer(x, gate_w, w_gate, w_up, w_down):
            T = x.shape[0]
            TK = T * K
            logits = x @ gate_w.T
            scores = jax.nn.softmax(logits, axis=-1)
            topk_w, topk_i = jax.lax.top_k(scores, K)
            flat_i = topk_i.reshape(-1)
            flat_w = topk_w.reshape(-1)
            token_ids = jnp.arange(TK, dtype=jnp.int32) // K
            order = jnp.argsort(flat_i)
            sorted_e = flat_i[order]
            counts = jnp.bincount(flat_i, length=E)
            starts = jnp.concatenate([jnp.zeros((1,), counts.dtype), jnp.cumsum(counts)[:-1]])
            pos_sorted = jnp.arange(TK) - starts[sorted_e]
            pos = jnp.zeros((TK,), jnp.int32).at[order].set(pos_sorted.astype(jnp.int32))
            valid = pos < CAP
            slot = jnp.where(valid, pos, CAP)
            buf = jnp.zeros((E, CAP + 1, H), x.dtype).at[flat_i, slot].set(x[token_ids])
            g = jnp.einsum('ech,ehi->eci', buf, w_gate)
            u = jnp.einsum('ech,ehi->eci', buf, w_up)
            y = jnp.einsum('eci,eih->ech', jax.nn.silu(g) * u, w_down)
            out_slots = y[flat_i, slot] * (flat_w * valid)[:, None]
            return out_slots.reshape(T, K, H).sum(axis=1)
        orig_shape = hidden_states.shape
        x = hidden_states.reshape(-1, orig_shape[-1])
        y = _moe_infer(x, gate_w, w_gate, w_up, w_down).reshape(orig_shape)
        shared = jax.nn.silu(hidden_states @ sw_gate) * (hidden_states @ sw_up) @ sw_down
        return y + shared
    x = x + jnp.tanh(g_xattn[0]) * _L0_xattn_ref(16, 256, 512, L0_xattn_w, L0_xattn_u, _layernorm(x, axis=-1), ctx_2048)
    x = x + jnp.tanh(g_ffn[0]) * _L0_ffn_ref(_layernorm(x, axis=-1), L0_ffn_gate_w, L0_ffn_w_gate, L0_ffn_w_up, L0_ffn_w_down, L0_ffn_sh_gate, L0_ffn_sh_up, L0_ffn_sh_down, L0_ffn_se_gate_w)
    x = x + jnp.tanh(g_xattn[1]) * _L1_xattn_ref(_layernorm(x, axis=-1), ctx_2048, ctx_2048)
    x = x + jnp.tanh(g_ffn[1]) * _L1_ffn_ref(_layernorm(x, axis=-1), L1_ffn_gate_w, L1_ffn_w_gate, L1_ffn_w_up, L1_ffn_w_down, L1_ffn_sw_gate, L1_ffn_sw_up, L1_ffn_sw_down)
    return x

_drawn_inputs = setup_inputs


def setup_inputs(seed=0):
    import zlib

    import numpy as np

    out = dict(_drawn_inputs(seed))
    spreads = {'g_ffn': (-1.0, 0.6)}
    factors = {'L0_ffn_gate_w': 3.709,
     'L0_ffn_w_gate': 3.277,
     'L0_ffn_w_up': 3.219,
     'L0_ffn_w_down': 3.218,
     'L0_ffn_sh_gate': 3.262,
     'L0_ffn_sh_up': 3.198,
     'L0_ffn_sh_down': 3.196,
     'L0_ffn_se_gate_w': 8.0,
     'L1_ffn_gate_w': 8.0,
     'L1_ffn_w_gate': 8.0,
     'L1_ffn_w_up': 8.0,
     'L1_ffn_w_down': 8.0,
     'L1_ffn_sw_gate': 7.673,
     'L1_ffn_sw_up': 7.509,
     'L1_ffn_sw_down': 7.494}
    for name, (base, spread) in spreads.items():
        noise = np.random.default_rng([zlib.crc32(name.encode()), seed]).standard_normal(out[name].shape)
        drawn = base * np.exp(spread * noise) if base else spread * noise
        out[name] = jnp.asarray(drawn.astype(out[name].dtype))
    for name, factor in factors.items():
        out[name] = (out[name] * factor).astype(out[name].dtype)
    return out
```

```python
import numpy as np
import concourse.bass as bass
from concourse import mybir
from contextlib import ExitStack

F32 = mybir.dt.float32
BF16 = mybir.dt.bfloat16
I32 = mybir.dt.int32
U32 = mybir.dt.uint32
ALU = mybir.AluOpType
ACT = mybir.ActivationFunctionType
AX = mybir.AxisListType

P = 128
B, T, C = 16, 256, 512
N = B * T
KC = C // P
TJ = T // P
EPS = 1e-5
DUMMY = P
E0, H0, S0, K0 = 8, 256, 512, 2
E1, H1, S1, K1, CAP = 64, 352, 704, 6, 64
TILES0 = N * K0 // P + E0
UNUSED = 2 * K0 * N
LIST0 = E0 * N + P
HEADS, D = 16, 32
M0 = S0 // P
FB0 = M0 + TJ
M1 = -(-S1 // P)
FB1 = M1 + TJ
POST_STEPS1 = 26
WAYS1, SLOTS1, AHEAD1 = 8, 4, 4
WAYS0, SLOTS0, AHEAD0 = 8, 4, 3
WKV_STEPS, POST_STEPS0 = 26, 24
UNITS = HEADS // 2
PRE_AT = 4
USES = UNITS + 3
NEG = -1e30
BEFORE_ALL = -1e38


def wait(eng, sem, value):
    if not isinstance(value, int) or value > 0:
        eng.wait_ge(sem, value)


def alone(eng):
    eng.nop(nofuse=True)


class Chain:

    def __init__(self, eng, sem, per_turn):
        self.eng, self.sem, self.per, self.n, self.base = eng, sem, per_turn, 0, 0

    def turn(self, i):
        assert self.n in (0, self.per), (self.n, self.per)
        self.n, self.base = 0, i * self.per

    def resume(self, i):
        self.base = i * self.per

    def did(self, ins):
        ins.then_inc(self.sem, 1)
        self.n += 1
        return self.n

    def need(self, n):
        self.eng.wait_ge(self.sem, self.base + n)


class Turn:

    def __init__(self, i, round, s, count, ways=2):
        self.i, self.round, self.s, self.count, self.ways = i, round, s, count, ways
        self.first = isinstance(i, int) and i == 0
        self.last = isinstance(i, int) and i == count - 1
        self.third = not isinstance(i, int) or i >= 2

    def before(self):
        wrap = self.s == 0
        return Turn(self.i - 1, self.round - wrap, (self.s - 1) % self.ways, self.count, self.ways)

    def after(self):
        wrap = self.s == self.ways - 1
        return Turn(self.i + 1, self.round + wrap, (self.s + 1) % self.ways, self.count, self.ways)


def first(count, ways=2):
    return Turn(0, 0, 0, count, ways)


def last(count, ways=2):
    return Turn(count - 1, count // ways - 1, ways - 1, count, ways)


def turns(eng, count, turn, ways=2):
    assert count % ways == 0
    for n in range(ways + 1):
        turn(Turn(n, n // ways, n % ways, count, ways))
    with eng.Fori(1, count // ways - 1) as j:
        for n in range(1, ways + 1):
            turn(Turn(ways * j + n, j + n // ways, n % ways, count, ways))
    for n in range(count - ways + 1, count):
        turn(Turn(n, n // ways, n % ways, count, ways))


def rounds(eng, count, turn, ways):
    for n in range(ways):
        turn(Turn(n, 0, n, count, ways))
    with eng.Fori(1, count // ways) as j:
        for n in range(ways):
            turn(Turn(ways * j + n, j, n, count, ways))


FIRST, LAST = first(B), last(B)


class Memory:

    def __init__(self, nc, phase):
        self.nc, self.phase, self.stack = nc, phase, ExitStack()

    def sb(self, name, shape, dt=F32):
        return self.stack.enter_context(self.nc.sbuf_tensor(self.phase + name, shape, dt))

    def ps(self, name, shape=(P, 512), dt=F32):
        return self.stack.enter_context(self.nc.psum_tensor(self.phase + name, list(shape), dt))

    def sem(self, name):
        return self.stack.enter_context(self.nc.semaphore(self.phase + name))

    def __enter__(self):
        return self

    def __exit__(self, *a):
        self.stack.close()


def rows(dram, b):
    return dram[bass.ds(b.i * T, T), :].rearrange("(j p) c -> p j c", p=P)


def setup(nc, io, c):
    with Memory(nc, "setup_") as m:
        ones_row = m.sb("ones_row", [1, P])
        gates_in = m.sb("gates_in", [1, 4])
        zeros = m.sb("zeros", [P, C])
        slot_no = m.sb("slot_no", [P, LIST0 // P], I32)
        slot_low = m.sb("slot_low", [P, LIST0 // P], I32)
        fill = m.sb("fill", [P, LIST0 // P, 3], I32)
        fill1 = m.sb("fill1", [P, E1 * CAP // P, 2], I32)
        gates_ps = m.ps("gates_ps")
        gates_in_s, const_s, made, bc_s, dve_s, stored = (m.sem(x) for x in (
            "gates_loaded", "consts_loaded", "pool_made", "gates_broadcast", "dve_setup", "setup_stored"))
        with nc.Block() as block:
            @block.sync
            def _(sp):
                sp.dma_start(gates_in[:, 0:2], io["g_xattn"][None, :]).then_inc(gates_in_s, 16)
                sp.dma_start(gates_in[:, 2:4], io["g_ffn"][None, :]).then_inc(gates_in_s, 16)
                sp.dma_start(c.w[:], io["w"].rearrange("(k p) -> p k", p=P), allow_slow_non_contiguous=True).then_inc(const_s, 16)
                sp.dma_start(c.u[:], io["u"].rearrange("(k p) -> p k", p=P), allow_slow_non_contiguous=True).then_inc(const_s, 16)
                sp.wait_ge(made, 3)
                for d in (io["xn0"], io["xn1"], io["out"]):
                    sp.dma_start(d[N:N + DUMMY, :], zeros[:]).then_inc(stored, 16)
                sp.wait_ge(dve_s, 7)
                sp.dma_start(io["list0"].rearrange("(p j) c -> p (j c)", p=P),
                             fill[:].rearrange("p j c -> p (j c)")).then_inc(stored, 16)
                sp.dma_start(io["list1"].rearrange("(p j) c -> p (j c)", p=P),
                             fill1[:].rearrange("p j c -> p (j c)")).then_inc(stored, 16)
                sp.wait_ge(const_s, 32)
                sp.wait_ge(stored, 5 * 16)

            @block.gpsimd
            def _(pool):
                nc.gpsimd.memset(c.ident[:], 0.0).then_inc(made, 1)
                nc.gpsimd.memset(ones_row[:], 1.0).then_inc(made, 1)
                nc.gpsimd.memset(zeros[:], 0.0).then_inc(made, 1)
                nc.gpsimd.memset(c.before[:], 1.0).then_inc(made, 1)
                nc.gpsimd.memset(c.ones[:], 1.0).then_inc(made, 1)
                nc.gpsimd.memset(c.causal[:], 0.0).then_inc(made, 1)
                nc.gpsimd.memset(c.half_power[:], -0.5).then_inc(made, 1)
                nc.gpsimd.iota(slot_no[:], [[1, LIST0 // P]], base=0, channel_multiplier=LIST0 // P).then_inc(made, 1)
                nc.gpsimd.iota(c.expert_no[:], [[1, E1]], base=0, channel_multiplier=0,
                               allow_small_or_imprecise_dtypes=True).then_inc(made, 1)
                nc.gpsimd.iota(c.token_no[:], [[P, TJ]], base=0, channel_multiplier=1,
                               allow_small_or_imprecise_dtypes=True).then_inc(made, 1)
                nc.gpsimd.iota(c.tile_no[:], [[1, TILES0]], base=0, channel_multiplier=0,
                               allow_small_or_imprecise_dtypes=True).then_inc(made, 1)
                nc.gpsimd.memset(fill[:, :, 2], 0).then_inc(made, 1)
                nc.gpsimd.memset(fill1[:], 0).then_inc(made, 1)
                pool.wait_ge(made, 6)
                nc.gpsimd.affine_select(out=c.ident[:], in_=c.ident[:], compare_op=ALU.not_equal, fill=1.0,
                                        base=0, pattern=[[-1, P]], channel_multiplier=1).then_inc(made, 1)
                nc.gpsimd.affine_select(out=c.before[:], in_=c.before[:], compare_op=ALU.is_gt, fill=0.0,
                                        base=0, pattern=[[1, P]], channel_multiplier=-1).then_inc(made, 1)
                for col in (0, 2 * P):
                    nc.gpsimd.affine_select(out=c.causal[:, col:col + P], in_=c.causal[:, col:col + P], compare_op=ALU.is_ge,
                                            fill=NEG, base=0, pattern=[[-1, P]], channel_multiplier=1).then_inc(made, 1)

            @block.tensor
            def _(pe):
                pe.wait_ge(gates_in_s, 32)
                pe.wait_ge(made, 2)
                nc.tensor.matmul(gates_ps[:, 0:4], ones_row[:], gates_in[:], start=True, stop=True).then_inc(bc_s, 1)

            @block.scalar
            def _(act):
                act.wait_ge(bc_s, 1)
                nc.scalar.activation(c.gate[:], gates_ps[:, 0:4], ACT.Tanh).then_inc(bc_s, 1)

            @block.vector
            def _(dve):
                dve.wait_ge(made, 17)
                nc.vector.tensor_single_scalar(slot_low[:], slot_no[:], P - 1, ALU.bitwise_and).then_inc(dve_s, 1)
                dve.wait_ge(dve_s, 1)
                nc.vector.tensor_scalar(fill[:, :, 0], slot_low[:], float(N), None, ALU.add).then_inc(dve_s, 1)
                nc.vector.memset(fill[:, :, 1], UNUSED).then_inc(dve_s, 1)
                nc.vector.tensor_copy(c.ident16[:], c.ident[:]).then_inc(dve_s, 1)
                nc.vector.tensor_scalar(c.base0[:], c.expert_no[:, 0:E0], float(N), None, ALU.mult).then_inc(dve_s, 1)
                nc.vector.memset(c.base1[:], 0.0).then_inc(dve_s, 1)
                n1 = E1 * CAP // P
                dve.wait_ge(dve_s, 2)
                nc.vector.tensor_copy(fill1[:, :, 0], fill[:, 0:n1, 0]).then_inc(dve_s, 1)
                dve.wait_ge(bc_s, 2)
                nc.vector.tensor_scalar(c.gate_half[:], c.gate[:], 0.5, None, ALU.mult).then_inc(dve_s, 1)
                nc.vector.tensor_scalar(c.gate_neg[:], c.gate[:], -0.5, None, ALU.mult).then_inc(dve_s, 1)
                nc.vector.tensor_scalar(c.gate_quarter[:], c.gate[:], 0.25, None, ALU.mult).then_inc(dve_s, 1)


class Norm:

    def __init__(self, m, c, tag):
        self.c = c
        self.stats = m.sb(f"{tag}_stats", [P, TJ, 6])
        self.mv = m.sb(f"{tag}_mean_var", [P, TJ, 2])
        self.var = m.sb(f"{tag}_var_eps", [P, TJ])
        self.neg = m.sb(f"{tag}_neg_mean", [P, TJ])
        self.rstd = m.sb(f"{tag}_rstd", [P, TJ])
        self.shift = m.sb(f"{tag}_shift", [P, TJ])
        self.stats_s = m.sem(f"{tag}_stats_s")
        self.rstd_s = m.sem(f"{tag}_rstd_s")
        self.done_s = m.sem(f"{tag}_normed_s")

    def dve(self, nc, dve, b, x):
        wait(dve, self.rstd_s, 4 * b.i)
        for j in range(TJ):
            nc.vector.bn_stats(self.stats[:, j, :], x[:, j, :]).then_inc(self.stats_s, 1)
        for j in range(TJ):
            dve.wait_ge(self.stats_s, 4 * b.i + 1 + j)
            alone(dve)
            nc.vector.bn_aggr(self.mv[:, j, :], self.stats[:, j, :]).then_inc(self.stats_s, 1)

    def pool(self, nc, pool, b):
        pool.wait_ge(self.stats_s, 4 * b.i + 4)
        wait(pool, self.done_s, 2 * b.i)
        alone(pool)
        nc.gpsimd.tensor_scalar(self.var[:], self.mv[:, :, 1], EPS, None, ALU.add).then_inc(self.rstd_s, 1)
        nc.gpsimd.tensor_scalar(self.neg[:], self.mv[:, :, 0], -1.0, None, ALU.mult).then_inc(self.rstd_s, 1)
        pool.wait_ge(self.rstd_s, 4 * b.i + 2)
        nc.gpsimd.tensor_tensor(self.rstd[:], self.var[:], self.c.half_power[:], ALU.pow).then_inc(self.rstd_s, 1)
        pool.wait_ge(self.rstd_s, 4 * b.i + 3)
        nc.gpsimd.tensor_tensor(self.shift[:], self.neg[:], self.rstd[:], ALU.mult).then_inc(self.rstd_s, 1)

    def act(self, nc, act, b, out, x):
        act.wait_ge(self.rstd_s, 4 * b.i + 4)
        for j in range(TJ):
            nc.scalar.activation(out[:, j, :], x[:, j, :], ACT.Identity, bias=self.shift[:, j:j + 1],
                                 scale=self.rstd[:, j:j + 1]).then_inc(self.done_s, 1)


def columns(ap, j):
    return ap[:, :, j * P:(j + 1) * P]


def blocks(bank):
    return bank[:].rearrange("p (k t) -> p k t", t=P)


def wkv_phase(nc, io, c):
    with Memory(nc, "wkv_") as m:
        x = [m.sb(f"x_{s}", [P, TJ, C]) for s in range(2)]
        ctx = [m.sb(f"ctx_{s}", [P, TJ, C]) for s in range(2)]
        k_tok = m.sb("k_tok", [P, TJ, C])
        kT = [m.sb(f"kT_{s}", [P, KC, T]) for s in range(2)]
        vT = [m.sb(f"vT_{s}", [P, KC, T]) for s in range(2)]
        o, p, q = (m.sb(f"run_{n}", [P, KC, T + 1]) for n in "opq")
        a2, e2, e2v, aq, em, am, ev, yT = (m.sb(n, [P, KC, T]) for n in (
            "decay", "enter", "enter_v", "bonus_q", "bonus_e", "bonus_a", "bonus_v", "yT"))
        x1 = [m.sb(f"x1_{s}", [P, TJ, C]) for s in range(2)]
        xn = m.sb("xn", [P, TJ, C])
        xnT = m.sb("xnT", [P, KC, T])
        tg = [m.sb(f"tanh_gate_{s}", [P, T]) for s in range(2)]
        sg = [m.sb(f"silu_gate_{s}", [P, T]) for s in range(2)]
        hT = m.sb("hT", [P, M0, T])
        wg, wu = m.sb("wg", [P, KC, S0]), m.sb("wu", [P, KC, S0])
        wd = m.sb("wd", [P, M0, C])
        wr = m.sb("wr", [P, KC, E0 + 1])
        lg = m.sb("lg", [P, TJ, E0 + 1])
        top = m.sb("top", [P, TJ, 8])
        at = m.sb("at", [P, TJ, 8], U32)
        atf = m.sb("atf", [P, TJ, K0])
        hot = m.sb("hot", [P, TJ, K0, E0])
        chosen = m.sb("chosen", [P, TJ, E0], BF16)
        slot = m.sb("slot", [P, TJ, E0])
        pick = m.sb("pick", [P, TJ, K0, E0])
        posf = m.sb("posf", [P, TJ, K0])
        pos = [m.sb(f"pos_{s}", [P, TJ, K0], U32) for s in range(2)]
        pair = [m.sb(f"pair_{s}", [P, TJ, K0, 3], I32) for s in range(2)]
        gap = m.sb("gap", [P, TJ, 2])
        tgap = m.sb("tgap", [P, TJ, 2])
        ssc = m.sb("ssc", [P, TJ])
        pre_ps = [m.ps(f"pre_ps{n}") for n in range(2)]
        post_ps = [m.ps(f"post_ps{n}") for n in range(2)]
        ffn_ps = [m.ps(f"ffn_ps{n}") for n in range(2)]
        route_ps = m.ps("route_ps")
        norm1, norm2 = Norm(m, c, "norm1"), Norm(m, c, "norm2")
        x_in = [m.sem(f"x_in{s}") for s in range(2)]
        ctx_in = [m.sem(f"ctx_in{s}") for s in range(2)]
        weights_in, init_s = m.sem("weights_in"), m.sem("state_init")
        pre_tr, pre_ev = m.sem("pre_transposed"), m.sem("pre_evacuated")
        wkv_c, post_c = m.sem("dve_wkv_steps"), m.sem("dve_post_steps")
        exp_in, exps, products = m.sem("exp_arguments"), m.sem("exps"), m.sem("pool_products")
        y_done, y_tr, x1_s = m.sem("y_done"), m.sem("y_transposed"), m.sem("x1_done")
        xn_tr, xn_ev = m.sem("xn_transposed"), m.sem("xn_evacuated")
        logit_s, chosen_s, rank_s = m.sem("logits"), m.sem("chosen_done"), m.sem("ranks")
        gap_s, tgap_s = m.sem("gap_done"), m.sem("tanh_gap")
        gu_s, tg_s, freed = m.sem("gate_up"), m.sem("tanh_of_gate"), m.sem("ffn_bank_read")
        down_s, pair_s = m.sem("down"), m.sem("pairs")
        scat = [m.sem(f"scattered{s}") for s in range(2)]
        xn_out = [m.sem(f"xn_out{s}") for s in range(2)]
        x2_out = [m.sem(f"x2_out{s}") for s in range(2)]
        with nc.Block() as block:
            @block.sync
            def _(sp):
                def load(b):
                    if not b.first:
                        wait(sp, x1_s, TJ * (b.i - 1))
                        alone(sp)
                        wait(sp, pre_tr, 4 * (b.i - 1))
                        alone(sp)
                    sp.dma_start(x[b.s][:], rows(io["x"], b)).then_inc(x_in[b.s], 16)
                    sp.dma_start(ctx[b.s][:], rows(io["ctx"], b)).then_inc(ctx_in[b.s], 16)

                def store_xn(b):
                    sp.wait_ge(norm2.done_s, 2 * b.i + 2)
                    alone(sp)
                    sp.dma_start(rows(io["xn0"], b), xn[:]).then_inc(xn_out[b.s], 16)

                def store_x2(b):
                    sp.wait_ge(freed, 2 + FB0 * (b.i + 1))
                    alone(sp)
                    sp.dma_start(rows(io["x2"], b), x1[b.s][:]).then_inc(x2_out[b.s], 16)

                def turn(b):
                    if not b.first:
                        if not b.last:
                            load(b.after())
                        store_xn(b.before())
                    if b.third:
                        store_x2(b.before().before())

                load(FIRST)
                for t, name in ((wr[:, :, 0:E0], "gate_w0"), (wr[:, :, E0:], "se_gate"),
                                (wg[:], "sh_gate"), (wu[:], "sh_up"), (wd[:], "sh_down")):
                    sp.dma_start(t, io[name].rearrange("(k p) n -> p k n", p=P),
                                 allow_slow_non_contiguous=name == "se_gate").then_inc(weights_in, 16)
                load(FIRST.after())
                for n, name in enumerate(("w_gate0", "w_up0")):
                    for e in range(E0):
                        sp.dma_start(c.wgu0[:, e, :, n * H0:(n + 1) * H0],
                                     io[name][e].rearrange("(k p) n -> p k n", p=P)).then_inc(c.wgu0_in, 16)
                turns(sp, B, turn)
                store_xn(LAST)
                store_x2(LAST.before())
                store_x2(LAST)
                for s in range(2):
                    sp.wait_ge(xn_out[s], 16 * (B // 2))
                    sp.wait_ge(x2_out[s], 16 * (B // 2))

            @block.tensor
            def _(pe):
                def pre(b):
                    for n, src in enumerate((k_tok, ctx[b.s])):
                        if n == 0:
                            pe.wait_ge(norm1.done_s, 2 * b.i + 2)
                        else:
                            pe.wait_ge(ctx_in[b.s], 16 * (b.round + 1))
                        for j in range(TJ):
                            wait(pe, pre_ev, 4 * b.i + 2 * n + j - 1)
                            for k in range(KC):
                                ins = nc.tensor.transpose(blocks(pre_ps[j])[:, k, :], src[:, j, k * P:(k + 1) * P], c.ident[:])
                            ins.then_inc(pre_tr, 1)

                def post_y(b):
                    pe.wait_ge(y_done, b.i + 1)
                    wait(pe, xn_ev, 2 * b.i)
                    for j in range(TJ):
                        for k in range(KC):
                            ins = nc.tensor.transpose(blocks(post_ps[j])[:, k, :], yT[:, k, j * P:(j + 1) * P], c.ident[:])
                        ins.then_inc(y_tr, 1)

                def post_xn(b):
                    for j in range(TJ):
                        pe.wait_ge(norm2.done_s, 2 * b.i + j + 1)
                        for k in range(KC):
                            ins = nc.tensor.transpose(blocks(post_ps[j])[:, k, :], xn[:, j, k * P:(k + 1) * P], c.ident[:])
                        ins.then_inc(xn_tr, 1)

                def logits(b):
                    pe.wait_ge(xn_ev, 2 * b.i + 2)
                    wait(pe, pair_s, b.i)
                    for j in range(TJ):
                        for k in range(KC):
                            ins = nc.tensor.matmul(route_ps[:, j * (E0 + 1):(j + 1) * (E0 + 1)], xnT[:, k, j * P:(j + 1) * P],
                                                   wr[:, k, :], start=(k == 0), stop=(k == KC - 1))
                    ins.then_inc(logit_s, 1)

                def gate_up(b, n):
                    pe.wait_ge(freed, FB0 * b.i + n + 1)
                    for w, col in ((wg, 0), (wu, T)):
                        for k in range(KC):
                            ins = nc.tensor.matmul(ffn_ps[n % 2][:, col:col + T], w[:, k, n * P:(n + 1) * P],
                                                   xnT[:, k, :], start=(k == 0), stop=(k == KC - 1))
                    ins.then_inc(gu_s, 1)

                def ranks(b):
                    pe.wait_ge(chosen_s, b.i + 1)
                    for r, parts in enumerate((((c.before, 0),), ((c.before, 1), (c.ones, 0)), ((c.ones, 0), (c.ones, 1)))):
                        for n, (lhs, j) in enumerate(parts):
                            ins = nc.tensor.matmul(route_ps[:, 32 + r * E0:32 + (r + 1) * E0], lhs[:], chosen[:, j, :],
                                                   start=(n == 0), stop=(n == len(parts) - 1))
                    ins.then_inc(rank_s, 1)

                def down(b, j):
                    pe.wait_ge(freed, FB0 * b.i + M0 + j + 1 + (j == 0))
                    for k in range(M0):
                        ins = nc.tensor.matmul(ffn_ps[j][:], hT[:, k, j * P:(j + 1) * P], wd[:, k, :],
                                               start=(k == 0), stop=(k == M0 - 1))
                    ins.then_inc(down_s, 1)

                def behind(one, two):
                    if one:
                        post_y(one)
                    if two:
                        gate_up(two, M0 - 1)
                        down(two, 0)
                    if one:
                        post_xn(one)
                    if two:
                        down(two, 1)
                    if one:
                        logits(one)
                        for n in range(M0 - 1):
                            gate_up(one, n)
                            if n == 1:
                                ranks(one)

                def turn(b):
                    behind(not b.first and b.before(), b.third and b.before().before())
                    if not b.last:
                        pre(b.after())

                pre(FIRST)
                pe.wait_ge(weights_in, 5 * 16)
                turns(pe, B, turn)
                behind(LAST, LAST.before())
                behind(None, LAST)

            @block.scalar
            def _(act):
                def norm_pre(b):
                    wait(act, pre_tr, 4 * b.i - 2)
                    norm1.act(nc, act, b, k_tok, x[b.s])

                def pre(b):
                    if not b.first:
                        wait(act, y_done, b.i - 1)
                    for n, dst in enumerate((kT[b.s], vT[b.s])):
                        for j in range(TJ):
                            act.wait_ge(pre_tr, 4 * b.i + 2 * n + j + 1)
                            nc.scalar.copy(columns(dst, j), blocks(pre_ps[j])).then_inc(pre_ev, 1)

                def wkv(b):
                    act.wait_ge(exp_in, 2 * b.i + 1)
                    for k in range(KC):
                        nc.scalar.activation(a2[:, k, :], a2[:, k, :], ACT.Exp, bias=c.w[:, k:k + 1]).then_inc(exps, 1)
                    act.wait_ge(exp_in, 2 * b.i + 2)
                    nc.scalar.activation(e2[:], e2[:], ACT.Exp).then_inc(exps, 1)
                    act.wait_ge(wkv_c, WKV_STEPS * b.i + 9)
                    nc.scalar.activation(em[:], em[:], ACT.Exp).then_inc(exps, 1)
                    act.wait_ge(wkv_c, WKV_STEPS * b.i + 13)
                    nc.scalar.activation(am[:], am[:], ACT.Exp, scale=-1.0).then_inc(exps, 1)

                def norm_post(b):
                    if not b.first:
                        wait(act, xn_out[1 - b.s], 16 * (b.before().round + 1))
                    norm2.act(nc, act, b, xn, x1[b.s])

                def post(b):
                    wait(act, gu_s, M0 * b.i)
                    for j in range(TJ):
                        act.wait_ge(xn_tr, 2 * b.i + j + 1)
                        nc.scalar.copy(columns(xnT, j), blocks(post_ps[j])).then_inc(xn_ev, 1)

                def gaps(b):
                    act.wait_ge(gap_s, b.i + 1)
                    nc.scalar.activation(tgap[:], gap[:], ACT.Tanh, scale=0.5).then_inc(tgap_s, 1)

                def tanh_gate(b, n):
                    act.wait_ge(gu_s, M0 * b.i + n + 1)
                    nc.scalar.activation(tg[n % 2][:], ffn_ps[n % 2][:, 0:T], ACT.Tanh, scale=0.5).then_inc(tg_s, 1)

                def turn(b):
                    wkv(b)
                    if b.third:
                        tanh_gate(b.before().before(), M0 - 1)
                    if not b.first:
                        norm_post(b.before())
                        post(b.before())
                        tanh_gate(b.before(), 0)
                    if not b.last:
                        norm_pre(b.after())
                    if not b.first:
                        gaps(b.before())
                        for n in range(1, M0 - 1):
                            tanh_gate(b.before(), n)
                    if not b.last:
                        pre(b.after())

                norm_pre(FIRST)
                pre(FIRST)
                turns(act, B, turn)
                tanh_gate(LAST.before(), M0 - 1)
                norm_post(LAST)
                post(LAST)
                tanh_gate(LAST, 0)
                gaps(LAST)
                for n in range(1, M0):
                    tanh_gate(LAST, n)

            @block.gpsimd
            def _(pool):
                def enter(b):
                    pool.wait_ge(exps, 7 * b.i + 5)
                    nc.gpsimd.tensor_tensor(e2v[:], e2[:], vT[b.s][:], ALU.mult).then_inc(products, 1)

                def bonus(b):
                    pool.wait_ge(exps, 7 * b.i + 6)
                    nc.gpsimd.tensor_tensor(ev[:], em[:], vT[b.s][:], ALU.mult).then_inc(products, 1)

                def scatter(b):
                    pool.wait_ge(pair_s, b.i + 1)
                    alone(pool)
                    for j in range(TJ):
                        for k in range(K0):
                            nc.gpsimd.indirect_dma_start(
                                io["list0"], bass.IndirectOffsetOnAxis(ap=pos[b.s][:, j, k:k + 1], axis=0),
                                pair[b.s][:, j, k, :], None).then_inc(scat[b.s], 16)

                def turn(b):
                    enter(b)
                    if not b.first:
                        norm2.pool(nc, pool, b.before())
                    bonus(b)
                    if b.third:
                        scatter(b.before().before())
                    if not b.last:
                        norm1.pool(nc, pool, b.after())

                norm1.pool(nc, pool, FIRST)
                turns(pool, B, turn)
                norm2.pool(nc, pool, LAST)
                scatter(LAST.before())
                scatter(LAST)
                for s in range(2):
                    pool.wait_ge(scat[s], 16 * TJ * K0 * (B // 2))

            @block.vector
            def _(dve):
                steps, posts = Chain(dve, wkv_c, WKV_STEPS), Chain(dve, post_c, POST_STEPS0)
                v = nc.vector

                def recurrences(b):
                    steps.turn(b.i)
                    dve.wait_ge(pre_ev, 4 * b.i + 2)
                    for k in range(KC):
                        steps.did(v.tensor_tensor_scan(o[:, k, 1:], c.w[:, k:k + 1].to_broadcast([P, T]),
                                                       kT[b.s][:, k, :], BEFORE_ALL, ALU.add, ALU.max))
                    steps.need(4)
                    v.tensor_tensor(a2[:], o[:, :, 0:T], o[:, :, 1:], ALU.subtract).then_inc(exp_in, 1)
                    v.tensor_tensor(e2[:], kT[b.s][:], o[:, :, 1:], ALU.subtract).then_inc(exp_in, 1)
                    steps.did(v.tensor_tensor(aq[:], kT[b.s][:], o[:, :, 0:T], ALU.subtract))
                    steps.need(5)
                    for k in range(KC):
                        steps.did(v.tensor_scalar(em[:, k, :], aq[:, k, :], c.u[:, k:k + 1], 0.0, ALU.add, ALU.min))
                    for k in range(KC):
                        steps.did(v.tensor_scalar(am[:, k, :], aq[:, k, :], c.u[:, k:k + 1], 0.0, ALU.add, ALU.max))

                def sums(b):
                    dve.wait_ge(exps, 7 * b.i + 5)
                    for k in range(KC):
                        steps.did(v.tensor_tensor_scan(q[:, k, 1:], a2[:, k, :], e2[:, k, :], 0.0, ALU.mult, ALU.add))
                    dve.wait_ge(products, 2 * b.i + 1)
                    for k in range(KC):
                        steps.did(v.tensor_tensor_scan(p[:, k, 1:], a2[:, k, :], e2v[:, k, :], 0.0, ALU.mult, ALU.add))

                def quotient(b):
                    dve.wait_ge(exps, 7 * b.i + 7)
                    steps.need(17)
                    steps.did(v.tensor_tensor(aq[:], am[:], q[:, :, 0:T], ALU.mult))
                    steps.need(21)
                    steps.did(v.tensor_tensor(am[:], am[:], p[:, :, 0:T], ALU.mult))
                    steps.need(22)
                    steps.did(v.tensor_tensor(aq[:], aq[:], em[:], ALU.add))
                    steps.need(23)
                    dve.wait_ge(products, 2 * b.i + 2)
                    steps.did(v.tensor_tensor(am[:], am[:], ev[:], ALU.add))

                def divide(b):
                    steps.need(24)
                    steps.did(v.reciprocal(aq[:], aq[:]))
                    steps.need(26)
                    wait(dve, y_tr, 2 * b.i)
                    v.tensor_tensor(yT[:], am[:], aq[:], ALU.mult).then_inc(y_done, 1)

                def residual(b):
                    wait(dve, x2_out[b.s], 16 * b.round)
                    for j in range(TJ):
                        dve.wait_ge(y_tr, 2 * b.i + j + 1)
                        v.scalar_tensor_tensor(x1[b.s][:, j, :], post_ps[j][:], c.gate[:, 0:1], x[b.s][:, j, :],
                                               ALU.mult, ALU.add).then_inc(x1_s, 1)
                    dve.wait_ge(x1_s, TJ * (b.i + 1))
                    norm2.dve(nc, dve, b, x1[b.s])

                def route(b):
                    posts.turn(b.i)
                    dve.wait_ge(logit_s, b.i + 1)
                    posts.did(v.tensor_copy(lg[:].rearrange("p j e -> p (j e)"), route_ps[:, 0:TJ * (E0 + 1)]))
                    posts.need(1)
                    alone(dve)
                    for j in range(TJ):
                        posts.did(v.max(top[:, j, :], lg[:, j, 0:E0]))
                    posts.need(3)
                    alone(dve)
                    for j in range(TJ):
                        posts.did(v.max_index(at[:, j, :], top[:, j, :], lg[:, j, 0:E0]))
                    wait(dve, tgap_s, b.i)
                    posts.did(v.tensor_copy(gap[:, :, 1:2], lg[:, :, E0:]))
                    v.tensor_tensor(gap[:, :, 0:1], top[:, :, 0:1], top[:, :, 1:2], ALU.subtract).then_inc(gap_s, 1)
                    posts.need(5)
                    posts.did(v.tensor_copy(atf[:], at[:, :, 0:K0]))
                    posts.need(7)
                    posts.did(v.tensor_tensor(
                        hot[:].rearrange("p j k e -> p (j k) e"),
                        c.expert_no[:, 0:E0].unsqueeze(1).to_broadcast([P, TJ * K0, E0]),
                        atf[:].rearrange("p j k -> p (j k)").unsqueeze(2).to_broadcast([P, TJ * K0, E0]), ALU.is_equal))
                    posts.need(8)
                    wait(dve, rank_s, b.i)
                    v.tensor_tensor(chosen[:], hot[:, :, 0, :], hot[:, :, 1, :], ALU.add).then_inc(chosen_s, 1)

                def slots(b):
                    posts.resume(b.i)
                    dve.wait_ge(rank_s, b.i + 1)
                    wait(dve, scat[b.s], 16 * TJ * K0 * b.round)
                    slotted = posts.did(v.tensor_tensor(
                        slot[:], route_ps[:, 32:32 + TJ * E0].rearrange("p (j e) -> p j e", e=E0),
                        c.base0[:].unsqueeze(1).to_broadcast([P, TJ, E0]), ALU.add))
                    posts.did(v.tensor_copy(pair[b.s][:, :, :, 0], c.token_no[:].unsqueeze(2).to_broadcast([P, TJ, K0])))
                    for k in range(K0):
                        numbered = posts.did(v.tensor_scalar(pair[b.s][:, :, k, 1], c.token_no[:], float(k * N), None, ALU.add))
                    dve.wait_ge(tgap_s, b.i + 1)
                    for k, sign in enumerate((c.gate_half, c.gate_neg)):
                        posts.did(v.tensor_scalar(pair[b.s][:, :, k, 2].bitcast(F32), tgap[:, :, 0], sign[:, 2:3],
                                                  c.gate_half[:, 2:3], ALU.mult, ALU.add))
                    scaled = posts.did(v.tensor_scalar(ssc[:], tgap[:, :, 1], 1.0, c.gate_quarter[:, 2:3], ALU.add, ALU.mult))
                    posts.need(slotted)
                    for j in range(TJ):
                        picked = posts.did(v.tensor_tensor(pick[:, j], hot[:, j], slot[:, j, :].unsqueeze(1).to_broadcast([P, K0, E0]), ALU.mult))
                    posts.did(v.tensor_tensor(c.base0[:], c.base0[:], route_ps[:, 32 + TJ * E0:32 + (TJ + 1) * E0], ALU.add))
                    posts.need(numbered)
                    posts.did(v.tensor_scalar(c.token_no[:], c.token_no[:], float(T), None, ALU.add))
                    posts.need(picked)
                    summed = posts.did(v.tensor_reduce(posf[:].rearrange("p j k -> p (j k)"), pick[:].rearrange("p j k e -> p (j k) e"),
                                                       AX.X, ALU.add))
                    posts.need(summed)
                    v.tensor_copy(pos[b.s][:], posf[:]).then_inc(pair_s, 1)

                def hidden(b, n):
                    posts.resume(b.i)
                    dve.wait_ge(tg_s, M0 * b.i + n + 1)
                    s = n % 2
                    posts.did(v.scalar_tensor_tensor(sg[s][:], tg[s][:], 1.0, ffn_ps[s][:, 0:T], ALU.add, ALU.mult))
                    posts.need(posts.n)
                    if n == 0:
                        wait(dve, down_s, TJ * b.i)
                    v.tensor_tensor(hT[:, n, :], sg[s][:], ffn_ps[s][:, T:2 * T], ALU.mult).then_inc(freed, 1)

                def shared(b, j):
                    dve.wait_ge(down_s, TJ * b.i + j + 1)
                    v.scalar_tensor_tensor(x1[b.s][:, j, :], ffn_ps[j][:], ssc[:, j:j + 1], x1[b.s][:, j, :],
                                           ALU.mult, ALU.add).then_inc(freed, 1)

                def turn(b):
                    one, two = not b.first and b.before(), b.third and b.before().before()
                    recurrences(b)
                    if one:
                        residual(one)
                    if two:
                        hidden(two, M0 - 1)
                        slots(two)
                    sums(b)
                    if two:
                        shared(two, 0)
                    quotient(b)
                    if two:
                        shared(two, 1)
                    if not b.last:
                        after = b.after()
                        dve.wait_ge(x_in[after.s], 16 * (after.round + 1))
                        norm1.dve(nc, dve, after, x[after.s])
                    if one:
                        route(one)
                        hidden(one, 0)
                    divide(b)
                    if one:
                        for n in range(1, M0 - 1):
                            hidden(one, n)

                for t, value in ((o, BEFORE_ALL), (p, 0.0), (q, 0.0)):
                    v.memset(t[:, :, 0:1], value).then_inc(init_s, 1)
                dve.wait_ge(init_s, 3)
                v.engine_nop().then_inc(freed, 2)
                dve.wait_ge(x_in[0], 16)
                norm1.dve(nc, dve, FIRST, x[0])
                turns(dve, B, turn)
                residual(LAST)
                hidden(LAST.before(), M0 - 1)
                slots(LAST.before())
                for j in range(TJ):
                    shared(LAST.before(), j)
                route(LAST)
                for n in range(M0):
                    hidden(LAST, n)
                slots(LAST)
                for j in range(TJ):
                    shared(LAST, j)


def routed0_phase(nc, io, c):
    with Memory(nc, "routed0_") as m:
        HW = H0 // P
        wgu = c.wgu0
        wdn = m.sb("wdn", [P, E0, HW, C])
        nt, ends, zero8 = m.sb("expert_tiles", [P, E0]), m.sb("ends", [P, E0]), m.sb("zero8", [P, E0])
        count_i = m.sb("count_i", [P, E0], I32)
        past = m.sb("past", [P, TILES0, E0])
        past_nt = m.sb("past_nt", [P, TILES0, E0])
        expert, start, row = (m.sb(n, [P, TILES0]) for n in ("expert", "start", "row"))
        expert_i, row_i = m.sb("expert_i", [P, TILES0], I32), m.sb("row_i", [P, TILES0], I32)
        pair = [m.sb(f"pair_{s}", [P, 3], I32) for s in range(WAYS0)]
        xg = [m.sb(f"xg_{s}", [P, C]) for s in range(SLOTS0)]
        xT = [m.sb(f"xT_{s}", [P, KC, P]) for s in range(2)]
        sg, h, hT = (m.sb(n, [P, H0]) for n in ("silu_gate", "h", "hT"))
        ys = [m.sb(f"ys_{s}", [P, C]) for s in range(SLOTS0)]
        xt_ps = [m.ps(f"xt_ps{n}") for n in range(2)]
        gu_ps = [m.ps(f"gu_ps{n}") for n in range(2)]
        ht_ps = m.ps("ht_ps")
        y_ps = [m.ps(f"y_ps{n}") for n in range(2)]
        weights_in, table, table_s = m.sem("weights0_in"), m.sem("table_steps"), m.sem("table_done")
        pair_in = [m.sem(f"pair_in{s}") for s in range(WAYS0)]
        xg_in = [m.sem(f"rows_gathered{s}") for s in range(SLOTS0)]
        xt_s, xt_ev, gu_s = m.sem("x_transposed"), m.sem("x_evacuated"), m.sem("gate_up0")
        silu_s, h_s = m.sem("silu_done"), m.sem("h_done")
        ht_s, ht_ev, y_s, ys_s = m.sem("h_transposed"), m.sem("h_evacuated"), m.sem("y_ready"), m.sem("y_scaled")
        placed = [m.sem(f"rows_placed{s}") for s in range(SLOTS0)]
        with nc.Block() as block:
            def uses(t):
                return t.round * (WAYS0 // SLOTS0) + t.s // SLOTS0 + 1

            @block.sync
            def _(sp):
                for e in range(E0):
                    sp.dma_start(wdn[:, e], io["w_down0"][e].rearrange("(k p) n -> p k n", p=P)).then_inc(weights_in, 16)
                sp.wait_ge(table_s, 1)

                def turn(t):
                    wait(sp, placed[t.s % SLOTS0], 16 * (uses(t) - WAYS0 // SLOTS0))
                    alone(sp)
                    at = sp.value_load(row_i[0:1, bass.ds(t.i, 1)], min_val=0, max_val=LIST0 - P)
                    sp.dma_start(pair[t.s][:], io["list0"][bass.ds(at, P), :]).then_inc(pair_in[t.s], 16)

                turns(sp, TILES0, turn, WAYS0)

            @block.gpsimd
            def _(pool):
                def gather(t):
                    if not isinstance(t.i, int) or t.i >= SLOTS0:
                        pool.wait_ge(xt_s, t.i - SLOTS0 + 1)
                        alone(pool)
                    pool.wait_ge(pair_in[t.s], 16 * (t.round + 1))
                    alone(pool)
                    nc.gpsimd.indirect_dma_start(xg[t.s % SLOTS0][:], None, io["xn0"],
                                                 bass.IndirectOffsetOnAxis(ap=pair[t.s][:, 0:1].bitcast(U32), axis=0)
                                                 ).then_inc(xg_in[t.s % SLOTS0], 16)

                def place(t):
                    pool.wait_ge(ys_s, t.i + 1)
                    alone(pool)
                    nc.gpsimd.indirect_dma_start(io["y0"], bass.IndirectOffsetOnAxis(ap=pair[t.s][:, 1:2].bitcast(U32), axis=0),
                                                 ys[t.s % SLOTS0][:], None, bounds_check=K0 * N - 1, oob_is_err=False).then_inc(placed[t.s % SLOTS0], 16)

                def turn(t):
                    if not isinstance(t.i, int) or t.i < TILES0 - AHEAD0:
                        for n in range(AHEAD0):
                            ahead = t.after() if n == 0 else ahead.after()
                        gather(ahead)
                    if not t.first:
                        place(t.before())

                ahead = first(TILES0, WAYS0)
                for n in range(AHEAD0):
                    gather(ahead)
                    ahead = ahead.after()
                turns(pool, TILES0, turn, WAYS0)
                place(last(TILES0, WAYS0))
                for s in range(SLOTS0):
                    pool.wait_ge(placed[s], 16 * (TILES0 // SLOTS0))

            @block.tensor
            def _(pe):
                def inputs(t):
                    pe.wait_ge(xg_in[t.s % SLOTS0], 16 * uses(t))
                    wait(pe, xt_ev, t.i - 1)
                    for k in range(KC):
                        ins = nc.tensor.transpose(blocks(xt_ps[t.s % 2])[:, k, :], xg[t.s % SLOTS0][:, k * P:(k + 1) * P], c.ident[:])
                    ins.then_inc(xt_s, 1)

                def gate_up(t):
                    pe.wait_ge(xt_ev, t.i + 1)
                    wait(pe, h_s, t.i - 1)
                    alone(pe)
                    e = pe.value_load(expert_i[0:1, bass.ds(t.i, 1)], min_val=0, max_val=E0 - 1)
                    for k in range(KC):
                        ins = nc.tensor.matmul(gu_ps[t.s % 2][:], xT[t.s % 2][:, k, :],
                                               wgu[:, bass.ds(e, 1), k, :].rearrange("p a n -> p (a n)"),
                                               start=(k == 0), stop=(k == KC - 1))
                    ins.then_inc(gu_s, 1)

                def hidden(t):
                    pe.wait_ge(h_s, t.i + 1)
                    wait(pe, ht_ev, t.i)
                    for k in range(HW):
                        ins = nc.tensor.transpose(ht_ps[:, k * P:(k + 1) * P], h[:, k * P:(k + 1) * P], c.ident[:])
                    ins.then_inc(ht_s, 1)

                def down(t):
                    pe.wait_ge(ht_ev, t.i + 1)
                    wait(pe, ys_s, t.i)
                    alone(pe)
                    e = pe.value_load(expert_i[0:1, bass.ds(t.i, 1)], min_val=0, max_val=E0 - 1)
                    for k in range(HW):
                        ins = nc.tensor.matmul(y_ps[t.s % 2][:], hT[:, k * P:(k + 1) * P],
                                               wdn[:, bass.ds(e, 1), k, :].rearrange("p a n -> p (a n)"),
                                               start=(k == 0), stop=(k == HW - 1))
                    ins.then_inc(y_s, 1)

                def turn(t):
                    if not t.last:
                        inputs(t.after())
                    if not t.first:
                        hidden(t.before())
                    gate_up(t)
                    if not t.first:
                        down(t.before())

                pe.wait_ge(table_s, 1)
                inputs(first(TILES0, WAYS0))
                pe.wait_ge(c.wgu0_in, 16 * 2 * E0)
                pe.wait_ge(weights_in, 16 * E0)
                turns(pe, TILES0, turn, WAYS0)
                hidden(last(TILES0, WAYS0))
                down(last(TILES0, WAYS0))

            @block.scalar
            def _(act):
                def inputs(t):
                    act.wait_ge(xt_s, t.i + 1)
                    wait(act, gu_s, t.i - 1)
                    nc.scalar.copy(xT[t.s % 2][:].rearrange("p k t -> p (k t)"), xt_ps[t.s % 2][:]).then_inc(xt_ev, 1)

                def turn(t):
                    if not t.last:
                        inputs(t.after())
                    act.wait_ge(gu_s, t.i + 1)
                    wait(act, h_s, t.i)
                    nc.scalar.activation(sg[:], gu_ps[t.s % 2][:, 0:H0], ACT.Silu).then_inc(silu_s, 1)

                inputs(first(TILES0, WAYS0))
                turns(act, TILES0, turn, WAYS0)

            @block.vector
            def _(dve):
                v = nc.vector
                made = [0]

                def link(ins):
                    made[0] += 1
                    ins.then_inc(table, 1)
                    dve.wait_ge(table, made[0])

                every = [P, TILES0, E0]
                link(v.tensor_scalar(nt[:], c.expert_no[:, 0:E0], -float(N), float(P - 1), ALU.mult, ALU.add))
                link(v.tensor_tensor(count_i[:], nt[:], c.base0[:], ALU.add))
                link(v.tensor_single_scalar(count_i[:], count_i[:], 7, ALU.logical_shift_right))
                link(v.tensor_copy(nt[:], count_i[:]))
                link(v.memset(zero8[:], 0.0))
                link(v.tensor_tensor_scan(ends[:], nt[:], zero8[:], 0.0, ALU.add, ALU.add))
                link(v.tensor_tensor(past[:], c.tile_no[:].unsqueeze(2).to_broadcast(every),
                                     ends[:].unsqueeze(1).to_broadcast(every), ALU.is_ge))
                link(v.tensor_reduce(expert[:], past[:], AX.X, ALU.add))
                link(v.tensor_tensor(past_nt[:], past[:], nt[:].unsqueeze(1).to_broadcast(every), ALU.mult))
                link(v.tensor_reduce(start[:], past_nt[:], AX.X, ALU.add))
                link(v.tensor_tensor(start[:], c.tile_no[:], start[:], ALU.subtract))
                link(v.tensor_scalar(row[:], expert[:], float(N), None, ALU.mult))
                link(v.scalar_tensor_tensor(row[:], start[:], float(P), row[:], ALU.mult, ALU.add))
                link(v.tensor_scalar(row_i[:], row[:], float(E0 * N), None, ALU.min))
                link(v.tensor_scalar(expert_i[:], expert[:], float(E0 - 1), None, ALU.min))
                v.engine_nop().then_inc(table_s, 1)

                def hidden(t):
                    dve.wait_ge(silu_s, t.i + 1)
                    wait(dve, ht_s, t.i)
                    v.tensor_tensor(h[:], sg[:], gu_ps[t.s % 2][:, H0:], ALU.mult).then_inc(h_s, 1)

                def outputs(t):
                    dve.wait_ge(ht_s, t.i + 1)
                    wait(dve, y_s, t.i)
                    v.tensor_copy(hT[:], ht_ps[:, 0:H0]).then_inc(ht_ev, 1)

                def scaled(t):
                    dve.wait_ge(y_s, t.i + 1)
                    wait(dve, placed[t.s % SLOTS0], 16 * (uses(t) - 1))
                    v.tensor_scalar(ys[t.s % SLOTS0][:], y_ps[t.s % 2][:], pair[t.s][:, 2:3].bitcast(F32), None, ALU.mult).then_inc(ys_s, 1)

                def turn(t):
                    if not t.first:
                        outputs(t.before())
                    hidden(t)
                    if not t.first:
                        scaled(t.before())

                turns(dve, TILES0, turn, WAYS0)
                outputs(last(TILES0, WAYS0))
                scaled(last(TILES0, WAYS0))


def attention_phase(nc, io, c):
    with Memory(nc, "attn_") as m:
        x = [m.sb(f"x_{s}", [P, TJ, C]) for s in range(2)]
        ctx = [m.sb(f"ctx_{s}", [P, TJ, C]) for s in range(2)]
        y0 = [m.sb(f"y0_{s}", [P, K0, TJ, C]) for s in range(2)]
        q_tok = m.sb("q_tok", [P, TJ, C])
        qT = [m.sb(f"qT_{s}", [P, KC, T]) for s in range(2)]
        kT = [m.sb(f"kT_{s}", [P, KC, T]) for s in range(2)]
        v1 = [m.sb(f"v1_{s}", [P, TJ, HEADS, D + 1]) for s in range(2)]
        nmax = [m.sb(f"nmax_{n}", [P, 2, TJ]) for n in range(2)]
        pr = [m.sb(f"pr_{n}", [P, 2, 3, P]) for n in range(2)]
        prT = [m.sb(f"prT_{n}", [P, 2, 3, P]) for n in range(2)]
        rden = m.sb("rden", [P, 4 * TJ])
        at = m.sb("at", [P, TJ, HEADS, D])
        x3 = [m.sb(f"x3_{s}", [P, TJ, C]) for s in range(2)]
        xn = m.sb("xn", [P, TJ, C])
        xnT = m.sb("xnT", [P, KC, T])
        tg = [m.sb(f"tanh_gate_{s}", [P, T]) for s in range(2)]
        sg = [m.sb(f"silu_gate_{s}", [P, T]) for s in range(2)]
        hT = m.sb("hT", [P, M1, T])
        wg, wu = m.sb("wg", [P, KC, S1]), m.sb("wu", [P, KC, S1])
        wd = m.sb("wd", [P, M1, C])
        wr = m.sb("wr", [P, KC, E1])
        nlmax = m.sb("nlmax", [P, TJ])
        es = m.sb("es", [P, TJ, E1])
        essum, esr = m.sb("essum", [P, TJ]), m.sb("esr", [P, TJ])
        top = m.sb("top", [P, TJ, 8])
        sel = m.sb("sel", [P, TJ, 8], U32)
        self_ = m.sb("self", [P, TJ, K1])
        hot = m.sb("hot", [P, TJ, K1, E1])
        chosen = m.sb("chosen", [P, TJ, E1], BF16)
        limit = m.sb("limit", [P, E1])
        slot, over = m.sb("slot", [P, TJ, E1]), m.sb("over", [P, TJ, E1])
        pick = m.sb("pick", [P, TJ, K1, E1])
        posf = m.sb("posf", [P, TJ, K1])
        pos = [m.sb(f"pos_{s}", [P, TJ, K1], U32) for s in range(2)]
        pair = [m.sb(f"pair_{s}", [P, TJ, K1, 2], I32) for s in range(2)]
        tok = m.sb("tok", [P, TJ])
        score_ps = m.ps("score_ps", [P, 2, 512])
        tr_ps = [m.ps(f"tr_ps{n}") for n in range(2)]
        out_ps = m.ps("out_ps")
        ffn_ps = [m.ps(f"ffn_ps{n}") for n in range(2)]
        route_ps = m.ps("route_ps")
        norm1, norm2 = Norm(m, c, "norm1"), Norm(m, c, "norm2")
        x_in = [m.sem(f"x_in{s}") for s in range(2)]
        merged = m.sem("routed_merged")
        ctx_in = [m.sem(f"ctx_in{s}") for s in range(2)]
        weights_in, init_s, ones_s = m.sem("weights_in"), m.sem("bases_made"), m.sem("ones_made")
        vals_s, score_s, max_s, exp_s = m.sem("values_made"), m.sem("scores"), m.sem("maxima"), m.sem("exps")
        tr_s = [m.sem("bank0_transposed"), m.sem("bank1_transposed")]
        tr_ev = [m.sem("bank0_read"), m.sem("bank1_read")]
        pv_s, out_c, out_ev = m.sem("outputs"), m.sem("out_steps"), m.sem("outputs_read")
        x3_s, logit_s, chosen_s, rank_s = m.sem("x3_done"), m.sem("logits"), m.sem("chosen_done"), m.sem("ranks")
        nlmax_s, es_s = m.sem("logit_max"), m.sem("logit_exps")
        gu_s, tg_s, freed = m.sem("gate_up"), m.sem("tanh_of_gate"), m.sem("ffn_bank_read")
        down_s, pair_s, post_c = m.sem("down"), m.sem("pairs"), m.sem("dve_post_steps")
        scat = [m.sem(f"scattered{s}") for s in range(2)]
        xn_out = [m.sem(f"xn_out{s}") for s in range(2)]
        x3_out = [m.sem(f"x3_out{s}") for s in range(2)]
        with nc.Block() as block:
            def use(b, u):
                return USES * b.i + 2 + u + (2 if u > PRE_AT and not b.last else 0)

            def use_pre(b, n):
                return n if b.first else use(b.before(), PRE_AT) + 1 + n

            def use_xn(b):
                return use(b, UNITS - 1) + 1

            def width(n):
                return min(P, S1 - n * P)

            @block.sync
            def _(sp):
                def load(b):
                    if not b.first:
                        wait(sp, x3_s, b.i - 1)
                        alone(sp)
                    sp.dma_start(x[b.s][:], rows(io["x2"], b)).then_inc(x_in[b.s], 16)
                    for k in range(K0):
                        sp.dma_start(y0[b.s][:, k], io["y0"][bass.ds(b.i * T + k * N, T), :].rearrange("(j p) c -> p j c", p=P)
                                     ).then_inc(x_in[b.s], 16)
                    if not b.first:
                        wait(sp, vals_s, b.i - 1)
                        alone(sp)
                        wait(sp, tr_s[0], use_pre(b.before(), 1))
                        alone(sp)
                        wait(sp, tr_s[1], use_pre(b.before(), 1))
                        alone(sp)
                    sp.dma_start(ctx[b.s][:], rows(io["ctx"], b)).then_inc(ctx_in[b.s], 16)

                def store(b):
                    sp.wait_ge(norm2.done_s, 2 * b.i + 2)
                    alone(sp)
                    sp.dma_start(rows(io["xn1"], b), xn[:]).then_inc(xn_out[b.s], 16)
                    if not b.last:
                        after = b.after()
                        if not after.last:
                            load(after.after())
                    sp.wait_ge(freed, 2 + FB1 * (b.i + 1))
                    alone(sp)
                    sp.dma_start(rows(io["out"], b), x3[b.s][:]).then_inc(x3_out[b.s], 16)

                def turn(b):
                    if not b.first:
                        store(b.before())

                load(FIRST)
                sp.dma_start(wr[:], io["gate_w1"].rearrange("(k p) n -> p k n", p=P)).then_inc(weights_in, 16)
                for t, name in ((wg, "sw_gate"), (wu, "sw_up")):
                    sp.dma_start(t[:], io[name].rearrange("(k p) n -> p k n", p=P)).then_inc(weights_in, 16)
                load(FIRST.after())
                full = S1 // P
                sp.dma_start(wd[:, 0:full, :], io["sw_down"][0:full * P, :].rearrange("(k p) n -> p k n", p=P)).then_inc(weights_in, 16)
                sp.dma_start(wd[0:S1 - full * P, full, :], io["sw_down"][full * P:, :]).then_inc(weights_in, 16)
                turns(sp, B, turn)
                store(LAST)
                for s in range(2):
                    sp.wait_ge(xn_out[s], 16 * (B // 2))
                    sp.wait_ge(x3_out[s], 16 * (B // 2))

            @block.tensor
            def _(pe):
                def to_channels(src, n):
                    for j in range(TJ):
                        wait(pe, tr_ev[j], n)
                        for k in range(KC):
                            ins = nc.tensor.transpose(blocks(tr_ps[j])[:, k, :], src[:, j, k * P:(k + 1) * P], c.ident[:])
                        ins.then_inc(tr_s[j], 1)

                def pre(b):
                    pe.wait_ge(norm1.done_s, 2 * b.i + 2)
                    to_channels(q_tok, use_pre(b, 0))
                    pe.wait_ge(ctx_in[b.s], 16 * (b.round + 1))
                    to_channels(ctx[b.s], use_pre(b, 1))

                def scores(b, u):
                    if u == 0:
                        for j in range(TJ):
                            pe.wait_ge(tr_ev[j], use_pre(b, 1) + 1)
                    wait(pe, exp_s, 4 * (UNITS * b.i + u))
                    for a in range(2):
                        nc.tensor.matmul(score_ps[:, a, 0:3 * P], c.ident16[:], c.causal[:], start=True, stop=False)
                    for j in range(TJ):
                        for a in range(2):
                            h = 2 * u + a
                            r, k = h * D % P, h * D // P
                            ins = nc.tensor.matmul(score_ps[:, a, j * P:(2 * j + 1) * P], qT[b.s][r:r + D, k, j * P:(j + 1) * P],
                                                   kT[b.s][r:r + D, k, 0:(j + 1) * P], start=False, stop=(j == TJ - 1))
                    ins.then_inc(score_s, 1)

                def transpose(b, u):
                    n = use(b, u)
                    pe.wait_ge(exp_s, 4 * (UNITS * b.i + u + 1))
                    for z in range(6):
                        bank, col = (0, z) if z < 4 else (1, z - 4)
                        if col == 0:
                            pe.wait_ge(tr_ev[bank], n)
                        ins = nc.tensor.transpose(tr_ps[bank][:, col * P:(col + 1) * P], pr[u % 2][:, z // 3, z % 3, :], c.ident[:])
                        if z == 3 or z == 5:
                            ins.then_inc(tr_s[bank], 1)

                def values(b, u):
                    for bank in range(2):
                        pe.wait_ge(tr_ev[bank], use(b, u) + 1)
                    if u == 0:
                        pe.wait_ge(vals_s, b.i + 1)
                    if u % 2 == 0:
                        wait(pe, out_ev, UNITS // 2 * b.i + u // 2)
                    for a in range(2):
                        h = 2 * u + a
                        for j in range(TJ):
                            at0 = ((h % 4) * TJ + j) * (D + 1)
                            for k in range(j + 1):
                                ins = nc.tensor.matmul(out_ps[:, at0:at0 + D + 1], prT[u % 2][:, a, j + k, :],
                                                       v1[b.s][:, k, h, :], start=(k == 0), stop=(k == j))
                    if u % 2:
                        ins.then_inc(pv_s, 1)

                def logits(b):
                    for j in range(TJ):
                        pe.wait_ge(tr_ev[j], use_xn(b) + 1)
                    wait(pe, pair_s, b.i)
                    for j in range(TJ):
                        for k in range(KC):
                            ins = nc.tensor.matmul(route_ps[:, j * E1:(j + 1) * E1], xnT[:, k, j * P:(j + 1) * P],
                                                   wr[:, k, :], start=(k == 0), stop=(k == KC - 1))
                    ins.then_inc(logit_s, 1)

                def gate_up(b, n):
                    pe.wait_ge(freed, FB1 * b.i + n + 1)
                    for w, col in ((wg, 0), (wu, T)):
                        for k in range(KC):
                            ins = nc.tensor.matmul(ffn_ps[n % 2][0:width(n), col:col + T], w[:, k, n * P:n * P + width(n)],
                                                   xnT[:, k, :], start=(k == 0), stop=(k == KC - 1))
                    ins.then_inc(gu_s, 1)

                def ranks(b):
                    pe.wait_ge(chosen_s, b.i + 1)
                    for r, parts in enumerate((((c.before, 0),), ((c.before, 1), (c.ones, 0)), ((c.ones, 0), (c.ones, 1)))):
                        for n, (lhs, j) in enumerate(parts):
                            ins = nc.tensor.matmul(route_ps[:, (2 + r) * E1:(3 + r) * E1], lhs[:], chosen[:, j, :],
                                                   start=(n == 0), stop=(n == len(parts) - 1))
                    ins.then_inc(rank_s, 1)

                def down(b, j):
                    pe.wait_ge(freed, FB1 * b.i + M1 + j + 1 + (j == 0))
                    for k in range(M1):
                        ins = nc.tensor.matmul(ffn_ps[j][:], hT[0:width(k), k, j * P:(j + 1) * P], wd[0:width(k), k, :],
                                               start=(k == 0), stop=(k == M1 - 1))
                    ins.then_inc(down_s, 1)

                def behind(b, u):
                    if u == 0:
                        pe.wait_ge(norm2.done_s, 2 * b.i + 2)
                        to_channels(xn, use_xn(b))
                        logits(b)
                    elif u - 1 < M1:
                        gate_up(b, u - 1)
                    else:
                        down(b, 0)
                    if u == 3:
                        ranks(b)

                def turn(b):
                    for u in range(UNITS):
                        if not b.first:
                            behind(b.before(), u)
                        transpose(b, u)
                        if u < UNITS - 1:
                            scores(b, u + 1)
                        values(b, u)
                        if u == PRE_AT and not b.last:
                            pre(b.after())
                    if not b.last:
                        scores(b.after(), 0)
                    if not b.first:
                        down(b.before(), 1)

                pe.wait_ge(ones_s, 2)
                pre(FIRST)
                scores(FIRST, 0)
                pe.wait_ge(weights_in, 5 * 16)
                turns(pe, B, turn)
                for u in range(UNITS):
                    behind(LAST, u)
                down(LAST, 1)

            @block.scalar
            def _(act):
                def emptied(b, n, dst, scale=1.0):
                    act.wait_ge(tr_s[1], n + 1)
                    nc.scalar.activation(columns(dst, 1), blocks(tr_ps[1]), ACT.Copy, scale=scale).then_inc(tr_ev[1], 1)

                def norm_pre(b):
                    if not b.first:
                        act.wait_ge(tr_s[0], use_pre(b.before(), 0) + 1)
                        act.wait_ge(tr_s[1], use_pre(b.before(), 0) + 1)
                    norm1.act(nc, act, b, q_tok, x[b.s])

                def pre(b):
                    if not b.first:
                        wait(act, score_s, UNITS * (b.i - 1))
                    emptied(b, use_pre(b, 0), qT[b.s], D ** -0.5)
                    emptied(b, use_pre(b, 1), kT[b.s])

                def exps(b, u):
                    act.wait_ge(max_s, 2 * (UNITS * b.i + u + 1))
                    for a in range(2):
                        for j in range(TJ):
                            nc.scalar.activation(
                                pr[u % 2][:, a, j:2 * j + 1, :].rearrange("p k t -> p (k t)"),
                                score_ps[:, a, j * P:(2 * j + 1) * P],
                                ACT.Exp, bias=nmax[u % 2][:, a, j:j + 1]).then_inc(exp_s, 1)

                def probs(b, u):
                    act.wait_ge(tr_s[1], use(b, u) + 1)
                    nc.scalar.copy(prT[u % 2][:, 1, 1:3, :].rearrange("p k t -> p (k t)"), tr_ps[1][:, 0:2 * P]).then_inc(tr_ev[1], 1)

                def norm_post(b):
                    if not b.first:
                        wait(act, xn_out[1 - b.s], 16 * (b.before().round + 1))
                    norm2.act(nc, act, b, xn, x3[b.s])

                def behind(b, u):
                    if u == 0:
                        wait(act, gu_s, M1 * b.i)
                        emptied(b, use_xn(b), xnT)
                    elif u - 1 < M1:
                        n = u - 1
                        act.wait_ge(gu_s, M1 * b.i + n + 1)
                        nc.scalar.activation(tg[n % 2][0:width(n)], ffn_ps[n % 2][0:width(n), 0:T], ACT.Tanh, scale=0.5).then_inc(tg_s, 1)

                def logit_exps(b):
                    act.wait_ge(nlmax_s, b.i + 1)
                    for j in range(TJ):
                        nc.scalar.activation(es[:, j, :], route_ps[:, j * E1:(j + 1) * E1], ACT.Exp, bias=nlmax[:, j:j + 1],
                                             accum_out=essum[:, j:j + 1]).then_inc(es_s, 1)

                def turn(b):
                    if not b.first:
                        norm_post(b.before())
                    exps(b, 0)
                    for u in range(UNITS):
                        if not b.first:
                            behind(b.before(), u)
                        probs(b, u)
                        if u < UNITS - 1:
                            exps(b, u + 1)
                        if u == 0 and not b.first:
                            logit_exps(b.before())
                        if u == PRE_AT - 1 and not b.last:
                            norm_pre(b.after())
                        if u == PRE_AT and not b.last:
                            pre(b.after())

                norm_pre(FIRST)
                pre(FIRST)
                turns(act, B, turn)
                norm_post(LAST)
                behind(LAST, 0)
                logit_exps(LAST)
                for u in range(1, UNITS):
                    behind(LAST, u)

            @block.gpsimd
            def _(pool):
                def values(b):
                    pool.wait_ge(ctx_in[b.s], 16 * (b.round + 1))
                    if not b.first:
                        wait(pool, pv_s, UNITS // 2 * (b.i - 1))
                    alone(pool)
                    nc.gpsimd.tensor_copy(v1[b.s][:, :, :, 0:D], ctx[b.s][:].rearrange("p j (h d) -> p j h d", d=D)).then_inc(vals_s, 1)

                def merge(b):
                    pool.wait_ge(x_in[b.s], 16 * (1 + K0) * (b.round + 1))
                    for k in range(K0):
                        if k:
                            pool.wait_ge(merged, K0 * b.i + k)
                        nc.gpsimd.tensor_tensor(x[b.s][:], x[b.s][:], y0[b.s][:, k], ALU.add).then_inc(merged, 1)

                def scatter(b):
                    pool.wait_ge(pair_s, b.i + 1)
                    alone(pool)
                    for j in range(TJ):
                        for k in range(K1):
                            nc.gpsimd.indirect_dma_start(
                                io["list1"], bass.IndirectOffsetOnAxis(ap=pos[b.s][:, j, k:k + 1], axis=0),
                                pair[b.s][:, j, k, :], None, bounds_check=E1 * CAP - 1, oob_is_err=False).then_inc(scat[b.s], 16)

                def turn(b):
                    if not b.first:
                        norm2.pool(nc, pool, b.before())
                    if not b.last:
                        merge(b.after())
                        norm1.pool(nc, pool, b.after())
                        values(b.after())
                    if not b.first:
                        scatter(b.before())

                for s in range(2):
                    nc.gpsimd.memset(v1[s][:, :, :, D:], 1.0).then_inc(ones_s, 1)
                merge(FIRST)
                norm1.pool(nc, pool, FIRST)
                values(FIRST)
                turns(pool, B, turn)
                norm2.pool(nc, pool, LAST)
                scatter(LAST)
                for s in range(2):
                    pool.wait_ge(scat[s], 16 * TJ * K1 * (B // 2))

            @block.vector
            def _(dve):
                posts = Chain(dve, post_c, POST_STEPS1)
                v = nc.vector

                def emptied(b, n, dst, scale=None):
                    dve.wait_ge(tr_s[0], n + 1)
                    if scale is None:
                        v.tensor_copy(columns(dst, 0), blocks(tr_ps[0])).then_inc(tr_ev[0], 1)
                    else:
                        v.tensor_scalar(columns(dst, 0), blocks(tr_ps[0]), scale, None, ALU.mult).then_inc(tr_ev[0], 1)

                def norm_pre(b):
                    dve.wait_ge(merged, K0 * (b.i + 1))
                    norm1.dve(nc, dve, b, x[b.s])

                def pre(b):
                    if not b.first:
                        wait(dve, score_s, UNITS * (b.i - 1))
                    emptied(b, use_pre(b, 0), qT[b.s], D ** -0.5)
                    emptied(b, use_pre(b, 1), kT[b.s])

                def maxima(b, u):
                    dve.wait_ge(score_s, UNITS * b.i + u + 1)
                    for j in range(TJ):
                        v.tensor_reduce(nmax[u % 2][:, :, j], score_ps[:, :, j * P:(2 * j + 1) * P],
                                        AX.X, ALU.max, negate=True).then_inc(max_s, 1)

                def probs(b, u):
                    dve.wait_ge(tr_s[0], use(b, u) + 1)
                    v.tensor_copy(prT[u % 2][:].rearrange("p a k t -> p (a k t)")[:, 0:4 * P], tr_ps[0][:]).then_inc(tr_ev[0], 1)

                def outputs(b, g):
                    dve.wait_ge(pv_s, UNITS // 2 * b.i + g + 1)
                    o = out_ps[:, 0:4 * TJ * (D + 1)].rearrange("p (h j d) -> p j h d", j=TJ, d=D + 1)
                    r = rden[:].rearrange("p (j h) -> p j h", j=TJ)
                    v.reciprocal(r, o[:, :, :, D]).then_inc(out_c, 1)
                    dve.wait_ge(out_c, UNITS // 2 * b.i + g + 1)
                    v.tensor_tensor(at[:, :, 4 * g:4 * g + 4, :], o[:, :, :, 0:D],
                                    r.unsqueeze(3).to_broadcast([P, TJ, 4, D]), ALU.mult).then_inc(out_ev, 1)

                def residual(b):
                    dve.wait_ge(out_ev, UNITS // 2 * (b.i + 1))
                    wait(dve, x3_out[b.s], 16 * b.round)
                    v.scalar_tensor_tensor(x3[b.s][:].rearrange("p j c -> p (j c)"), at[:].rearrange("p j h d -> p (j h d)"),
                                           c.gate[:, 1:2], x[b.s][:].rearrange("p j c -> p (j c)"), ALU.mult, ALU.add).then_inc(x3_s, 1)
                    dve.wait_ge(x3_s, b.i + 1)
                    norm2.dve(nc, dve, b, x3[b.s])

                def logit_max(b):
                    posts.turn(b.i)
                    dve.wait_ge(logit_s, b.i + 1)
                    v.tensor_reduce(nlmax[:], route_ps[:, 0:TJ * E1].rearrange("p (j e) -> p j e", j=TJ), AX.X, ALU.max,
                                    negate=True).then_inc(nlmax_s, 1)

                def route(b):
                    dve.wait_ge(es_s, TJ * (b.i + 1))
                    posts.need(posts.did(v.reciprocal(esr[:], essum[:])))
                    for j in range(TJ):
                        n = posts.did(v.tensor_scalar(es[:, j, :], es[:, j, :], esr[:, j:j + 1], None, ALU.mult))
                    posts.need(n)
                    alone(dve)
                    for j in range(TJ):
                        n = posts.did(v.max(top[:, j, :], es[:, j, :]))
                    posts.need(n)
                    alone(dve)
                    for j in range(TJ):
                        n = posts.did(v.max_index(sel[:, j, :], top[:, j, :], es[:, j, :]))
                    posts.need(n)
                    posts.need(posts.did(v.tensor_copy(self_[:], sel[:, :, 0:K1])))
                    for j in range(TJ):
                        n = posts.did(v.tensor_tensor(hot[:, j], c.expert_no[:].unsqueeze(1).to_broadcast([P, K1, E1]),
                                                      self_[:, j, :].unsqueeze(2).to_broadcast([P, K1, E1]), ALU.is_equal))
                    posts.need(n)
                    wait(dve, rank_s, b.i)
                    with nc.allow_low_precision(reason="each sum is 0 or 1"):
                        v.tensor_reduce(chosen[:], hot[:].rearrange("p j k e -> p j e k"), AX.X, ALU.add).then_inc(chosen_s, 1)

                def slots(b):
                    dve.wait_ge(rank_s, b.i + 1)
                    wait(dve, scat[b.s], 16 * TJ * K1 * b.round)
                    every = [P, TJ, E1]
                    n = posts.did(v.tensor_tensor(slot[:], route_ps[:, TJ * E1:2 * TJ * E1].rearrange("p (j e) -> p j e", e=E1),
                                                  c.base1[:].unsqueeze(1).to_broadcast(every), ALU.add))
                    posts.need(n)
                    posts.need(posts.did(v.tensor_tensor(over[:], slot[:], limit[:].unsqueeze(1).to_broadcast(every), ALU.is_ge)))
                    posts.need(posts.did(v.scalar_tensor_tensor(slot[:].rearrange("p j e -> p (j e)"), over[:].rearrange("p j e -> p (j e)"),
                                                                float(2 * E1 * CAP), slot[:].rearrange("p j e -> p (j e)"), ALU.mult, ALU.add)))
                    for j in range(TJ):
                        n = posts.did(v.tensor_tensor(pick[:, j], hot[:, j], slot[:, j, :].unsqueeze(1).to_broadcast([P, K1, E1]), ALU.mult))
                    numbered = posts.did(v.tensor_copy(pair[b.s][:, :, :, 0], tok[:].unsqueeze(2).to_broadcast([P, TJ, K1])))
                    posts.did(v.tensor_scalar(pair[b.s][:, :, :, 1].bitcast(F32), top[:, :, 0:K1], c.gate[:, 3:4], None, ALU.mult))
                    posts.did(v.tensor_tensor(c.base1[:], c.base1[:], route_ps[:, 2 * TJ * E1:(2 * TJ + 1) * E1], ALU.add))
                    posts.need(n)
                    n = posts.did(v.tensor_reduce(posf[:].rearrange("p j k -> p (j k)"), pick[:].rearrange("p j k e -> p (j k) e"),
                                                  AX.X, ALU.add))
                    posts.need(numbered)
                    posts.did(v.tensor_scalar(tok[:], tok[:], float(T), None, ALU.add))
                    posts.need(n)
                    v.tensor_copy(pos[b.s][:], posf[:]).then_inc(pair_s, 1)

                def hidden(b, n):
                    dve.wait_ge(tg_s, M1 * b.i + n + 1)
                    s, r = n % 2, width(n)
                    posts.need(posts.did(v.scalar_tensor_tensor(sg[s][0:r], tg[s][0:r], 1.0, ffn_ps[s][0:r, 0:T], ALU.add, ALU.mult)))
                    if n == 0:
                        wait(dve, down_s, TJ * b.i)
                    v.tensor_tensor(hT[0:r, n, :], sg[s][0:r], ffn_ps[s][0:r, T:2 * T], ALU.mult).then_inc(freed, 1)

                def shared(b, j):
                    dve.wait_ge(down_s, TJ * b.i + j + 1)
                    v.scalar_tensor_tensor(x3[b.s][:, j, :], ffn_ps[j][:], c.gate_half[:, 3:4], x3[b.s][:, j, :],
                                           ALU.mult, ALU.add).then_inc(freed, 1)

                def behind(b, u):
                    if u == 0:
                        wait(dve, gu_s, M1 * b.i)
                        emptied(b, use_xn(b), xnT)
                    elif u - 1 < M1:
                        hidden(b, u - 1)

                def turn(b):
                    for u in range(UNITS):
                        if not b.first:
                            behind(b.before(), u)
                        probs(b, u)
                        if u < UNITS - 1:
                            maxima(b, u + 1)
                        if u == 0 and not b.first:
                            logit_max(b.before())
                        if u == 1 and not b.first:
                            route(b.before())
                        if u == 3 and not b.first:
                            slots(b.before())
                        if u % 2:
                            outputs(b, u // 2)
                        if u == PRE_AT - 2 and not b.last:
                            norm_pre(b.after())
                        if u == PRE_AT and not b.last:
                            pre(b.after())
                    residual(b)
                    if not b.first:
                        shared(b.before(), 0)
                    if not b.last:
                        maxima(b.after(), 0)
                    if not b.first:
                        shared(b.before(), 1)

                v.engine_nop().then_inc(freed, 2)
                n = 0
                for ins in (v.tensor_scalar(c.base1[:], c.expert_no[:], float(CAP), None, ALU.mult),
                            v.tensor_scalar(limit[:], c.expert_no[:], float(CAP), float(CAP), ALU.mult, ALU.add),
                            v.tensor_scalar(tok[:], c.token_no[:], -float(N), None, ALU.add)):
                    ins.then_inc(init_s, 1)
                dve.wait_ge(init_s, 3)
                norm_pre(FIRST)
                pre(FIRST)
                maxima(FIRST, 0)
                turns(dve, B, turn)
                behind(LAST, 0)
                logit_max(LAST)
                route(LAST)
                for u in range(1, 4):
                    behind(LAST, u)
                slots(LAST)
                for u in range(4, UNITS):
                    behind(LAST, u)
                for j in range(TJ):
                    shared(LAST, j)


def routed1_phase(nc, io, c):
    with Memory(nc, "routed1_") as m:
        HW = -(-H1 // P)
        GU = KC * H1
        wgu = [m.sb(f"wgu_{s}", [P, 2 * GU + HW * P - H1]) for s in range(SLOTS1)]
        wdn = [m.sb(f"wdn_{s}", [P, HW, C]) for s in range(SLOTS1)]
        pair = [m.sb(f"pair_{s}", [CAP, 2], I32) for s in range(WAYS1)]
        xg = [m.sb(f"xg_{s}", [CAP, C]) for s in range(SLOTS1)]
        xT = [m.sb(f"xT_{s}", [P, KC, CAP]) for s in range(2)]
        sg = [m.sb(f"silu_gate_{s}", [P, HW * CAP]) for s in range(2)]
        hT = [m.sb(f"hT_{s}", [P, HW, CAP]) for s in range(2)]
        ys = [m.sb(f"ys_{s}", [CAP, C]) for s in range(2)]
        xt_ps = [m.ps(f"xt_ps{n}") for n in range(2)]
        gu_ps = [m.ps(f"gu_ps{n}") for n in range(2)]
        y_ps = [m.ps(f"y_ps{n}") for n in range(2)]
        pads = m.sem("pads_made")
        up_in = [m.sem(f"gate_up_in{s}") for s in range(SLOTS1)]
        down_in = [m.sem(f"down_in{s}") for s in range(SLOTS1)]
        pair_in = [m.sem(f"pair_in{s}") for s in range(WAYS1)]
        xg_in = [m.sem(f"rows_gathered{s}") for s in range(SLOTS1)]
        xt_s, xt_ev, gu_s = m.sem("x_transposed"), m.sem("x_evacuated"), m.sem("gate_up")
        silu_s, h_s, y_s, ys_s = m.sem("silu_done"), m.sem("h_done"), m.sem("y_ready"), m.sem("y_scaled")
        added = [m.sem(f"rows_added{s}") for s in range(WAYS1)]
        with nc.Block() as block:
            def of(name, e):
                return io[name][bass.ds(e, 1)].rearrange("a r n -> (a r) n")

            def uses(e):
                return e.round * (WAYS1 // SLOTS1) + e.s // SLOTS1 + 1

            @block.sync
            def _(sp):
                def turn(e):
                    wait(sp, added[e.s], 16 * e.round)
                    alone(sp)
                    sp.dma_start(pair[e.s][:], io["list1"][bass.ds(e.i * CAP, CAP), :]).then_inc(pair_in[e.s], 16)
                    if not isinstance(e.i, int) or e.i >= SLOTS1:
                        sp.wait_ge(gu_s, e.i - SLOTS1 + 1)
                        alone(sp)
                    for n, name in enumerate(("w_gate1", "w_up1")):
                        sp.dma_start(wgu[e.s % SLOTS1][:, n * GU:(n + 1) * GU].rearrange("p (k n) -> p k n", k=KC),
                                     of(name, e.i).rearrange("(k p) n -> p k n", p=P)).then_inc(up_in[e.s % SLOTS1], 16)
                    if not isinstance(e.i, int) or e.i >= SLOTS1:
                        sp.wait_ge(y_s, e.i - SLOTS1 + 1)
                        alone(sp)
                    full = H1 // P
                    w = of("w_down1", e.i)
                    sp.dma_start(wdn[e.s % SLOTS1][:, 0:full, :], w[0:full * P, :].rearrange("(k p) n -> p k n", p=P)).then_inc(down_in[e.s % SLOTS1], 16)
                    sp.dma_start(wdn[e.s % SLOTS1][0:H1 - full * P, full, :], w[full * P:, :]).then_inc(down_in[e.s % SLOTS1], 16)

                rounds(sp, E1, turn, WAYS1)

            @block.gpsimd
            def _(pool):
                def rows_of(e):
                    return bass.IndirectOffsetOnAxis(ap=pair[e.s][:, 0:1].bitcast(U32), axis=0)

                def gather(e):
                    if not isinstance(e.i, int) or e.i >= SLOTS1:
                        pool.wait_ge(xt_s, e.i - SLOTS1 + 1)
                        alone(pool)
                    pool.wait_ge(pair_in[e.s], 16 * (e.round + 1))
                    alone(pool)
                    nc.gpsimd.indirect_dma_start(xg[e.s % SLOTS1][:], None, io["xn1"], rows_of(e)).then_inc(xg_in[e.s % SLOTS1], 16)

                def add(e):
                    pool.wait_ge(ys_s, e.i + 1)
                    alone(pool)
                    if not e.first:
                        pool.wait_ge(added[e.before().s], 16 * (e.before().round + 1))
                        alone(pool)
                    nc.gpsimd.indirect_dma_start(io["out"], rows_of(e), ys[e.s % 2][:], None,
                                                 compute_op=ALU.add).then_inc(added[e.s], 16)

                def turn(e):
                    if not isinstance(e.i, int) or e.i < E1 - AHEAD1:
                        ahead = e
                        for _ in range(AHEAD1):
                            ahead = ahead.after()
                        gather(ahead)
                    if not e.first:
                        add(e.before())

                for s in range(SLOTS1):
                    nc.gpsimd.memset(wgu[s][:, 2 * GU:], 0.0).then_inc(pads, 1)
                ahead = first(E1, WAYS1)
                for n in range(AHEAD1):
                    gather(ahead)
                    ahead = ahead.after()
                turns(pool, E1, turn, WAYS1)
                add(last(E1, WAYS1))
                for s in range(WAYS1):
                    pool.wait_ge(added[s], 16 * (E1 // WAYS1))

            @block.tensor
            def _(pe):
                def inputs(e):
                    pe.wait_ge(xg_in[e.s % SLOTS1], 16 * uses(e))
                    wait(pe, xt_ev, e.i - 1)
                    alone(pe)
                    for k in range(KC):
                        ins = nc.tensor.transpose(xt_ps[e.s % 2][:, k * CAP:(k + 1) * CAP], xg[e.s % SLOTS1][:, k * P:(k + 1) * P],
                                                  c.ident[0:CAP, 0:CAP])
                    ins.then_inc(xt_s, 1)

                def gate_up(e):
                    pe.wait_ge(xt_ev, e.i + 1)
                    pe.wait_ge(up_in[e.s % SLOTS1], 32 * uses(e))
                    wait(pe, h_s, e.i - 1)
                    for n in range(2):
                        for t in range(HW):
                            for k in range(KC):
                                at = n * GU + k * H1 + t * P
                                ins = nc.tensor.matmul(gu_ps[e.s % 2][:, (n * HW + t) * CAP:(n * HW + t + 1) * CAP],
                                                       wgu[e.s % SLOTS1][:, at:at + P], xT[e.s % 2][:, k, :],
                                                       start=(k == 0), stop=(k == KC - 1))
                    ins.then_inc(gu_s, 1)

                def down(e):
                    pe.wait_ge(h_s, e.i + 1)
                    pe.wait_ge(down_in[e.s % SLOTS1], 32 * uses(e))
                    wait(pe, ys_s, e.i)
                    for k in range(HW):
                        r = min(P, H1 - k * P)
                        ins = nc.tensor.matmul(y_ps[e.s % 2][0:CAP, :], hT[e.s % 2][0:r, k, :], wdn[e.s % SLOTS1][0:r, k, :],
                                               start=(k == 0), stop=(k == HW - 1))
                    ins.then_inc(y_s, 1)

                def turn(e):
                    if not e.last:
                        inputs(e.after())
                    gate_up(e)
                    if not e.first:
                        down(e.before())

                pe.wait_ge(pads, SLOTS1)
                inputs(first(E1, WAYS1))
                turns(pe, E1, turn, WAYS1)
                down(last(E1, WAYS1))

            @block.scalar
            def _(act):
                def inputs(e):
                    act.wait_ge(xt_s, e.i + 1)
                    wait(act, gu_s, e.i - 1)
                    nc.scalar.copy(xT[e.s % 2][:].rearrange("p k t -> p (k t)"), xt_ps[e.s % 2][:, 0:KC * CAP]).then_inc(xt_ev, 1)

                def turn(e):
                    if not e.last:
                        inputs(e.after())
                    act.wait_ge(gu_s, e.i + 1)
                    nc.scalar.activation(sg[e.s % 2][:], gu_ps[e.s % 2][:, 0:HW * CAP], ACT.Silu).then_inc(silu_s, 1)

                inputs(first(E1, WAYS1))
                turns(act, E1, turn, WAYS1)

            @block.vector
            def _(dve):
                v = nc.vector

                def scaled(e):
                    dve.wait_ge(y_s, e.i + 1)
                    two = e.before().before()
                    wait(dve, added[two.s], 16 * (two.round + 1))
                    v.tensor_scalar(ys[e.s % 2][:], y_ps[e.s % 2][0:CAP, :], pair[e.s][:, 1:2].bitcast(F32), None,
                                    ALU.mult).then_inc(ys_s, 1)

                def turn(e):
                    dve.wait_ge(silu_s, e.i + 1)
                    wait(dve, y_s, e.i - 1)
                    v.tensor_tensor(hT[e.s % 2][:].rearrange("p t s -> p (t s)"), sg[e.s % 2][:],
                                    gu_ps[e.s % 2][:, HW * CAP:2 * HW * CAP], ALU.mult).then_inc(h_s, 1)
                    if not e.first:
                        scaled(e.before())

                turns(dve, E1, turn, WAYS1)
                scaled(last(E1, WAYS1))


class Constants:

    def __init__(self, m):
        self.ident = m.sb("ident", [P, P])
        self.ident16 = m.sb("ident16", [P, P], BF16)
        self.before = m.sb("before", [P, P], BF16)
        self.ones = m.sb("ones", [P, P], BF16)
        self.causal = m.sb("causal", [P, 3 * P], BF16)
        self.half_power = m.sb("half_power", [P, TJ])
        self.expert_no = m.sb("expert_no", [P, E1])
        self.token_no = m.sb("token_no", [P, TJ])
        self.tile_no = m.sb("tile_no", [P, TILES0])
        self.w, self.u = m.sb("w", [P, KC]), m.sb("u", [P, KC])
        self.gate = m.sb("gate", [P, 4])
        self.gate_half = m.sb("gate_half", [P, 4])
        self.gate_neg = m.sb("gate_neg", [P, 4])
        self.gate_quarter = m.sb("gate_quarter", [P, 4])
        self.base0 = m.sb("base0", [P, E0])
        self.base1 = m.sb("base1", [P, E1])


def build(nc, io):
    with Memory(nc, "") as m:
        c = Constants(m)
        with Memory(nc, "first_ffn_") as f:
            c.wgu0 = f.sb("wgu", [P, E0, KC, 2 * H0])
            c.wgu0_in = f.sem("wgu_in")
            for phase in (setup, wkv_phase, routed0_phase):
                phase(nc, io, c)
        for phase in (attention_phase, routed1_phase):
            phase(nc, io, c)


def laid_out(i):
    def turned(a):
        return np.ascontiguousarray(np.swapaxes(a, -1, -2))

    i = {k: np.ascontiguousarray(v) for k, v in i.items()}
    return {
        "x": i["x"].reshape(N, C), "ctx": i["ctx_2048"].reshape(N, C),
        "g_xattn": i["g_xattn"], "g_ffn": i["g_ffn"], "w": i["L0_xattn_w"], "u": i["L0_xattn_u"],
        "gate_w0": turned(i["L0_ffn_gate_w"]), "se_gate": turned(i["L0_ffn_se_gate_w"]),
        "sh_gate": turned(i["L0_ffn_sh_gate"]), "sh_up": turned(i["L0_ffn_sh_up"]),
        "sh_down": turned(i["L0_ffn_sh_down"]),
        "w_gate0": turned(i["L0_ffn_w_gate"]), "w_up0": turned(i["L0_ffn_w_up"]),
        "w_down0": turned(i["L0_ffn_w_down"]),
        "gate_w1": turned(i["L1_ffn_gate_w"]), "w_gate1": i["L1_ffn_w_gate"], "w_up1": i["L1_ffn_w_up"],
        "w_down1": i["L1_ffn_w_down"], "sw_gate": i["L1_ffn_sw_gate"], "sw_up": i["L1_ffn_sw_up"],
        "sw_down": i["L1_ffn_sw_down"],
    }


SCRATCH = {"x2": ((N, C), F32), "xn0": ((N + DUMMY, C), F32), "xn1": ((N + DUMMY, C), F32),
           "list0": ((LIST0, 3), I32), "y0": ((K0 * N, C), F32), "list1": ((E1 * CAP, 2), I32)}


def kernel(**inputs):
    import concourse.bacc as _bacc
    from concourse.bass_utils import run_bass_kernel_spmd as _run

    nc = _bacc.Bacc("TRN2", target_bir_lowering=False, num_devices=1)
    arrays = laid_out(inputs)
    io = {name: nc.dram_tensor(f"in_{name}", a.shape, mybir.dt.from_np(a.dtype), kind="ExternalInput").ap()
          for name, a in arrays.items()}
    io["out"] = nc.dram_tensor("out_0", (N + DUMMY, C), F32, kind="ExternalOutput").ap()
    for name, (shape, dt) in SCRATCH.items():
        io[name] = nc.dram_tensor(name, shape, dt, kind="Internal").ap()
    build(nc, io)
    r = _run(nc, [{f"in_{name}": a for name, a in arrays.items()}], core_ids=[0])
    return r.results[0]["out_0"][:N].reshape(B, T, C)
```

```python
import numpy as np
import concourse.bass as bass
from concourse import mybir
from contextlib import ExitStack

F32 = mybir.dt.float32
BF16 = mybir.dt.bfloat16
F32R = mybir.dt.float32r
I32 = mybir.dt.int32
U32 = mybir.dt.uint32
ALU = mybir.AluOpType
ACT = mybir.ActivationFunctionType
AX = mybir.AxisListType

P = 128
B, T, C = 16, 256, 512
N = B * T
KC = C // P
TJ = T // P
EPS = 1e-5
DUMMY = P
E0, H0, S0, K0 = 8, 256, 512, 2
E1, H1, S1, K1, CAP = 64, 352, 704, 6, 64
TILES0 = N * K0 // P + E0
UNUSED = 2 * K0 * N
LIST0 = E0 * N + P
HEADS, D = 16, 32
M0 = S0 // P
FB0 = M0 + TJ
M1 = -(-S1 // P)
FB1 = TJ + M1 + TJ
POST_STEPS1 = 38
WAYS1, SLOTS1, AHEAD1 = 8, 4, 4
WAYS0, SLOTS0, AHEAD0 = 8, 4, 3
WKV_STEPS, EXP_STEPS, POST_STEPS0, TABLE_STEPS0 = 18, 15, 24, 15
UNITS = HEADS // 2
PRE_AT = 4
USES = UNITS + 2
NEG = -1e30
BEFORE_ALL = -1e38


def wait(eng, sem, value):
    if not isinstance(value, int) or value > 0:
        eng.wait_ge(sem, value)


def alone(eng):
    eng.nop(nofuse=True)


class Chain:

    def __init__(self, eng, sem, per_turn):
        self.eng, self.sem, self.per, self.n, self.base = eng, sem, per_turn, 0, 0

    def turn(self, i):
        assert self.n in (0, self.per), (self.n, self.per)
        self.n, self.base = 0, i * self.per

    def resume(self, i):
        self.base = i * self.per

    def did(self, ins):
        ins.then_inc(self.sem, 1)
        self.n += 1
        return self.n

    def need(self, n):
        self.eng.wait_ge(self.sem, self.base + n)


class Turn:

    def __init__(self, i, round, s, count, ways=2):
        self.i, self.round, self.s, self.count, self.ways = i, round, s, count, ways
        self.first = isinstance(i, int) and i == 0
        self.last = isinstance(i, int) and i == count - 1
        self.third = not isinstance(i, int) or i >= 2

    def before(self):
        wrap = self.s == 0
        return Turn(self.i - 1, self.round - wrap, (self.s - 1) % self.ways, self.count, self.ways)

    def after(self):
        wrap = self.s == self.ways - 1
        return Turn(self.i + 1, self.round + wrap, (self.s + 1) % self.ways, self.count, self.ways)


def first(count, ways=2):
    return Turn(0, 0, 0, count, ways)


def last(count, ways=2):
    return Turn(count - 1, count // ways - 1, ways - 1, count, ways)


def turns(eng, count, turn, ways=2):
    assert count % ways == 0
    for n in range(ways + 1):
        turn(Turn(n, n // ways, n % ways, count, ways))
    with eng.Fori(1, count // ways - 1) as j:
        for n in range(1, ways + 1):
            turn(Turn(ways * j + n, j + n // ways, n % ways, count, ways))
    for n in range(count - ways + 1, count):
        turn(Turn(n, n // ways, n % ways, count, ways))


def rounds(eng, count, turn, ways):
    for n in range(ways):
        turn(Turn(n, 0, n, count, ways))
    with eng.Fori(1, count // ways) as j:
        for n in range(ways):
            turn(Turn(ways * j + n, j, n, count, ways))


FIRST, LAST = first(B), last(B)


class Memory:

    def __init__(self, nc, phase):
        self.nc, self.phase, self.stack = nc, phase, ExitStack()

    def sb(self, name, shape, dt=F32):
        return self.stack.enter_context(self.nc.sbuf_tensor(self.phase + name, shape, dt))

    def ps(self, name, shape=(P, 512), dt=F32):
        return self.stack.enter_context(self.nc.psum_tensor(self.phase + name, list(shape), dt))

    def sem(self, name):
        return self.stack.enter_context(self.nc.semaphore(self.phase + name))

    def __enter__(self):
        return self

    def __exit__(self, *a):
        self.stack.close()


def rows(dram, b):
    return dram[bass.ds(b.i * T, T), :].rearrange("(j p) c -> p j c", p=P)


def setup(nc, io, c):
    with Memory(nc, "setup_") as m:
        ones_row = m.sb("ones_row", [1, P])
        gates_in = m.sb("gates_in", [1, 4])
        zeros = m.sb("zeros", [P, C])
        slot_no = m.sb("slot_no", [P, LIST0 // P], I32)
        slot_low = m.sb("slot_low", [P, LIST0 // P], I32)
        fill = m.sb("fill", [P, LIST0 // P, 3], I32)
        fill1 = m.sb("fill1", [P, E1 * CAP // P, 2], I32)
        gates_ps = m.ps("gates_ps")
        const_s, made, bc_s, dve_s, stored = (m.sem(x) for x in (
            "consts_loaded", "pool_made", "gates_broadcast", "dve_setup", "setup_stored"))
        with nc.Block() as block:
            @block.sync
            def _(sp):
                sp.dma_start(gates_in[:, 0:2], io["g_xattn"][None, :]).then_inc(const_s, 16)
                sp.dma_start(gates_in[:, 2:4], io["g_ffn"][None, :]).then_inc(const_s, 16)
                sp.dma_start(c.w[:], io["w"].rearrange("(k p) -> p k", p=P), allow_slow_non_contiguous=True).then_inc(const_s, 16)
                sp.dma_start(c.u[:], io["u"].rearrange("(k p) -> p k", p=P), allow_slow_non_contiguous=True).then_inc(const_s, 16)
                sp.wait_ge(made, 3)
                for d in (io["xn0"], io["xn1"], io["out"]):
                    sp.dma_start(d[N:N + DUMMY, :], zeros[:]).then_inc(stored, 16)
                sp.wait_ge(dve_s, 7)
                sp.dma_start(io["list0"].rearrange("(p j) c -> p (j c)", p=P),
                             fill[:].rearrange("p j c -> p (j c)")).then_inc(stored, 16)
                sp.dma_start(io["list1"].rearrange("(p j) c -> p (j c)", p=P),
                             fill1[:].rearrange("p j c -> p (j c)")).then_inc(stored, 16)
                sp.wait_ge(const_s, 64)
                sp.wait_ge(stored, 5 * 16)

            @block.gpsimd
            def _(pool):
                nc.gpsimd.memset(c.ident[:], 0.0).then_inc(made, 1)
                nc.gpsimd.memset(ones_row[:], 1.0).then_inc(made, 1)
                nc.gpsimd.memset(zeros[:], 0.0).then_inc(made, 1)
                nc.gpsimd.memset(c.before[:], 1.0).then_inc(made, 1)
                nc.gpsimd.memset(c.ones[:], 1.0).then_inc(made, 1)
                nc.gpsimd.memset(c.causal[:], 0.0).then_inc(made, 1)
                nc.gpsimd.memset(c.half_power[:], -0.5).then_inc(made, 1)
                nc.gpsimd.iota(slot_no[:], [[1, LIST0 // P]], base=0, channel_multiplier=LIST0 // P).then_inc(made, 1)
                nc.gpsimd.iota(c.expert_no[:], [[1, E1]], base=0, channel_multiplier=0,
                               allow_small_or_imprecise_dtypes=True).then_inc(made, 1)
                nc.gpsimd.iota(c.token_no[:], [[P, TJ]], base=0, channel_multiplier=1,
                               allow_small_or_imprecise_dtypes=True).then_inc(made, 1)
                nc.gpsimd.iota(c.tile_no[:], [[1, TILES0]], base=0, channel_multiplier=0,
                               allow_small_or_imprecise_dtypes=True).then_inc(made, 1)
                nc.gpsimd.memset(fill[:, :, 2], 0).then_inc(made, 1)
                nc.gpsimd.memset(fill1[:], 0).then_inc(made, 1)
                pool.wait_ge(made, 6)
                nc.gpsimd.affine_select(out=c.ident[:], in_=c.ident[:], compare_op=ALU.not_equal, fill=1.0,
                                        base=0, pattern=[[-1, P]], channel_multiplier=1).then_inc(made, 1)
                nc.gpsimd.affine_select(out=c.before[:], in_=c.before[:], compare_op=ALU.is_gt, fill=0.0,
                                        base=0, pattern=[[1, P]], channel_multiplier=-1).then_inc(made, 1)
                for col in (0, 2 * P):
                    nc.gpsimd.affine_select(out=c.causal[:, col:col + P], in_=c.causal[:, col:col + P], compare_op=ALU.is_ge,
                                            fill=NEG, base=0, pattern=[[-1, P]], channel_multiplier=1).then_inc(made, 1)

            @block.tensor
            def _(pe):
                pe.wait_ge(const_s, 64)
                pe.wait_ge(made, 2)
                nc.tensor.matmul(gates_ps[:, 0:4], ones_row[:], gates_in[:], start=True, stop=True).then_inc(bc_s, 1)

            @block.scalar
            def _(act):
                act.wait_ge(bc_s, 1)
                nc.scalar.activation(c.gate[:], gates_ps[:, 0:4], ACT.Tanh).then_inc(bc_s, 1)

            @block.vector
            def _(dve):
                dve.wait_ge(made, 17)
                nc.vector.tensor_single_scalar(slot_low[:], slot_no[:], P - 1, ALU.bitwise_and).then_inc(dve_s, 1)
                dve.wait_ge(dve_s, 1)
                nc.vector.tensor_scalar(fill[:, :, 0], slot_low[:], float(N), None, ALU.add).then_inc(dve_s, 1)
                nc.vector.memset(fill[:, :, 1], UNUSED).then_inc(dve_s, 1)
                nc.vector.tensor_copy(c.ident16[:], c.ident[:]).then_inc(dve_s, 1)
                nc.vector.tensor_scalar(c.base0[:], c.expert_no[:, 0:E0], float(N), None, ALU.mult).then_inc(dve_s, 1)
                nc.vector.memset(c.base1[:], 0.0).then_inc(dve_s, 1)
                n1 = E1 * CAP // P
                dve.wait_ge(dve_s, 2)
                nc.vector.tensor_copy(fill1[:, :, 0], fill[:, 0:n1, 0]).then_inc(dve_s, 1)
                dve.wait_ge(bc_s, 2)
                nc.vector.tensor_scalar(c.gate_half[:], c.gate[:], 0.5, None, ALU.mult).then_inc(dve_s, 1)
                dve.wait_ge(const_s, 64)
                nc.vector.tensor_scalar(c.u_neg[:], c.u[:], -1.0, None, ALU.mult).then_inc(dve_s, 1)
                nc.vector.tensor_scalar(c.gate_neg[:], c.gate[:], -0.5, None, ALU.mult).then_inc(dve_s, 1)
                nc.vector.tensor_scalar(c.gate_quarter[:], c.gate[:], 0.25, None, ALU.mult).then_inc(dve_s, 1)


class Norm:

    def __init__(self, m, c, tag):
        self.c = c
        self.stats = m.sb(f"{tag}_stats", [P, TJ, 6])
        self.mv = m.sb(f"{tag}_mean_var", [P, TJ, 2])
        self.var = m.sb(f"{tag}_var_eps", [P, TJ])
        self.neg = m.sb(f"{tag}_neg_mean", [P, TJ])
        self.rstd = m.sb(f"{tag}_rstd", [P, TJ])
        self.shift = m.sb(f"{tag}_shift", [P, TJ])
        self.stats_s = m.sem(f"{tag}_stats_s")
        self.rstd_s = m.sem(f"{tag}_rstd_s")
        self.done_s = m.sem(f"{tag}_normed_s")

    def dve(self, nc, dve, b, x):
        wait(dve, self.rstd_s, 4 * b.i)
        for j in range(TJ):
            nc.vector.bn_stats(self.stats[:, j, :], x[:, j, :]).then_inc(self.stats_s, 1)
        for j in range(TJ):
            dve.wait_ge(self.stats_s, 4 * b.i + 1 + j)
            alone(dve)
            nc.vector.bn_aggr(self.mv[:, j, :], self.stats[:, j, :]).then_inc(self.stats_s, 1)

    def pool(self, nc, pool, b):
        pool.wait_ge(self.stats_s, 4 * b.i + 4)
        wait(pool, self.done_s, 2 * b.i)
        alone(pool)
        nc.gpsimd.tensor_scalar(self.var[:], self.mv[:, :, 1], EPS, None, ALU.add).then_inc(self.rstd_s, 1)
        nc.gpsimd.tensor_scalar(self.neg[:], self.mv[:, :, 0], -1.0, None, ALU.mult).then_inc(self.rstd_s, 1)
        pool.wait_ge(self.rstd_s, 4 * b.i + 2)
        nc.gpsimd.tensor_tensor(self.rstd[:], self.var[:], self.c.half_power[:], ALU.pow).then_inc(self.rstd_s, 1)
        pool.wait_ge(self.rstd_s, 4 * b.i + 3)
        nc.gpsimd.tensor_tensor(self.shift[:], self.neg[:], self.rstd[:], ALU.mult).then_inc(self.rstd_s, 1)

    def act(self, nc, act, b, out, x):
        act.wait_ge(self.rstd_s, 4 * b.i + 4)
        for j in range(TJ):
            nc.scalar.activation(out[:, j, :], x[:, j, :], ACT.Identity, bias=self.shift[:, j:j + 1],
                                 scale=self.rstd[:, j:j + 1]).then_inc(self.done_s, 1)


def columns(ap, j):
    return ap[:, :, j * P:(j + 1) * P]


def blocks(bank):
    return bank[:].rearrange("p (k t) -> p k t", t=P)


def product(nc, out, a, b, start, stop):
    for n, (i, j) in enumerate(((0, 0), (0, 1), (1, 0))):
        ins = nc.tensor.matmul(out, a[i], b[j], start=start and n == 0, stop=stop and n == 2)
    return ins


def wkv_phase(nc, io, c):
    with Memory(nc, "wkv_") as m:
        x = [m.sb(f"x_{s}", [P, TJ, C]) for s in range(2)]
        ctx = [m.sb(f"ctx_{s}", [P, TJ, C]) for s in range(2)]
        k_tok = m.sb("k_tok", [P, TJ, C])
        kT = [m.sb(f"kT_{s}", [P, KC, T]) for s in range(2)]
        vT = [m.sb(f"vT_{s}", [P, KC, T]) for s in range(2)]
        o, p, q = (m.sb(f"run_{n}", [P, KC, T + 1]) for n in "opq")
        a2, e2, e2v, aq, em, am, ev, yT = (m.sb(n, [P, KC, T]) for n in (
            "decay", "enter", "enter_v", "bonus_q", "bonus_e", "bonus_a", "bonus_v", "yT"))
        x1 = [m.sb(f"x1_{s}", [P, TJ, C]) for s in range(2)]
        xn = m.sb("xn", [P, TJ, C])
        xnT = m.sb("xnT", [P, KC, T])
        tg = [m.sb(f"tanh_gate_{s}", [P, T]) for s in range(2)]
        sg = [m.sb(f"silu_gate_{s}", [P, T]) for s in range(2)]
        hT = m.sb("hT", [P, M0, T])
        wg, wu = m.sb("wg", [P, KC, S0]), m.sb("wu", [P, KC, S0])
        wd = m.sb("wd", [P, M0, C])
        wr = m.sb("wr", [P, KC, E0 + 1])
        lg = m.sb("lg", [P, TJ, E0 + 1])
        top = m.sb("top", [P, TJ, 8])
        at = m.sb("at", [P, TJ, 8], U32)
        atf = m.sb("atf", [P, TJ, K0])
        hot = m.sb("hot", [P, TJ, K0, E0])
        chosen = m.sb("chosen", [P, TJ, E0], BF16)
        slot = m.sb("slot", [P, TJ, E0])
        pick = m.sb("pick", [P, TJ, K0, E0])
        posf = m.sb("posf", [P, TJ, K0])
        pos = [m.sb(f"pos_{s}", [P, TJ, K0], U32) for s in range(2)]
        pair = [m.sb(f"pair_{s}", [P, TJ, K0, 3], I32) for s in range(2)]
        gap = m.sb("gap", [P, TJ, 2])
        tgap = m.sb("tgap", [P, TJ, 2])
        ssc = m.sb("ssc", [P, TJ])
        pre_ps = [m.ps(f"pre_ps{n}") for n in range(2)]
        post_ps = [m.ps(f"post_ps{n}") for n in range(2)]
        ffn_ps = [m.ps(f"ffn_ps{n}") for n in range(2)]
        route_ps = m.ps("route_ps")
        norm1, norm2 = Norm(m, c, "norm1"), Norm(m, c, "norm2")
        x_in = [m.sem(f"x_in{s}") for s in range(2)]
        ctx_in = [m.sem(f"ctx_in{s}") for s in range(2)]
        weights_in, init_s = m.sem("weights_in"), m.sem("state_init")
        pre_tr, pre_ev = m.sem("pre_transposed"), m.sem("pre_evacuated")
        wkv_c, post_c = m.sem("dve_wkv_steps"), m.sem("dve_post_steps")
        exps, products = m.sem("exps"), m.sem("pool_products")
        y_done, y_tr, x1_s = m.sem("y_done"), m.sem("y_transposed"), m.sem("x1_done")
        xn_tr, xn_ev = m.sem("xn_transposed"), m.sem("xn_evacuated")
        logit_s, chosen_s, rank_s = m.sem("logits"), m.sem("chosen_done"), m.sem("ranks")
        gap_s, tgap_s = m.sem("gap_done"), m.sem("tanh_gap")
        gu_s, tg_s, freed = m.sem("gate_up"), m.sem("tanh_of_gate"), m.sem("ffn_bank_read")
        down_s, pair_s = m.sem("down"), m.sem("pairs")
        scat = [m.sem(f"scattered{s}") for s in range(2)]
        xn_out = [m.sem(f"xn_out{s}") for s in range(2)]
        x2_out = [m.sem(f"x2_out{s}") for s in range(2)]
        with nc.Block() as block:
            @block.sync
            def _(sp):
                def load(b):
                    if not b.first:
                        wait(sp, x1_s, TJ * (b.i - 1))
                        alone(sp)
                        wait(sp, pre_tr, 4 * (b.i - 1))
                        alone(sp)
                    sp.dma_start(x[b.s][:], rows(io["x"], b)).then_inc(x_in[b.s], 16)
                    sp.dma_start(ctx[b.s][:], rows(io["ctx"], b)).then_inc(ctx_in[b.s], 16)

                def store_xn(b):
                    sp.wait_ge(norm2.done_s, 2 * b.i + 2)
                    alone(sp)
                    sp.dma_start(rows(io["xn0"], b), xn[:]).then_inc(xn_out[b.s], 16)

                def store_x2(b):
                    sp.wait_ge(freed, 2 + FB0 * (b.i + 1))
                    alone(sp)
                    sp.dma_start(rows(io["x2"], b), x1[b.s][:]).then_inc(x2_out[b.s], 16)

                def turn(b):
                    if not b.first:
                        if not b.last:
                            load(b.after())
                        store_xn(b.before())
                    if b.third:
                        store_x2(b.before().before())

                load(FIRST)
                for t, name in ((wr[:, :, 0:E0], "gate_w0"), (wr[:, :, E0:], "se_gate"),
                                (wg[:], "sh_gate"), (wu[:], "sh_up"), (wd[:], "sh_down")):
                    sp.dma_start(t, io[name].rearrange("(k p) n -> p k n", p=P),
                                 allow_slow_non_contiguous=name == "se_gate").then_inc(weights_in, 16)
                load(FIRST.after())
                for n, name in enumerate(("w_gate0", "w_up0")):
                    for e in range(E0):
                        sp.dma_start(c.wgu0[:, e, :, n * H0:(n + 1) * H0],
                                     io[name][e].rearrange("(k p) n -> p k n", p=P)).then_inc(c.weights0_in, 16)
                turns(sp, B, turn)
                store_xn(LAST)
                store_x2(LAST.before())
                store_x2(LAST)
                sp.wait_ge(c.weights0_in, 16 * 2 * E0)
                for s in range(2):
                    sp.wait_ge(xn_out[s], 16 * (B // 2))
                    sp.wait_ge(x2_out[s], 16 * (B // 2))

            @block.tensor
            def _(pe):
                def pre(b):
                    for n, src in enumerate((k_tok, ctx[b.s])):
                        if n == 0:
                            pe.wait_ge(norm1.done_s, 2 * b.i + 2)
                        else:
                            pe.wait_ge(ctx_in[b.s], 16 * (b.round + 1))
                        for j in range(TJ):
                            wait(pe, pre_ev, 4 * b.i + 2 * n + j - 1)
                            for k in range(KC):
                                ins = nc.tensor.transpose(blocks(pre_ps[j])[:, k, :], src[:, j, k * P:(k + 1) * P], c.ident[:])
                            ins.then_inc(pre_tr, 1)

                def post_y(b):
                    pe.wait_ge(y_done, b.i + 1)
                    wait(pe, xn_ev, 2 * b.i)
                    for j in range(TJ):
                        for k in range(KC):
                            ins = nc.tensor.transpose(blocks(post_ps[j])[:, k, :], yT[:, k, j * P:(j + 1) * P], c.ident[:])
                        ins.then_inc(y_tr, 1)

                def post_xn(b):
                    for j in range(TJ):
                        pe.wait_ge(norm2.done_s, 2 * b.i + j + 1)
                        for k in range(KC):
                            ins = nc.tensor.transpose(blocks(post_ps[j])[:, k, :], xn[:, j, k * P:(k + 1) * P], c.ident[:])
                        ins.then_inc(xn_tr, 1)

                def logits(b):
                    pe.wait_ge(xn_ev, 2 * b.i + 2)
                    wait(pe, pair_s, b.i)
                    for j in range(TJ):
                        for k in range(KC):
                            ins = nc.tensor.matmul(route_ps[:, j * (E0 + 1):(j + 1) * (E0 + 1)], xnT[:, k, j * P:(j + 1) * P],
                                                   wr[:, k, :], start=(k == 0), stop=(k == KC - 1))
                    ins.then_inc(logit_s, 1)

                def gate_up(b, n):
                    pe.wait_ge(freed, FB0 * b.i + n + 1)
                    for w, col in ((wg, 0), (wu, T)):
                        for k in range(KC):
                            ins = nc.tensor.matmul(ffn_ps[n % 2][:, col:col + T], w[:, k, n * P:(n + 1) * P],
                                                   xnT[:, k, :], start=(k == 0), stop=(k == KC - 1))
                    ins.then_inc(gu_s, 1)

                def ranks(b):
                    pe.wait_ge(chosen_s, b.i + 1)
                    for r, parts in enumerate((((c.before, 0),), ((c.before, 1), (c.ones, 0)), ((c.ones, 0), (c.ones, 1)))):
                        for n, (lhs, j) in enumerate(parts):
                            ins = nc.tensor.matmul(route_ps[:, 32 + r * E0:32 + (r + 1) * E0], lhs[:], chosen[:, j, :],
                                                   start=(n == 0), stop=(n == len(parts) - 1))
                    ins.then_inc(rank_s, 1)

                def down(b, j):
                    pe.wait_ge(freed, FB0 * b.i + M0 + j + 1 + (j == 0))
                    for k in range(M0):
                        ins = nc.tensor.matmul(ffn_ps[j][:], hT[:, k, j * P:(j + 1) * P], wd[:, k, :],
                                               start=(k == 0), stop=(k == M0 - 1))
                    ins.then_inc(down_s, 1)

                def behind(one, two):
                    if one:
                        post_y(one)
                    if two:
                        gate_up(two, M0 - 1)
                        for j in range(TJ):
                            down(two, j)
                    if one:
                        post_xn(one)
                        logits(one)
                        for n in range(M0 - 1):
                            gate_up(one, n)
                            if n == 1:
                                ranks(one)

                def turn(b):
                    behind(not b.first and b.before(), b.third and b.before().before())
                    if not b.last:
                        pre(b.after())

                pre(FIRST)
                pe.wait_ge(weights_in, 5 * 16)
                turns(pe, B, turn)
                behind(LAST, LAST.before())
                behind(None, LAST)

            @block.scalar
            def _(act):
                def norm_pre(b):
                    wait(act, pre_tr, 4 * b.i - 2)
                    norm1.act(nc, act, b, k_tok, x[b.s])

                def pre(b):
                    if not b.first:
                        wait(act, y_done, b.i - 1)
                    for n, dst in enumerate((kT[b.s], vT[b.s])):
                        for j in range(TJ):
                            act.wait_ge(pre_tr, 4 * b.i + 2 * n + j + 1)
                            nc.scalar.copy(columns(dst, j), blocks(pre_ps[j])).then_inc(pre_ev, 1)

                def recurrence_exps(b):
                    act.wait_ge(wkv_c, WKV_STEPS * b.i + 5)
                    for k in range(KC):
                        nc.scalar.activation(a2[:, k, :], a2[:, k, :], ACT.Exp, bias=c.w[:, k:k + 1]).then_inc(exps, 1)
                    act.wait_ge(wkv_c, WKV_STEPS * b.i + 6)
                    nc.scalar.activation(e2[:], e2[:], ACT.Exp).then_inc(exps, 1)

                def bonus_exp(b, t, u, sign, made):
                    act.wait_ge(wkv_c, WKV_STEPS * b.i + 7)
                    wait(act, y_done, b.i)
                    for k in range(KC):
                        nc.scalar.activation(t[:, k, :], aq[:, k, :], ACT.Relu, bias=u[:, k:k + 1], scale=sign).then_inc(exps, 1)
                    act.wait_ge(exps, EXP_STEPS * b.i + made)
                    nc.scalar.activation(t[:], t[:], ACT.Exp, scale=-1.0).then_inc(exps, 1)

                def norm_post(b):
                    if not b.first:
                        wait(act, xn_out[1 - b.s], 16 * (b.before().round + 1))
                    norm2.act(nc, act, b, xn, x1[b.s])

                def post(b):
                    wait(act, gu_s, M0 * b.i)
                    for j in range(TJ):
                        act.wait_ge(xn_tr, 2 * b.i + j + 1)
                        nc.scalar.copy(columns(xnT, j), blocks(post_ps[j])).then_inc(xn_ev, 1)

                def gaps(b):
                    act.wait_ge(gap_s, b.i + 1)
                    nc.scalar.activation(tgap[:], gap[:], ACT.Tanh, scale=0.5).then_inc(tgap_s, 1)

                def tanh_gate(b, n):
                    act.wait_ge(gu_s, M0 * b.i + n + 1)
                    nc.scalar.activation(tg[n % 2][:], ffn_ps[n % 2][:, 0:T], ACT.Tanh, scale=0.5).then_inc(tg_s, 1)

                def turn(b):
                    if b.third:
                        tanh_gate(b.before().before(), M0 - 1)
                    recurrence_exps(b)
                    bonus_exp(b, em, c.u_neg, -1.0, 9)
                    bonus_exp(b, am, c.u, 1.0, 14)
                    if not b.first:
                        norm_post(b.before())
                        post(b.before())
                        tanh_gate(b.before(), 0)
                    if not b.last:
                        norm_pre(b.after())
                    if not b.first:
                        gaps(b.before())
                        for n in range(1, M0 - 1):
                            tanh_gate(b.before(), n)
                    if not b.last:
                        pre(b.after())

                norm_pre(FIRST)
                pre(FIRST)
                turns(act, B, turn)
                tanh_gate(LAST.before(), M0 - 1)
                norm_post(LAST)
                post(LAST)
                tanh_gate(LAST, 0)
                gaps(LAST)
                for n in range(1, M0):
                    tanh_gate(LAST, n)

            @block.gpsimd
            def _(pool):
                def enter(b):
                    pool.wait_ge(exps, EXP_STEPS * b.i + 5)
                    nc.gpsimd.tensor_tensor(e2v[:], e2[:], vT[b.s][:], ALU.mult).then_inc(products, 1)

                def bonus(b):
                    pool.wait_ge(exps, EXP_STEPS * b.i + 10)
                    nc.gpsimd.tensor_tensor(ev[:], em[:], vT[b.s][:], ALU.mult).then_inc(products, 1)

                def quotient(b):
                    pool.wait_ge(wkv_c, WKV_STEPS * b.i + 16)
                    nc.gpsimd.tensor_tensor(aq[:], aq[:], em[:], ALU.add).then_inc(products, 1)
                    pool.wait_ge(wkv_c, WKV_STEPS * b.i + 17)
                    pool.wait_ge(products, 4 * b.i + 2)
                    nc.gpsimd.tensor_tensor(am[:], am[:], ev[:], ALU.add).then_inc(products, 1)

                def scatter(b):
                    pool.wait_ge(pair_s, b.i + 1)
                    alone(pool)
                    for j in range(TJ):
                        for k in range(K0):
                            nc.gpsimd.indirect_dma_start(
                                io["list0"], bass.IndirectOffsetOnAxis(ap=pos[b.s][:, j, k:k + 1], axis=0),
                                pair[b.s][:, j, k, :], None).then_inc(scat[b.s], 16)

                def turn(b):
                    enter(b)
                    if not b.first:
                        norm2.pool(nc, pool, b.before())
                    bonus(b)
                    quotient(b)
                    if not b.last:
                        norm1.pool(nc, pool, b.after())
                    if b.third:
                        scatter(b.before().before())

                norm1.pool(nc, pool, FIRST)
                turns(pool, B, turn)
                norm2.pool(nc, pool, LAST)
                scatter(LAST.before())
                scatter(LAST)
                for s in range(2):
                    pool.wait_ge(scat[s], 16 * TJ * K0 * (B // 2))

            @block.vector
            def _(dve):
                steps, posts = Chain(dve, wkv_c, WKV_STEPS), Chain(dve, post_c, POST_STEPS0)
                v = nc.vector

                def recurrences(b):
                    steps.turn(b.i)
                    dve.wait_ge(pre_ev, 4 * b.i + 2)
                    for k in range(KC):
                        steps.did(v.tensor_tensor_scan(o[:, k, 1:], c.w[:, k:k + 1].to_broadcast([P, T]),
                                                       kT[b.s][:, k, :], BEFORE_ALL, ALU.add, ALU.max))
                    steps.need(4)
                    steps.did(v.tensor_tensor(a2[:], o[:, :, 0:T], o[:, :, 1:], ALU.subtract))
                    steps.did(v.tensor_tensor(e2[:], kT[b.s][:], o[:, :, 1:], ALU.subtract))

                def bonus_argument(b):
                    steps.did(v.tensor_tensor(aq[:], kT[b.s][:], o[:, :, 0:T], ALU.subtract))

                def sums(b):
                    dve.wait_ge(exps, EXP_STEPS * b.i + 5)
                    for k in range(KC):
                        steps.did(v.tensor_tensor_scan(q[:, k, 1:], a2[:, k, :], e2[:, k, :], 0.0, ALU.mult, ALU.add))

                def value_sums(b):
                    dve.wait_ge(products, 4 * b.i + 1)
                    for k in range(KC):
                        steps.did(v.tensor_tensor_scan(p[:, k, 1:], a2[:, k, :], e2v[:, k, :], 0.0, ALU.mult, ALU.add))

                def quotient(b):
                    dve.wait_ge(exps, EXP_STEPS * b.i + 15)
                    steps.need(11)
                    steps.did(v.tensor_tensor(aq[:], am[:], q[:, :, 0:T], ALU.mult))
                    steps.need(16)
                    steps.did(v.tensor_tensor(am[:], am[:], p[:, :, 0:T], ALU.mult))

                def divide(b):
                    dve.wait_ge(products, 4 * b.i + 3)
                    steps.did(v.reciprocal(aq[:], aq[:]))
                    steps.need(18)
                    dve.wait_ge(products, 4 * b.i + 4)
                    wait(dve, y_tr, 2 * b.i)
                    v.tensor_tensor(yT[:], am[:], aq[:], ALU.mult).then_inc(y_done, 1)

                def residual(b):
                    wait(dve, x2_out[b.s], 16 * b.round)
                    for j in range(TJ):
                        dve.wait_ge(y_tr, 2 * b.i + j + 1)
                        v.scalar_tensor_tensor(x1[b.s][:, j, :], post_ps[j][:], c.gate[:, 0:1], x[b.s][:, j, :],
                                               ALU.mult, ALU.add).then_inc(x1_s, 1)

                def norm_post(b):
                    dve.wait_ge(x1_s, TJ * (b.i + 1))
                    norm2.dve(nc, dve, b, x1[b.s])

                def route(b):
                    posts.turn(b.i)
                    dve.wait_ge(logit_s, b.i + 1)
                    posts.did(v.tensor_copy(lg[:].rearrange("p j e -> p (j e)"), route_ps[:, 0:TJ * (E0 + 1)]))
                    posts.need(1)
                    alone(dve)
                    for j in range(TJ):
                        posts.did(v.max(top[:, j, :], lg[:, j, 0:E0]))
                    posts.need(3)
                    alone(dve)
                    for j in range(TJ):
                        posts.did(v.max_index(at[:, j, :], top[:, j, :], lg[:, j, 0:E0]))
                    wait(dve, tgap_s, b.i)
                    posts.did(v.tensor_copy(gap[:, :, 1:2], lg[:, :, E0:]))
                    v.tensor_tensor(gap[:, :, 0:1], top[:, :, 0:1], top[:, :, 1:2], ALU.subtract).then_inc(gap_s, 1)
                    posts.need(5)
                    posts.did(v.tensor_copy(atf[:], at[:, :, 0:K0]))
                    posts.need(7)
                    posts.did(v.tensor_tensor(
                        hot[:].rearrange("p j k e -> p (j k) e"),
                        c.expert_no[:, 0:E0].unsqueeze(1).to_broadcast([P, TJ * K0, E0]),
                        atf[:].rearrange("p j k -> p (j k)").unsqueeze(2).to_broadcast([P, TJ * K0, E0]), ALU.is_equal))
                    posts.need(8)
                    wait(dve, rank_s, b.i)
                    v.tensor_tensor(chosen[:], hot[:, :, 0, :], hot[:, :, 1, :], ALU.add).then_inc(chosen_s, 1)

                def slots(b):
                    posts.resume(b.i)
                    dve.wait_ge(rank_s, b.i + 1)
                    wait(dve, scat[b.s], 16 * TJ * K0 * b.round)
                    slotted = posts.did(v.tensor_tensor(
                        slot[:], route_ps[:, 32:32 + TJ * E0].rearrange("p (j e) -> p j e", e=E0),
                        c.base0[:].unsqueeze(1).to_broadcast([P, TJ, E0]), ALU.add))
                    posts.did(v.tensor_copy(pair[b.s][:, :, :, 0], c.token_no[:].unsqueeze(2).to_broadcast([P, TJ, K0])))
                    for k in range(K0):
                        numbered = posts.did(v.tensor_scalar(pair[b.s][:, :, k, 1], c.token_no[:], float(k * N), None, ALU.add))
                    dve.wait_ge(tgap_s, b.i + 1)
                    for k, sign in enumerate((c.gate_half, c.gate_neg)):
                        posts.did(v.tensor_scalar(pair[b.s][:, :, k, 2].bitcast(F32), tgap[:, :, 0], sign[:, 2:3],
                                                  c.gate_half[:, 2:3], ALU.mult, ALU.add))
                    scaled = posts.did(v.tensor_scalar(ssc[:], tgap[:, :, 1], 1.0, c.gate_quarter[:, 2:3], ALU.add, ALU.mult))
                    posts.need(slotted)
                    for j in range(TJ):
                        picked = posts.did(v.tensor_tensor(pick[:, j], hot[:, j], slot[:, j, :].unsqueeze(1).to_broadcast([P, K0, E0]), ALU.mult))
                    posts.did(v.tensor_tensor(c.base0[:], c.base0[:], route_ps[:, 32 + TJ * E0:32 + (TJ + 1) * E0], ALU.add))
                    posts.need(numbered)
                    posts.did(v.tensor_scalar(c.token_no[:], c.token_no[:], float(T), None, ALU.add))
                    posts.need(picked)
                    summed = posts.did(v.tensor_reduce(posf[:].rearrange("p j k -> p (j k)"), pick[:].rearrange("p j k e -> p (j k) e"),
                                                       AX.X, ALU.add))
                    posts.need(summed)
                    v.tensor_copy(pos[b.s][:], posf[:]).then_inc(pair_s, 1)

                def hidden(b, n):
                    posts.resume(b.i)
                    dve.wait_ge(tg_s, M0 * b.i + n + 1)
                    s = n % 2
                    posts.did(v.scalar_tensor_tensor(sg[s][:], tg[s][:], 1.0, ffn_ps[s][:, 0:T], ALU.add, ALU.mult))
                    posts.need(posts.n)
                    if n == 0:
                        wait(dve, down_s, TJ * b.i)
                    v.tensor_tensor(hT[:, n, :], sg[s][:], ffn_ps[s][:, T:2 * T], ALU.mult).then_inc(freed, 1)

                def shared(b, j):
                    dve.wait_ge(down_s, TJ * b.i + j + 1)
                    v.scalar_tensor_tensor(x1[b.s][:, j, :], ffn_ps[j][:], ssc[:, j:j + 1], x1[b.s][:, j, :],
                                           ALU.mult, ALU.add).then_inc(freed, 1)

                def turn(b):
                    one, two = not b.first and b.before(), b.third and b.before().before()
                    recurrences(b)
                    if two:
                        hidden(two, M0 - 1)
                    bonus_argument(b)
                    if one:
                        residual(one)
                        norm_post(one)
                    sums(b)
                    if two:
                        slots(two)
                    value_sums(b)
                    if two:
                        shared(two, 0)
                    quotient(b)
                    if two:
                        shared(two, 1)
                    if not b.last:
                        after = b.after()
                        dve.wait_ge(x_in[after.s], 16 * (after.round + 1))
                        norm1.dve(nc, dve, after, x[after.s])
                    if one:
                        route(one)
                        hidden(one, 0)
                    divide(b)
                    if one:
                        for n in range(1, M0 - 1):
                            hidden(one, n)

                for t, value in ((o, BEFORE_ALL), (p, 0.0), (q, 0.0)):
                    v.memset(t[:, :, 0:1], value).then_inc(init_s, 1)
                dve.wait_ge(init_s, 3)
                v.engine_nop().then_inc(freed, 2)
                dve.wait_ge(x_in[0], 16)
                norm1.dve(nc, dve, FIRST, x[0])
                turns(dve, B, turn)
                residual(LAST)
                hidden(LAST.before(), M0 - 1)
                norm_post(LAST)
                slots(LAST.before())
                for j in range(TJ):
                    shared(LAST.before(), j)
                route(LAST)
                for n in range(2):
                    hidden(LAST, n)
                slots(LAST)
                for n in range(2, M0):
                    hidden(LAST, n)
                for j in range(TJ):
                    shared(LAST, j)


def routed0_phase(nc, io, c):
    with Memory(nc, "routed0_") as m:
        HW = H0 // P
        wgu = c.wgu0
        wdn = m.sb("wdn", [P, E0, HW, C])
        wdn_parts = [m.sb(f"wdn_{z}", [P, E0, HW, C], F32R) for z in ("high", "low")]
        nt, ends, zero8 = m.sb("expert_tiles", [P, E0]), m.sb("ends", [P, E0]), m.sb("zero8", [P, E0])
        count_i = m.sb("count_i", [P, E0], I32)
        past = m.sb("past", [P, TILES0, E0])
        past_nt = m.sb("past_nt", [P, TILES0, E0])
        expert, start, row = (m.sb(n, [P, TILES0]) for n in ("expert", "start", "row"))
        expert_i, row_i = m.sb("expert_i", [P, TILES0], I32), m.sb("row_i", [P, TILES0], I32)
        pair = [m.sb(f"pair_{s}", [P, 3], I32) for s in range(WAYS0)]
        xg = [m.sb(f"xg_{s}", [P, C]) for s in range(SLOTS0)]
        xT = [m.sb(f"xT_{s}", [P, KC, P]) for s in range(2)]
        sg, h = (m.sb(n, [P, H0]) for n in ("silu_gate", "h"))
        hT = [m.sb(f"hT_{z}", [P, H0], F32R) for z in ("high", "low")]
        ys = [m.sb(f"ys_{s}", [P, C]) for s in range(SLOTS0)]
        xt_ps = [m.ps(f"xt_ps{n}") for n in range(2)]
        gu_ps = [m.ps(f"gu_ps{n}") for n in range(2)]
        ht_ps = m.ps("ht_ps")
        y_ps = [m.ps(f"y_ps{n}") for n in range(2)]
        table = m.sem("table_steps")
        pair_in = [m.sem(f"pair_in{s}") for s in range(SLOTS0)]
        high_s, low_s, ht_high = m.sem("down_high"), m.sem("down_low"), m.sem("h_high")
        xg_in = [m.sem(f"rows_gathered{s}") for s in range(SLOTS0)]
        xt_s, xt_ev, gu_s = m.sem("x_transposed"), m.sem("x_evacuated"), m.sem("gate_up0")
        silu_s, h_s = m.sem("silu_done"), m.sem("h_done")
        ht_s, ht_ev, y_s, ys_s = m.sem("h_transposed"), m.sem("h_evacuated"), m.sem("y_ready"), m.sem("y_scaled")
        placed = [m.sem(f"rows_placed{s}") for s in range(SLOTS0)]
        with nc.Block() as block:
            def uses(t):
                return t.round * (WAYS0 // SLOTS0) + t.s // SLOTS0 + 1

            @block.sync
            def _(sp):
                for e in range(E0):
                    sp.dma_start(wdn[:, e], io["w_down0"][e].rearrange("(k p) n -> p k n", p=P)).then_inc(c.weights0_in, 16)
                sp.wait_ge(table, TABLE_STEPS0)

                def turn(t):
                    wait(sp, placed[t.s % SLOTS0], 16 * (uses(t) - WAYS0 // SLOTS0))
                    alone(sp)
                    wait(sp, pair_in[t.s % SLOTS0], 16 * (uses(t) - 1))
                    alone(sp)
                    at = sp.value_load(row_i[0:1, bass.ds(t.i, 1)], min_val=0, max_val=LIST0 - P)
                    sp.dma_start(pair[t.s][:], io["list0"][bass.ds(at, P), :]).then_inc(pair_in[t.s % SLOTS0], 16)

                turns(sp, TILES0, turn, WAYS0)

            @block.gpsimd
            def _(pool):
                def gather(t):
                    if not isinstance(t.i, int) or t.i >= SLOTS0:
                        pool.wait_ge(xt_s, t.i - SLOTS0 + 1)
                        alone(pool)
                    pool.wait_ge(pair_in[t.s % SLOTS0], 16 * uses(t))
                    alone(pool)
                    nc.gpsimd.indirect_dma_start(xg[t.s % SLOTS0][:], None, io["xn0"],
                                                 bass.IndirectOffsetOnAxis(ap=pair[t.s][:, 0:1].bitcast(U32), axis=0)
                                                 ).then_inc(xg_in[t.s % SLOTS0], 16)

                def place(t):
                    pool.wait_ge(ys_s, t.i + 1)
                    alone(pool)
                    nc.gpsimd.indirect_dma_start(io["y0"], bass.IndirectOffsetOnAxis(ap=pair[t.s][:, 1:2].bitcast(U32), axis=0),
                                                 ys[t.s % SLOTS0][:], None, bounds_check=K0 * N - 1, oob_is_err=False).then_inc(placed[t.s % SLOTS0], 16)

                def turn(t):
                    if not isinstance(t.i, int) or t.i < TILES0 - AHEAD0:
                        for n in range(AHEAD0):
                            ahead = t.after() if n == 0 else ahead.after()
                        gather(ahead)
                    if not t.first:
                        place(t.before())

                ahead = first(TILES0, WAYS0)
                for n in range(AHEAD0):
                    gather(ahead)
                    ahead = ahead.after()
                turns(pool, TILES0, turn, WAYS0)
                place(last(TILES0, WAYS0))
                for s in range(SLOTS0):
                    pool.wait_ge(placed[s], 16 * (TILES0 // SLOTS0))

            @block.tensor
            def _(pe):
                def inputs(t):
                    pe.wait_ge(xg_in[t.s % SLOTS0], 16 * uses(t))
                    wait(pe, xt_ev, t.i - 1)
                    for k in range(KC):
                        ins = nc.tensor.transpose(blocks(xt_ps[t.s % 2])[:, k, :], xg[t.s % SLOTS0][:, k * P:(k + 1) * P], c.ident[:])
                    ins.then_inc(xt_s, 1)

                def expert_of(t):
                    return pe.value_load(expert_i[0:1, bass.ds(t.i, 1)], min_val=0, max_val=E0 - 1)

                def gate_up(t, e):
                    pe.wait_ge(xt_ev, t.i + 1)
                    wait(pe, h_s, t.i - 1)
                    alone(pe)
                    for k in range(KC):
                        ins = nc.tensor.matmul(gu_ps[t.s % 2][:], xT[t.s % 2][:, k, :],
                                               wgu[:, bass.ds(e, 1), k, :].rearrange("p a n -> p (a n)"),
                                               start=(k == 0), stop=(k == KC - 1))
                    ins.then_inc(gu_s, 1)

                def hidden(t):
                    pe.wait_ge(h_s, t.i + 1)
                    wait(pe, ht_ev, t.i)
                    for k in range(HW):
                        ins = nc.tensor.transpose(ht_ps[:, k * P:(k + 1) * P], h[:, k * P:(k + 1) * P], c.ident[:])
                    ins.then_inc(ht_s, 1)

                def down(t, e):
                    pe.wait_ge(ht_ev, t.i + 1)
                    if t.first:
                        pe.wait_ge(low_s, E0)
                    wait(pe, ys_s, t.i)
                    alone(pe)
                    for k in range(HW):
                        ins = product(nc, y_ps[t.s % 2][:], [part[:, k * P:(k + 1) * P] for part in hT],
                                      [w[:, bass.ds(e, 1), k, :].rearrange("p a n -> p (a n)") for w in wdn_parts],
                                      k == 0, k == HW - 1)
                    ins.then_inc(y_s, 1)

                def turn(t):
                    e = expert_of(t)
                    last_e = None if t.first else expert_of(t.before())
                    if not t.last:
                        inputs(t.after())
                    if not t.first:
                        hidden(t.before())
                    gate_up(t, e)
                    if not t.first:
                        down(t.before(), last_e)

                pe.wait_ge(table, TABLE_STEPS0)
                inputs(first(TILES0, WAYS0))
                turns(pe, TILES0, turn, WAYS0)
                hidden(last(TILES0, WAYS0))
                down(last(TILES0, WAYS0), expert_of(last(TILES0, WAYS0)))

            @block.scalar
            def _(act):
                def inputs(t):
                    act.wait_ge(xt_s, t.i + 1)
                    wait(act, gu_s, t.i - 1)
                    nc.scalar.copy(xT[t.s % 2][:].rearrange("p k t -> p (k t)"), xt_ps[t.s % 2][:]).then_inc(xt_ev, 1)

                def hidden(t):
                    act.wait_ge(ht_s, t.i + 1)
                    wait(act, y_s, t.i)
                    nc.scalar.copy(hT[0][:], ht_ps[:, 0:H0]).then_inc(ht_high, 1)

                def turn(t):
                    if not t.last:
                        inputs(t.after())
                    if t.first:
                        act.wait_ge(c.weights0_in, 16 * 3 * E0)
                        for e in range(E0):
                            nc.scalar.copy(wdn_parts[0][:, e], wdn[:, e]).then_inc(high_s, 1)
                    else:
                        hidden(t.before())
                    act.wait_ge(gu_s, t.i + 1)
                    wait(act, h_s, t.i)
                    nc.scalar.activation(sg[:], gu_ps[t.s % 2][:, 0:H0], ACT.Silu).then_inc(silu_s, 1)

                inputs(first(TILES0, WAYS0))
                turns(act, TILES0, turn, WAYS0)
                hidden(last(TILES0, WAYS0))

            @block.vector
            def _(dve):
                v = nc.vector
                made = [0]

                def link(ins):
                    made[0] += 1
                    ins.then_inc(table, 1)
                    dve.wait_ge(table, made[0])

                every = [P, TILES0, E0]
                link(v.tensor_scalar(nt[:], c.expert_no[:, 0:E0], -float(N), float(P - 1), ALU.mult, ALU.add))
                link(v.tensor_tensor(count_i[:], nt[:], c.base0[:], ALU.add))
                link(v.tensor_single_scalar(count_i[:], count_i[:], 7, ALU.logical_shift_right))
                link(v.tensor_copy(nt[:], count_i[:]))
                link(v.memset(zero8[:], 0.0))
                link(v.tensor_tensor_scan(ends[:], nt[:], zero8[:], 0.0, ALU.add, ALU.add))
                link(v.tensor_tensor(past[:], c.tile_no[:].unsqueeze(2).to_broadcast(every),
                                     ends[:].unsqueeze(1).to_broadcast(every), ALU.is_ge))
                link(v.tensor_reduce(expert[:], past[:], AX.X, ALU.add))
                link(v.tensor_tensor(past_nt[:], past[:], nt[:].unsqueeze(1).to_broadcast(every), ALU.mult))
                link(v.tensor_reduce(start[:], past_nt[:], AX.X, ALU.add))
                link(v.tensor_tensor(start[:], c.tile_no[:], start[:], ALU.subtract))
                link(v.tensor_scalar(row[:], expert[:], float(N), None, ALU.mult))
                link(v.scalar_tensor_tensor(row[:], start[:], float(P), row[:], ALU.mult, ALU.add))
                link(v.tensor_scalar(row_i[:], row[:], float(E0 * N), None, ALU.min))
                link(v.tensor_scalar(expert_i[:], expert[:], float(E0 - 1), None, ALU.min))
                assert made[0] == TABLE_STEPS0

                def hidden(t):
                    dve.wait_ge(silu_s, t.i + 1)
                    wait(dve, ht_s, t.i)
                    v.tensor_tensor(h[:], sg[:], gu_ps[t.s % 2][:, H0:], ALU.mult).then_inc(h_s, 1)

                def outputs(t):
                    dve.wait_ge(ht_high, t.i + 1)
                    alone(dve)
                    v.tensor_tensor(hT[1][:], ht_ps[:, 0:H0], hT[0][:], ALU.subtract).then_inc(ht_ev, 1)

                def scaled(t):
                    dve.wait_ge(y_s, t.i + 1)
                    wait(dve, placed[t.s % SLOTS0], 16 * (uses(t) - 1))
                    v.tensor_scalar(ys[t.s % SLOTS0][:], y_ps[t.s % 2][:], pair[t.s][:, 2:3].bitcast(F32), None, ALU.mult).then_inc(ys_s, 1)

                def turn(t):
                    if not t.first:
                        outputs(t.before())
                    hidden(t)
                    if not t.first:
                        scaled(t.before())

                for e in range(E0):
                    dve.wait_ge(high_s, e + 1)
                    v.tensor_tensor(wdn_parts[1][:, e], wdn[:, e], wdn_parts[0][:, e], ALU.subtract).then_inc(low_s, 1)
                turns(dve, TILES0, turn, WAYS0)
                outputs(last(TILES0, WAYS0))
                scaled(last(TILES0, WAYS0))


def attention_phase(nc, io, c):
    with Memory(nc, "attn_") as m:
        x = [m.sb(f"x_{s}", [P, TJ, C]) for s in range(2)]
        ctx = [m.sb(f"ctx_{s}", [P, TJ, C]) for s in range(2)]
        y0 = m.sb("y0", [P, K0, TJ, C])
        q_tok = m.sb("q_tok", [P, TJ, C])
        qT = [m.sb(f"qT_{s}", [P, KC, T]) for s in range(2)]
        kT = [m.sb(f"kT_{s}", [P, KC, T]) for s in range(2)]
        v1 = [m.sb(f"v1_{s}", [P, TJ, HEADS, D + 1]) for s in range(2)]
        nmax = [m.sb(f"nmax_{n}", [P, 2, TJ]) for n in range(2)]
        pr = [m.sb(f"pr_{n}", [P, 2, 3, P]) for n in range(2)]
        prT = [m.sb(f"prT_{n}", [P, 2, 3, P]) for n in range(2)]
        rden = m.sb("rden", [P, 4 * TJ])
        at = m.sb("at", [P, TJ, HEADS, D])
        x3 = [m.sb(f"x3_{s}", [P, TJ, C]) for s in range(2)]
        xn = m.sb("xn", [P, TJ, C])
        xnT = [m.sb(f"xnT_{z}", [P, KC, T], F32R) for z in ("high", "low")]
        tg = [m.sb(f"tanh_gate_{s}", [P, T]) for s in range(2)]
        sg = [m.sb(f"silu_gate_{s}", [P, T]) for s in range(2)]
        hT = [m.sb(f"hT_{z}", [P, M1, T], F32R) for z in ("high", "low")]
        wgu = [m.sb(f"wgu_{z}", [P, KC, 2 * S1], F32R) for z in ("high", "low")]
        wd = [m.sb(f"wd_{z}", [P, M1, C], F32R) for z in ("high", "low")]
        stage = [m.sb(f"stage_{n}", [P, 2 * S1]) for n in range(2)]
        wr = m.sb("wr", [P, KC, E1])
        nlmax = m.sb("nlmax", [P, TJ])
        es = m.sb("es", [P, TJ, E1])
        essum, esr = m.sb("essum", [P, TJ]), m.sb("esr", [P, TJ])
        top = m.sb("top", [P, TJ, 8])
        sel = m.sb("sel", [P, TJ, 8], U32)
        self_ = m.sb("self", [P, TJ, K1])
        hot = m.sb("hot", [P, TJ, K1, E1])
        chosen = m.sb("chosen", [P, TJ, E1], BF16)
        limit = m.sb("limit", [P, E1])
        slot, over = m.sb("slot", [P, TJ, E1]), m.sb("over", [P, TJ, E1])
        pick = m.sb("pick", [P, TJ, K1, E1])
        posf = m.sb("posf", [P, TJ, K1])
        pos = [m.sb(f"pos_{s}", [P, TJ, K1], U32) for s in range(2)]
        pair = [m.sb(f"pair_{s}", [P, TJ, K1, 2], I32) for s in range(2)]
        tok = m.sb("tok", [P, TJ])
        score_ps = m.ps("score_ps", [P, 2, 512])
        tr_ps = [m.ps(f"tr_ps{n}") for n in range(2)]
        out_ps = m.ps("out_ps")
        ffn_ps = [m.ps(f"ffn_ps{n}") for n in range(2)]
        route_ps = m.ps("route_ps")
        norm1, norm2 = Norm(m, c, "norm1"), Norm(m, c, "norm2")
        x_in = [m.sem(f"x_in{s}") for s in range(2)]
        merged = m.sem("routed_merged")
        ctx_in = [m.sem(f"ctx_in{s}") for s in range(2)]
        staged = [m.sem(f"weights_staged{n}") for n in range(2)]
        high_s, low_s = m.sem("weights_high"), m.sem("weights_low")
        weights_in, init_s, ones_s = m.sem("weights_in"), m.sem("bases_made"), m.sem("ones_made")
        vals_s, score_s, max_s, exp_s = m.sem("values_made"), m.sem("scores"), m.sem("maxima"), m.sem("exps")
        tr_s = [m.sem("bank0_transposed"), m.sem("bank1_transposed")]
        tr_ev = [m.sem("bank0_read"), m.sem("bank1_read")]
        pv_s, out_c, out_ev = m.sem("outputs"), m.sem("out_steps"), m.sem("outputs_read")
        xn_tr, xn_high = m.sem("xn_transposed"), m.sem("xn_high")
        x3_s, logit_s, chosen_s, rank_s = m.sem("x3_done"), m.sem("logits"), m.sem("chosen_done"), m.sem("ranks")
        nlmax_s, es_s = m.sem("logit_max"), m.sem("logit_exps")
        gu_s, tg_s, freed = m.sem("gate_up"), m.sem("tanh_of_gate"), m.sem("ffn_bank_read")
        down_s, pair_s, post_c = m.sem("down"), m.sem("pairs"), m.sem("dve_post_steps")
        scat = [m.sem(f"scattered{s}") for s in range(2)]
        xn_out = [m.sem(f"xn_out{s}") for s in range(2)]
        x3_out = [m.sem(f"x3_out{s}") for s in range(2)]
        with nc.Block() as block:
            def use(b, u):
                return USES * b.i + 2 + u + (0 if b.last else (u > PRE_AT) + (u > PRE_AT + 1))

            def use_pre(b, n):
                return n if b.first else use(b.before(), PRE_AT + n) + 1

            WHOLE, PARTS = S1 // P * P, KC + M1

            def weight_part(n):
                if n < KC:
                    return stage[n % 2][:], [w[:, n, :] for w in wgu]
                k = n - KC
                return stage[n % 2][0:width(k), 0:C], [w[0:width(k), k, :] for w in wd]

            def staged_by(n):
                return 16 * sum(4 if k < KC else 1 for k in range(n % 2, n + 1, 2))

            def width(n):
                return min(P, S1 - n * P)

            @block.sync
            def _(sp):
                def load(b):
                    if not b.first:
                        wait(sp, x3_s, b.i - 1)
                        alone(sp)
                    sp.dma_start(x[b.s][:], rows(io["x2"], b)).then_inc(x_in[b.s], 16)
                    wait(sp, merged, K0 * b.i)
                    alone(sp)
                    for k in range(K0):
                        sp.dma_start(y0[:, k], io["y0"][bass.ds(b.i * T + k * N, T), :].rearrange("(j p) c -> p j c", p=P)
                                     ).then_inc(x_in[b.s], 16)
                    if not b.first:
                        wait(sp, vals_s, b.i - 1)
                        alone(sp)
                        wait(sp, tr_s[0], use_pre(b.before(), 1))
                        alone(sp)
                        wait(sp, tr_s[1], use_pre(b.before(), 1))
                        alone(sp)
                    sp.dma_start(ctx[b.s][:], rows(io["ctx"], b)).then_inc(ctx_in[b.s], 16)

                def store(b):
                    sp.wait_ge(norm2.done_s, 2 * b.i + 2)
                    alone(sp)
                    sp.dma_start(rows(io["xn1"], b), xn[:]).then_inc(xn_out[b.s], 16)
                    if not b.last:
                        after = b.after()
                        if not after.last:
                            load(after.after())
                    sp.wait_ge(freed, 2 + FB1 * (b.i + 1))
                    alone(sp)
                    sp.dma_start(rows(io["out"], b), x3[b.s][:]).then_inc(x3_out[b.s], 16)

                def turn(b):
                    if not b.first:
                        store(b.before())

                load(FIRST)
                sp.dma_start(wr[:], io["gate_w1"].rearrange("(k p) n -> p k n", p=P)).then_inc(weights_in, 16)
                load(FIRST.after())
                for n in range(PARTS):
                    if n >= 2:
                        sp.wait_ge(high_s, n - 1)
                        sp.wait_ge(low_s, n - 1)
                    if n < KC:
                        for z, name in enumerate(("sw_gate", "sw_up")):
                            w = io[name][n * P:(n + 1) * P, :]
                            at0, at1 = z * WHOLE, 2 * WHOLE + z * (S1 - WHOLE)
                            sp.dma_start(stage[n % 2][:, at0:at0 + WHOLE], w[:, 0:WHOLE]).then_inc(staged[n % 2], 16)
                            sp.dma_start(stage[n % 2][:, at1:at1 + S1 - WHOLE], w[:, WHOLE:]).then_inc(staged[n % 2], 16)
                    else:
                        k = n - KC
                        sp.dma_start(stage[n % 2][0:width(k), 0:C], io["sw_down"][k * P:k * P + width(k), :]).then_inc(staged[n % 2], 16)
                turns(sp, B, turn)
                store(LAST)
                for s in range(2):
                    sp.wait_ge(xn_out[s], 16 * (B // 2))
                    sp.wait_ge(x3_out[s], 16 * (B // 2))

            @block.tensor
            def _(pe):
                def to_channels(src, n):
                    for j in range(TJ):
                        wait(pe, tr_ev[j], n)
                        for k in range(KC):
                            ins = nc.tensor.transpose(blocks(tr_ps[j])[:, k, :], src[:, j, k * P:(k + 1) * P], c.ident[:])
                        ins.then_inc(tr_s[j], 1)

                def pre(b, n):
                    if n == 0:
                        pe.wait_ge(norm1.done_s, 2 * b.i + 2)
                        to_channels(q_tok, use_pre(b, 0))
                    else:
                        pe.wait_ge(ctx_in[b.s], 16 * (b.round + 1))
                        to_channels(ctx[b.s], use_pre(b, 1))

                def ffn_inputs(b):
                    pe.wait_ge(norm2.done_s, 2 * b.i + 2)
                    for j in range(TJ):
                        pe.wait_ge(freed, FB1 * b.i + j + 1)
                        for k in range(KC):
                            ins = nc.tensor.transpose(blocks(ffn_ps[j])[:, k, :], xn[:, j, k * P:(k + 1) * P], c.ident[:])
                        ins.then_inc(xn_tr, 1)

                def scores(b, u):
                    if u == 0:
                        for j in range(TJ):
                            pe.wait_ge(tr_ev[j], use_pre(b, 1) + 1)
                    wait(pe, exp_s, 4 * (UNITS * b.i + u))
                    for a in range(2):
                        nc.tensor.matmul(score_ps[:, a, 0:3 * P], c.ident16[:], c.causal[:], start=True, stop=False)
                    for j in range(TJ):
                        for a in range(2):
                            h = 2 * u + a
                            r, k = h * D % P, h * D // P
                            ins = nc.tensor.matmul(score_ps[:, a, j * P:(2 * j + 1) * P], qT[b.s][r:r + D, k, j * P:(j + 1) * P],
                                                   kT[b.s][r:r + D, k, 0:(j + 1) * P], start=False, stop=(j == TJ - 1))
                    ins.then_inc(score_s, 1)

                def transpose(b, u):
                    n = use(b, u)
                    pe.wait_ge(exp_s, 4 * (UNITS * b.i + u + 1))
                    for z in range(6):
                        bank, col = z // 3, z % 3
                        if col == 0:
                            pe.wait_ge(tr_ev[bank], n)
                        ins = nc.tensor.transpose(tr_ps[bank][:, col * P:(col + 1) * P], pr[u % 2][:, z // 3, z % 3, :], c.ident[:])
                        if col == 2:
                            ins.then_inc(tr_s[bank], 1)

                def values(b, u):
                    for bank in range(2):
                        pe.wait_ge(tr_ev[bank], use(b, u) + 1)
                    if u == 0:
                        pe.wait_ge(vals_s, b.i + 1)
                    if u % 2 == 0:
                        wait(pe, out_ev, UNITS // 2 * b.i + u // 2)
                    for a in range(2):
                        h = 2 * u + a
                        for j in range(TJ):
                            at0 = ((h % 4) * TJ + j) * (D + 1)
                            for k in range(j + 1):
                                ins = nc.tensor.matmul(out_ps[:, at0:at0 + D + 1], prT[u % 2][:, a, j + k, :],
                                                       v1[b.s][:, k, h, :], start=(k == 0), stop=(k == j))
                    if u % 2:
                        ins.then_inc(pv_s, 1)

                def logits(b):
                    pe.wait_ge(freed, 2 + FB1 * b.i + TJ)
                    wait(pe, pair_s, b.i)
                    for j in range(TJ):
                        for k in range(KC):
                            for z in range(2):
                                ins = nc.tensor.matmul(route_ps[:, j * E1:(j + 1) * E1], xnT[z][:, k, j * P:(j + 1) * P].bitcast(F32),
                                                       wr[:, k, :], start=(k + z == 0), stop=(k + z == KC))
                    ins.then_inc(logit_s, 1)

                def gate_up(b, n):
                    pe.wait_ge(freed, FB1 * b.i + TJ + n + 1)
                    for col, at0 in ((0, n * P), (T, WHOLE + n * P)) if n < M1 - 1 else ((0, 2 * WHOLE),):
                        for k in range(KC):
                            ins = product(nc, ffn_ps[n % 2][:, col:col + T], [w[:, k, at0:at0 + P] for w in wgu],
                                          [x[:, k, :] for x in xnT], k == 0, k == KC - 1)
                    ins.then_inc(gu_s, 1)

                def ranks(b):
                    pe.wait_ge(chosen_s, b.i + 1)
                    for r, parts in enumerate((((c.before, 0),), ((c.before, 1), (c.ones, 0)), ((c.ones, 0), (c.ones, 1)))):
                        for n, (lhs, j) in enumerate(parts):
                            ins = nc.tensor.matmul(route_ps[:, (2 + r) * E1:(3 + r) * E1], lhs[:], chosen[:, j, :],
                                                   start=(n == 0), stop=(n == len(parts) - 1))
                    ins.then_inc(rank_s, 1)

                def down(b, j):
                    pe.wait_ge(freed, FB1 * b.i + TJ + M1 + j + 1 + (j == 0))
                    for k in range(M1):
                        ins = product(nc, ffn_ps[j][:], [h[0:width(k), k, j * P:(j + 1) * P] for h in hT],
                                      [w[0:width(k), k, :] for w in wd], k == 0, k == M1 - 1)
                    ins.then_inc(down_s, 1)

                def behind(b, u):
                    if u == 1:
                        if b.first:
                            pe.wait_ge(weights_in, 16)
                            pe.wait_ge(high_s, PARTS)
                            pe.wait_ge(low_s, PARTS)
                        logits(b)
                    if 0 < u <= M1:
                        gate_up(b, u - 1)
                    if u == (3 if b.last else 4):
                        ranks(b)

                def turn(b):
                    for u in range(UNITS):
                        transpose(b, u)
                        if u < UNITS - 1:
                            scores(b, u + 1)
                        elif not b.last:
                            scores(b.after(), 0)
                        if PRE_AT <= u < PRE_AT + 2 and not b.last:
                            pre(b.after(), u - PRE_AT)
                        if u == 0 and b.third:
                            down(b.before().before(), 1)
                        if not b.first:
                            behind(b.before(), u)
                        values(b, u)
                        if u == 0 and not b.first:
                            ffn_inputs(b.before())
                    if not b.first:
                        down(b.before(), 0)

                pe.wait_ge(ones_s, 2)
                for n in range(2):
                    pre(FIRST, n)
                scores(FIRST, 0)
                turns(pe, B, turn)
                down(LAST.before(), 1)
                ffn_inputs(LAST)
                for u in range(UNITS):
                    behind(LAST, u)
                for j in range(TJ):
                    down(LAST, j)

            @block.scalar
            def _(act):
                def emptied(b, n, dst, scale=1.0):
                    for j in range(TJ):
                        act.wait_ge(tr_s[j], n + 1)
                        nc.scalar.activation(columns(dst, j), blocks(tr_ps[j]), ACT.Copy, scale=scale).then_inc(tr_ev[j], 1)

                def norm_pre(b):
                    if not b.first:
                        act.wait_ge(tr_s[0], use_pre(b.before(), 0) + 1)
                        act.wait_ge(tr_s[1], use_pre(b.before(), 0) + 1)
                    norm1.act(nc, act, b, q_tok, x[b.s])

                def pre(b, n):
                    if n == 0:
                        if not b.first:
                            wait(act, score_s, UNITS * (b.i - 1))
                        emptied(b, use_pre(b, 0), qT[b.s], D ** -0.5)
                    else:
                        emptied(b, use_pre(b, 1), kT[b.s])

                def exps(b, u):
                    act.wait_ge(max_s, 2 * (UNITS * b.i + u + 1))
                    for a in range(2):
                        for j in range(TJ):
                            nc.scalar.activation(
                                pr[u % 2][:, a, j:2 * j + 1, :].rearrange("p k t -> p (k t)"),
                                score_ps[:, a, j * P:(2 * j + 1) * P],
                                ACT.Exp, bias=nmax[u % 2][:, a, j:j + 1]).then_inc(exp_s, 1)

                def probs(b, u):
                    act.wait_ge(tr_s[1], use(b, u) + 1)
                    nc.scalar.copy(prT[u % 2][:, 1].rearrange("p k t -> p (k t)"), tr_ps[1][:, 0:3 * P]).then_inc(tr_ev[1], 1)

                def norm_post(b):
                    if not b.first:
                        wait(act, xn_out[1 - b.s], 16 * (b.before().round + 1))
                    norm2.act(nc, act, b, xn, x3[b.s])

                def tanh_gate(b, n):
                    act.wait_ge(gu_s, M1 * b.i + n + 1)
                    nc.scalar.activation(tg[n % 2][0:width(n)], ffn_ps[n % 2][0:width(n), 0:T], ACT.Tanh, scale=0.5).then_inc(tg_s, 1)

                def logit_exps(b):
                    act.wait_ge(nlmax_s, b.i + 1)
                    for j in range(TJ):
                        nc.scalar.activation(es[:, j, :], route_ps[:, j * E1:(j + 1) * E1], ACT.Exp, bias=nlmax[:, j:j + 1],
                                             accum_out=essum[:, j:j + 1]).then_inc(es_s, 1)

                def ffn_inputs(b):
                    wait(act, gu_s, M1 * b.i)
                    for j in range(TJ):
                        act.wait_ge(xn_tr, TJ * b.i + j + 1)
                        nc.scalar.copy(columns(xnT[0], j), blocks(ffn_ps[j])).then_inc(xn_high, 1)

                def split_weights(u):
                    for n in range(2 * u, min(2 * u + 2, PARTS)):
                        act.wait_ge(staged[n % 2], staged_by(n))
                        w, (high, _) = weight_part(n)
                        nc.scalar.copy(high, w).then_inc(high_s, 1)

                def turn(b):
                    exps(b, 0)
                    for u in range(UNITS):
                        probs(b, u)
                        if u == 0 and not b.first:
                            norm_post(b.before())
                        if u < UNITS - 1:
                            exps(b, u + 1)
                        if b.first:
                            split_weights(u)
                        elif u == 0:
                            ffn_inputs(b.before())
                        if PRE_AT <= u < PRE_AT + 2 and not b.last:
                            pre(b.after(), u - PRE_AT)
                        if u == 2 and not b.first:
                            logit_exps(b.before())
                        if 0 < u <= M1 and not b.first:
                            tanh_gate(b.before(), u - 1)
                        if u == PRE_AT - 1 and not b.last:
                            norm_pre(b.after())

                norm_pre(FIRST)
                for n in range(2):
                    pre(FIRST, n)
                turns(act, B, turn)
                norm_post(LAST)
                ffn_inputs(LAST)
                logit_exps(LAST)
                for n in range(M1):
                    tanh_gate(LAST, n)

            @block.gpsimd
            def _(pool):
                def values(b):
                    pool.wait_ge(ctx_in[b.s], 16 * (b.round + 1))
                    if not b.first:
                        wait(pool, pv_s, UNITS // 2 * (b.i - 1))
                    alone(pool)
                    nc.gpsimd.tensor_copy(v1[b.s][:, :, :, 0:D], ctx[b.s][:].rearrange("p j (h d) -> p j h d", d=D)).then_inc(vals_s, 1)

                def merge(b):
                    pool.wait_ge(x_in[b.s], 16 * (1 + K0) * (b.round + 1))
                    for k in range(K0):
                        if k:
                            pool.wait_ge(merged, K0 * b.i + k)
                        nc.gpsimd.tensor_tensor(x[b.s][:], x[b.s][:], y0[:, k], ALU.add).then_inc(merged, 1)

                def scatter(b):
                    pool.wait_ge(pair_s, b.i + 1)
                    alone(pool)
                    for j in range(TJ):
                        for k in range(K1):
                            nc.gpsimd.indirect_dma_start(
                                io["list1"], bass.IndirectOffsetOnAxis(ap=pos[b.s][:, j, k:k + 1], axis=0),
                                pair[b.s][:, j, k, :], None, bounds_check=E1 * CAP - 1, oob_is_err=False).then_inc(scat[b.s], 16)

                def turn(b):
                    if not b.first:
                        norm2.pool(nc, pool, b.before())
                    if not b.last:
                        merge(b.after())
                        norm1.pool(nc, pool, b.after())
                        values(b.after())
                    if not b.first:
                        scatter(b.before())

                for s in range(2):
                    nc.gpsimd.memset(v1[s][:, :, :, D:], 1.0).then_inc(ones_s, 1)
                merge(FIRST)
                norm1.pool(nc, pool, FIRST)
                values(FIRST)
                turns(pool, B, turn)
                norm2.pool(nc, pool, LAST)
                scatter(LAST)
                for s in range(2):
                    pool.wait_ge(scat[s], 16 * TJ * K1 * (B // 2))

            @block.vector
            def _(dve):
                posts = Chain(dve, post_c, POST_STEPS1)
                v = nc.vector

                def norm_pre(b):
                    dve.wait_ge(merged, K0 * (b.i + 1))
                    norm1.dve(nc, dve, b, x[b.s])

                def maxima(b, u):
                    dve.wait_ge(score_s, UNITS * b.i + u + 1)
                    for j in range(TJ):
                        v.tensor_reduce(nmax[u % 2][:, :, j], score_ps[:, :, j * P:(2 * j + 1) * P],
                                        AX.X, ALU.max, negate=True).then_inc(max_s, 1)

                def probs(b, u):
                    dve.wait_ge(tr_s[0], use(b, u) + 1)
                    v.tensor_copy(prT[u % 2][:, 0].rearrange("p k t -> p (k t)"), tr_ps[0][:, 0:3 * P]).then_inc(tr_ev[0], 1)

                def outputs(b, g):
                    dve.wait_ge(pv_s, UNITS // 2 * b.i + g + 1)
                    o = out_ps[:, 0:4 * TJ * (D + 1)].rearrange("p (h j d) -> p j h d", j=TJ, d=D + 1)
                    r = rden[:].rearrange("p (j h) -> p j h", j=TJ)
                    v.reciprocal(r, o[:, :, :, D]).then_inc(out_c, 1)
                    dve.wait_ge(out_c, UNITS // 2 * b.i + g + 1)
                    v.tensor_tensor(at[:, :, 4 * g:4 * g + 4, :], o[:, :, :, 0:D],
                                    r.unsqueeze(3).to_broadcast([P, TJ, 4, D]), ALU.mult).then_inc(out_ev, 1)

                def residual(b):
                    dve.wait_ge(out_ev, UNITS // 2 * (b.i + 1))
                    wait(dve, x3_out[b.s], 16 * b.round)
                    v.scalar_tensor_tensor(x3[b.s][:].rearrange("p j c -> p (j c)"), at[:].rearrange("p j h d -> p (j h d)"),
                                           c.gate[:, 1:2], x[b.s][:].rearrange("p j c -> p (j c)"), ALU.mult, ALU.add).then_inc(x3_s, 1)
                    dve.wait_ge(x3_s, b.i + 1)
                    norm2.dve(nc, dve, b, x3[b.s])

                def logit_max(b):
                    dve.wait_ge(logit_s, b.i + 1)
                    v.tensor_reduce(nlmax[:], route_ps[:, 0:TJ * E1].rearrange("p (j e) -> p j e", j=TJ), AX.X, ALU.max,
                                    negate=True).then_inc(nlmax_s, 1)

                def route(b):
                    dve.wait_ge(es_s, TJ * (b.i + 1))
                    posts.need(posts.did(v.reciprocal(esr[:], essum[:])))
                    for j in range(TJ):
                        n = posts.did(v.tensor_scalar(es[:, j, :], es[:, j, :], esr[:, j:j + 1], None, ALU.mult))
                    posts.need(n)
                    alone(dve)
                    for j in range(TJ):
                        n = posts.did(v.max(top[:, j, :], es[:, j, :]))
                    posts.need(n)
                    alone(dve)
                    for j in range(TJ):
                        n = posts.did(v.max_index(sel[:, j, :], top[:, j, :], es[:, j, :]))
                    posts.need(n)
                    posts.did(v.tensor_copy(self_[:], sel[:, :, 0:K1]))

                def choose(b):
                    posts.need(posts.n)
                    for j in range(TJ):
                        n = posts.did(v.tensor_tensor(hot[:, j], c.expert_no[:].unsqueeze(1).to_broadcast([P, K1, E1]),
                                                      self_[:, j, :].unsqueeze(2).to_broadcast([P, K1, E1]), ALU.is_equal))
                    posts.need(n)
                    wait(dve, rank_s, b.i)
                    with nc.allow_low_precision(reason="each sum is 0 or 1"):
                        v.tensor_reduce(chosen[:], hot[:].rearrange("p j k e -> p j e k"), AX.X, ALU.add).then_inc(chosen_s, 1)

                def slots(b):
                    dve.wait_ge(rank_s, b.i + 1)
                    wait(dve, scat[b.s], 16 * TJ * K1 * b.round)
                    every = [P, TJ, E1]
                    n = posts.did(v.tensor_tensor(slot[:], route_ps[:, TJ * E1:2 * TJ * E1].rearrange("p (j e) -> p j e", e=E1),
                                                  c.base1[:].unsqueeze(1).to_broadcast(every), ALU.add))
                    posts.need(n)
                    posts.need(posts.did(v.tensor_tensor(over[:], slot[:], limit[:].unsqueeze(1).to_broadcast(every), ALU.is_ge)))
                    posts.need(posts.did(v.scalar_tensor_tensor(slot[:].rearrange("p j e -> p (j e)"), over[:].rearrange("p j e -> p (j e)"),
                                                                float(2 * E1 * CAP), slot[:].rearrange("p j e -> p (j e)"), ALU.mult, ALU.add)))
                    for j in range(TJ):
                        n = posts.did(v.tensor_tensor(pick[:, j], hot[:, j], slot[:, j, :].unsqueeze(1).to_broadcast([P, K1, E1]), ALU.mult))
                    numbered = posts.did(v.tensor_copy(pair[b.s][:, :, :, 0], tok[:].unsqueeze(2).to_broadcast([P, TJ, K1])))
                    posts.did(v.tensor_scalar(pair[b.s][:, :, :, 1].bitcast(F32), top[:, :, 0:K1], c.gate[:, 3:4], None, ALU.mult))
                    posts.did(v.tensor_tensor(c.base1[:], c.base1[:], route_ps[:, 2 * TJ * E1:(2 * TJ + 1) * E1], ALU.add))
                    posts.need(n)
                    n = posts.did(v.tensor_reduce(posf[:].rearrange("p j k -> p (j k)"), pick[:].rearrange("p j k e -> p (j k) e"),
                                                  AX.X, ALU.add))
                    posts.need(numbered)
                    posts.did(v.tensor_scalar(tok[:], tok[:], float(T), None, ALU.add))
                    posts.need(n)
                    v.tensor_copy(pos[b.s][:], posf[:]).then_inc(pair_s, 1)

                def hidden(b, n):
                    dve.wait_ge(tg_s, M1 * b.i + n + 1)
                    s, r = n % 2, width(n)
                    up = ffn_ps[s][0:P, T:2 * T] if n < M1 - 1 else ffn_ps[s][r:2 * r, 0:T]
                    posts.need(posts.did(v.scalar_tensor_tensor(sg[s][0:r], tg[s][0:r], 1.0, ffn_ps[s][0:r, 0:T], ALU.add, ALU.mult)))
                    posts.need(posts.did(v.tensor_tensor(sg[s][0:r], sg[s][0:r], up, ALU.mult)))
                    if n == 0:
                        wait(dve, down_s, TJ * b.i)
                    posts.need(posts.did(v.tensor_copy(hT[0][0:r, n, :], sg[s][0:r])))
                    v.tensor_tensor(hT[1][0:r, n, :], sg[s][0:r], hT[0][0:r, n, :], ALU.subtract).then_inc(freed, 1)

                def shared(b, j):
                    dve.wait_ge(down_s, TJ * b.i + j + 1)
                    v.scalar_tensor_tensor(x3[b.s][:, j, :], ffn_ps[j][:], c.gate_half[:, 3:4], x3[b.s][:, j, :],
                                           ALU.mult, ALU.add).then_inc(freed, 1)

                def ffn_inputs(b):
                    posts.turn(b.i)
                    for j in range(TJ):
                        dve.wait_ge(xn_high, TJ * b.i + j + 1)
                        v.tensor_tensor(columns(xnT[1], j), blocks(ffn_ps[j]), columns(xnT[0], j), ALU.subtract).then_inc(freed, 1)

                def split_weights(u):
                    for n in range(2 * u, min(2 * u + 2, PARTS)):
                        dve.wait_ge(high_s, n + 1)
                        w, (high, low) = weight_part(n)
                        v.tensor_tensor(low, w, high, ALU.subtract).then_inc(low_s, 1)

                def turn(b):
                    for u in range(UNITS):
                        probs(b, u)
                        if u < UNITS - 1:
                            maxima(b, u + 1)
                        elif not b.first:
                            hidden(b.before(), M1 - 1)
                        if u == 0 and b.third:
                            for j in range(TJ):
                                shared(b.before().before(), j)
                        if u == PRE_AT - 2 and not b.last:
                            norm_pre(b.after())
                        if b.first:
                            split_weights(u)
                        else:
                            if u == 0:
                                ffn_inputs(b.before())
                            elif u == 2:
                                logit_max(b.before())
                            elif u == 3:
                                route(b.before())
                            elif u == 4:
                                choose(b.before())
                            elif u == 5:
                                slots(b.before())
                            if 1 < u < M1 + 1:
                                hidden(b.before(), u - 2)
                        if u == UNITS - 1 and not b.last:
                            maxima(b.after(), 0)
                        if u % 2:
                            outputs(b, u // 2)
                    residual(b)

                v.engine_nop().then_inc(freed, 2)
                for ins in (v.tensor_scalar(c.base1[:], c.expert_no[:], float(CAP), None, ALU.mult),
                            v.tensor_scalar(limit[:], c.expert_no[:], float(CAP), float(CAP), ALU.mult, ALU.add),
                            v.tensor_scalar(tok[:], c.token_no[:], -float(N), None, ALU.add)):
                    ins.then_inc(init_s, 1)
                dve.wait_ge(init_s, 3)
                norm_pre(FIRST)
                maxima(FIRST, 0)
                turns(dve, B, turn)
                for j in range(TJ):
                    shared(LAST.before(), j)
                ffn_inputs(LAST)
                logit_max(LAST)
                route(LAST)
                choose(LAST)
                for n in range(2):
                    hidden(LAST, n)
                slots(LAST)
                for n in range(2, M1):
                    hidden(LAST, n)
                for j in range(TJ):
                    shared(LAST, j)


def routed1_phase(nc, io, c):
    with Memory(nc, "routed1_") as m:
        HW = -(-H1 // P)
        FULL = H1 // P
        REST = H1 - FULL * P
        wgu = [m.sb(f"wgu_{s}", [P, 2, KC, H1]) for s in range(SLOTS1)]
        wdn = [m.sb(f"wdn_{s}", [P, HW, C]) for s in range(SLOTS1)]
        wgu_high = [m.sb(f"wgu_high_{s}", [P, 2, KC, H1], F32R) for s in range(SLOTS1)]
        wgu_low = [m.sb(f"wgu_low_{s}", [P, 2, KC, H1], F32R) for s in range(2)]
        wdn_high = [m.sb(f"wdn_high_{s}", [P, HW, C], F32R) for s in range(SLOTS1)]
        wdn_low = [m.sb(f"wdn_low_{s}", [P, HW, C], F32R) for s in range(2)]
        pair = [m.sb(f"pair_{s}", [CAP, 2], I32) for s in range(WAYS1)]
        xg = [m.sb(f"xg_{s}", [CAP, C]) for s in range(SLOTS1)]
        xT = [[m.sb(f"xT_{z}_{s}", [P, KC, CAP], F32R) for z in ("high", "low")] for s in range(2)]
        sg = m.sb("silu_gate", [CAP, H1])
        h = m.sb("h", [CAP, HW * P])
        hT = [m.sb(f"hT_{z}", [P, HW, CAP], F32R) for z in ("high", "low")]
        ys = [m.sb(f"ys_{s}", [CAP, C]) for s in range(2)]
        xt_ps, ht_ps = m.ps("xt_ps"), m.ps("ht_ps")
        gate_ps = [m.ps(f"gate_ps{n}") for n in range(2)]
        up_ps = [m.ps(f"up_ps{n}") for n in range(2)]
        y_ps = [m.ps(f"y_ps{n}") for n in range(2)]
        up_in = [m.sem(f"gate_up_in{s}") for s in range(SLOTS1)]
        down_in = [m.sem(f"down_in{s}") for s in range(SLOTS1)]
        pair_in = [m.sem(f"pair_in{s}") for s in range(SLOTS1)]
        xg_in = [m.sem(f"rows_gathered{s}") for s in range(SLOTS1)]
        added = [m.sem(f"rows_added{s}") for s in range(SLOTS1)]
        up_high, up_low = m.sem("gate_up_high"), m.sem("gate_up_low")
        down_high, down_low, down_low_whole = m.sem("down_high"), m.sem("down_low"), m.sem("down_low_whole")
        xt_s, xt_high, xt_ev = m.sem("x_transposed"), m.sem("x_high"), m.sem("x_evacuated")
        ht_s, ht_high, ht_ev = m.sem("h_transposed"), m.sem("h_high"), m.sem("h_evacuated")
        gu_s, silu_s, h_s = m.sem("gate_up"), m.sem("silu_done"), m.sem("h_done")
        y_s, ys_s, zeros_s = m.sem("y_ready"), m.sem("y_scaled"), m.sem("zeros_made")
        with nc.Block() as block:
            def of(name, e):
                return io[name][bass.ds(e, 1)].rearrange("a r n -> (a r) n")

            def uses(e):
                return e.round * (WAYS1 // SLOTS1) + e.s // SLOTS1 + 1

            @block.sync
            def _(sp):
                def turn(e):
                    wait(sp, added[e.s % SLOTS1], 16 * (uses(e) - WAYS1 // SLOTS1))
                    alone(sp)
                    wait(sp, pair_in[e.s % SLOTS1], 16 * (uses(e) - 1))
                    alone(sp)
                    sp.dma_start(pair[e.s][:], io["list1"][bass.ds(e.i * CAP, CAP), :]).then_inc(pair_in[e.s % SLOTS1], 16)
                    used = not isinstance(e.i, int) or e.i >= SLOTS1
                    slot = e.s % SLOTS1
                    if used:
                        sp.wait_ge(up_high, e.i - SLOTS1 + 1)
                        alone(sp)
                        sp.wait_ge(up_low, e.i - SLOTS1 + 1)
                        alone(sp)
                    last = e.before()
                    if not e.first:
                        sp.wait_ge(up_in[last.s % SLOTS1], 32 * uses(last))
                        alone(sp)
                    for n, name in enumerate(("w_gate1", "w_up1")):
                        sp.dma_start(wgu[slot][:, n], of(name, e.i).rearrange("(k p) n -> p k n", p=P)).then_inc(up_in[slot], 16)
                    if used:
                        sp.wait_ge(down_high, 2 * (e.i - SLOTS1 + 1))
                        alone(sp)
                        sp.wait_ge(down_low, e.i - SLOTS1 + 1)
                        alone(sp)
                        sp.wait_ge(down_low_whole, e.i - SLOTS1 + 1)
                        alone(sp)
                    if not e.first:
                        sp.wait_ge(down_in[last.s % SLOTS1], 32 * uses(last))
                        alone(sp)
                    w = of("w_down1", e.i)
                    sp.dma_start(wdn[slot][:, 0:FULL, :], w[0:FULL * P, :].rearrange("(k p) n -> p k n", p=P)).then_inc(down_in[slot], 16)
                    sp.dma_start(wdn[slot][0:REST, FULL, :], w[FULL * P:, :]).then_inc(down_in[slot], 16)

                rounds(sp, E1, turn, WAYS1)

            @block.gpsimd
            def _(pool):
                def rows_of(e):
                    return bass.IndirectOffsetOnAxis(ap=pair[e.s][:, 0:1].bitcast(U32), axis=0)

                def gather(e):
                    if not isinstance(e.i, int) or e.i >= SLOTS1:
                        pool.wait_ge(xt_s, e.i - SLOTS1 + 1)
                        alone(pool)
                    pool.wait_ge(pair_in[e.s % SLOTS1], 16 * uses(e))
                    alone(pool)
                    nc.gpsimd.indirect_dma_start(xg[e.s % SLOTS1][:], None, io["xn1"], rows_of(e)).then_inc(xg_in[e.s % SLOTS1], 16)

                def add(e):
                    pool.wait_ge(ys_s, e.i + 1)
                    alone(pool)
                    if not e.first:
                        pool.wait_ge(added[e.before().s % SLOTS1], 16 * uses(e.before()))
                        alone(pool)
                    nc.gpsimd.indirect_dma_start(io["out"], rows_of(e), ys[e.s % 2][:], None,
                                                 compute_op=ALU.add).then_inc(added[e.s % SLOTS1], 16)

                def low(e):
                    pool.wait_ge(down_high, 2 * e.i + 1)
                    wait(pool, y_s, e.i - 1)
                    alone(pool)
                    nc.gpsimd.tensor_tensor(wdn_low[e.s % 2][:, 0:FULL, :], wdn[e.s % SLOTS1][:, 0:FULL, :],
                                            wdn_high[e.s % SLOTS1][:, 0:FULL, :], ALU.subtract).then_inc(down_low_whole, 1)

                def turn(e):
                    low(e)
                    if not e.first:
                        add(e.before())
                    if not isinstance(e.i, int) or e.i < E1 - AHEAD1:
                        ahead = e
                        for _ in range(AHEAD1):
                            ahead = ahead.after()
                        gather(ahead)

                ahead = first(E1, WAYS1)
                for n in range(AHEAD1):
                    gather(ahead)
                    ahead = ahead.after()
                turns(pool, E1, turn, WAYS1)
                add(last(E1, WAYS1))
                for s in range(SLOTS1):
                    pool.wait_ge(added[s], 16 * (E1 // SLOTS1))

            @block.tensor
            def _(pe):
                def inputs(e):
                    pe.wait_ge(xg_in[e.s % SLOTS1], 16 * uses(e))
                    wait(pe, xt_ev, e.i)
                    alone(pe)
                    for k in range(KC):
                        ins = nc.tensor.transpose(xt_ps[:, k * CAP:(k + 1) * CAP], xg[e.s % SLOTS1][:, k * P:(k + 1) * P],
                                                  c.ident[0:CAP, 0:CAP])
                    ins.then_inc(xt_s, 1)

                def gate_up(e):
                    pe.wait_ge(xt_ev, e.i + 1)
                    pe.wait_ge(up_low, e.i + 1)
                    wait(pe, h_s, e.i - 1)
                    weights = (wgu_high[e.s % SLOTS1], wgu_low[e.s % 2])
                    for n, bank in enumerate((gate_ps, up_ps)):
                        for k in range(KC):
                            ins = product(nc, bank[e.s % 2][0:CAP, 0:H1], [x[:, k, :] for x in xT[e.s % 2]],
                                          [w[:, n, k, :] for w in weights], k == 0, k == KC - 1)
                    ins.then_inc(gu_s, 1)

                def hidden(e):
                    pe.wait_ge(h_s, e.i + 1)
                    wait(pe, ht_ev, e.i)
                    alone(pe)
                    for k in range(HW):
                        ins = nc.tensor.transpose(ht_ps[:, k * CAP:(k + 1) * CAP], h[:, k * P:(k + 1) * P], c.ident[0:CAP, 0:CAP])
                    ins.then_inc(ht_s, 1)

                def down(e):
                    pe.wait_ge(ht_ev, e.i + 1)
                    pe.wait_ge(down_low, e.i + 1)
                    pe.wait_ge(down_low_whole, e.i + 1)
                    wait(pe, ys_s, e.i - 1)
                    weights = (wdn_high[e.s % SLOTS1], wdn_low[e.s % 2])
                    for k in range(HW):
                        r = min(P, H1 - k * P)
                        ins = product(nc, y_ps[e.s % 2][0:CAP, :], [t[0:r, k, :] for t in hT], [w[0:r, k, :] for w in weights],
                                      k == 0, k == HW - 1)
                    ins.then_inc(y_s, 1)

                def turn(e):
                    if not e.last:
                        inputs(e.after())
                    if not e.first:
                        hidden(e.before())
                    gate_up(e)
                    if not e.first:
                        down(e.before())

                inputs(first(E1, WAYS1))
                pe.wait_ge(zeros_s, 1)
                turns(pe, E1, turn, WAYS1)
                hidden(last(E1, WAYS1))
                down(last(E1, WAYS1))

            @block.scalar
            def _(act):
                def high_up(e):
                    act.wait_ge(up_in[e.s % SLOTS1], 32 * uses(e))
                    wait(act, gu_s, e.i - SLOTS1 + 1)
                    alone(act)
                    nc.scalar.copy(wgu_high[e.s % SLOTS1][:], wgu[e.s % SLOTS1][:]).then_inc(up_high, 1)

                def high_down(e):
                    act.wait_ge(down_in[e.s % SLOTS1], 32 * uses(e))
                    wait(act, y_s, e.i - SLOTS1 + 1)
                    alone(act)
                    nc.scalar.copy(wdn_high[e.s % SLOTS1][:, 0:FULL, :], wdn[e.s % SLOTS1][:, 0:FULL, :]).then_inc(down_high, 1)
                    nc.scalar.copy(wdn_high[e.s % SLOTS1][0:REST, FULL, :], wdn[e.s % SLOTS1][0:REST, FULL, :]).then_inc(down_high, 1)

                def inputs(e):
                    act.wait_ge(xt_s, e.i + 1)
                    wait(act, gu_s, e.i - 1)
                    nc.scalar.copy(xT[e.s % 2][0][:].rearrange("p k t -> p (k t)"), xt_ps[:, 0:KC * CAP]).then_inc(xt_high, 1)

                def hidden(e):
                    act.wait_ge(ht_s, e.i + 1)
                    wait(act, y_s, e.i)
                    nc.scalar.copy(hT[0][:].rearrange("p k t -> p (k t)"), ht_ps[:, 0:HW * CAP]).then_inc(ht_high, 1)

                def turn(e):
                    if not e.last:
                        inputs(e.after())
                    if not e.first:
                        hidden(e.before())
                    if not isinstance(e.i, int) or e.i < E1 - 2:
                        high_up(e.after().after())
                    act.wait_ge(gu_s, e.i + 1)
                    wait(act, h_s, e.i)
                    nc.scalar.activation(sg[:], gate_ps[e.s % 2][0:CAP, 0:H1], ACT.Silu).then_inc(silu_s, 1)
                    if not e.last:
                        high_down(e.after())

                high_up(first(E1, WAYS1))
                inputs(first(E1, WAYS1))
                high_up(first(E1, WAYS1).after())
                high_down(first(E1, WAYS1))
                turns(act, E1, turn, WAYS1)
                hidden(last(E1, WAYS1))

            @block.vector
            def _(dve):
                v = nc.vector

                def low_up(e):
                    dve.wait_ge(up_high, e.i + 1)
                    wait(dve, gu_s, e.i - 1)
                    alone(dve)
                    v.tensor_tensor(wgu_low[e.s % 2][:], wgu[e.s % SLOTS1][:], wgu_high[e.s % SLOTS1][:], ALU.subtract).then_inc(up_low, 1)

                def low_down(e):
                    dve.wait_ge(down_high, 2 * e.i + 2)
                    wait(dve, y_s, e.i - 1)
                    alone(dve)
                    v.tensor_tensor(wdn_low[e.s % 2][0:REST, FULL, :], wdn[e.s % SLOTS1][0:REST, FULL, :],
                                    wdn_high[e.s % SLOTS1][0:REST, FULL, :], ALU.subtract).then_inc(down_low, 1)

                def inputs(e):
                    dve.wait_ge(xt_high, e.i + 1)
                    alone(dve)
                    v.tensor_tensor(xT[e.s % 2][1][:].rearrange("p k t -> p (k t)"), xt_ps[:, 0:KC * CAP],
                                    xT[e.s % 2][0][:].rearrange("p k t -> p (k t)"), ALU.subtract).then_inc(xt_ev, 1)

                def hidden(e):
                    dve.wait_ge(ht_high, e.i + 1)
                    alone(dve)
                    v.tensor_tensor(hT[1][:].rearrange("p k t -> p (k t)"), ht_ps[:, 0:HW * CAP],
                                    hT[0][:].rearrange("p k t -> p (k t)"), ALU.subtract).then_inc(ht_ev, 1)

                def scaled(e):
                    dve.wait_ge(y_s, e.i + 1)
                    two = e.before().before()
                    if not isinstance(e.i, int) or e.i >= 2:
                        dve.wait_ge(added[two.s % SLOTS1], 16 * uses(two))
                    v.tensor_scalar(ys[e.s % 2][:], y_ps[e.s % 2][0:CAP, :], pair[e.s][:, 1:2].bitcast(F32), None,
                                    ALU.mult).then_inc(ys_s, 1)

                def turn(e):
                    if not e.last:
                        inputs(e.after())
                    if not e.first:
                        hidden(e.before())
                    if not e.last:
                        low_up(e.after())
                    dve.wait_ge(silu_s, e.i + 1)
                    wait(dve, ht_s, e.i)
                    v.tensor_tensor(h[:, 0:H1], sg[:], up_ps[e.s % 2][0:CAP, 0:H1], ALU.mult).then_inc(h_s, 1)
                    low_down(e)
                    if not e.first:
                        scaled(e.before())

                v.memset(h[:, H1:], 0.0).then_inc(zeros_s, 1)
                low_up(first(E1, WAYS1))
                inputs(first(E1, WAYS1))
                turns(dve, E1, turn, WAYS1)
                hidden(last(E1, WAYS1))
                scaled(last(E1, WAYS1))


class Constants:

    def __init__(self, m):
        self.ident = m.sb("ident", [P, P])
        self.ident16 = m.sb("ident16", [P, P], BF16)
        self.before = m.sb("before", [P, P], BF16)
        self.ones = m.sb("ones", [P, P], BF16)
        self.causal = m.sb("causal", [P, 3 * P], BF16)
        self.half_power = m.sb("half_power", [P, TJ])
        self.expert_no = m.sb("expert_no", [P, E1])
        self.token_no = m.sb("token_no", [P, TJ])
        self.tile_no = m.sb("tile_no", [P, TILES0])
        self.w, self.u, self.u_neg = m.sb("w", [P, KC]), m.sb("u", [P, KC]), m.sb("u_neg", [P, KC])
        self.gate = m.sb("gate", [P, 4])
        self.gate_half = m.sb("gate_half", [P, 4])
        self.gate_neg = m.sb("gate_neg", [P, 4])
        self.gate_quarter = m.sb("gate_quarter", [P, 4])
        self.base0 = m.sb("base0", [P, E0])
        self.base1 = m.sb("base1", [P, E1])


def build(nc, io):
    with Memory(nc, "") as m:
        c = Constants(m)
        with Memory(nc, "first_ffn_") as f:
            c.wgu0 = f.sb("wgu", [P, E0, KC, 2 * H0])
            c.weights0_in = f.sem("weights_in")
            for phase in (setup, wkv_phase, routed0_phase):
                phase(nc, io, c)
        for phase in (attention_phase, routed1_phase):
            phase(nc, io, c)


def laid_out(i):
    def turned(a):
        return np.ascontiguousarray(np.swapaxes(a, -1, -2))

    i = {k: np.ascontiguousarray(v) for k, v in i.items()}
    return {
        "x": i["x"].reshape(N, C), "ctx": i["ctx_2048"].reshape(N, C),
        "g_xattn": i["g_xattn"], "g_ffn": i["g_ffn"], "w": i["L0_xattn_w"], "u": i["L0_xattn_u"],
        "gate_w0": turned(i["L0_ffn_gate_w"]), "se_gate": turned(i["L0_ffn_se_gate_w"]),
        "sh_gate": turned(i["L0_ffn_sh_gate"]), "sh_up": turned(i["L0_ffn_sh_up"]),
        "sh_down": turned(i["L0_ffn_sh_down"]),
        "w_gate0": turned(i["L0_ffn_w_gate"]), "w_up0": turned(i["L0_ffn_w_up"]),
        "w_down0": turned(i["L0_ffn_w_down"]),
        "gate_w1": turned(i["L1_ffn_gate_w"]), "w_gate1": i["L1_ffn_w_gate"], "w_up1": i["L1_ffn_w_up"],
        "w_down1": i["L1_ffn_w_down"], "sw_gate": i["L1_ffn_sw_gate"], "sw_up": i["L1_ffn_sw_up"],
        "sw_down": i["L1_ffn_sw_down"],
    }


SCRATCH = {"x2": ((N, C), F32), "xn0": ((N + DUMMY, C), F32), "xn1": ((N + DUMMY, C), F32),
           "list0": ((LIST0, 3), I32), "y0": ((K0 * N, C), F32), "list1": ((E1 * CAP, 2), I32)}


def kernel(**inputs):
    import concourse.bacc as _bacc
    from concourse.bass_utils import run_bass_kernel_spmd as _run

    nc = _bacc.Bacc("TRN2", target_bir_lowering=False, num_devices=1)
    arrays = laid_out(inputs)
    io = {name: nc.dram_tensor(f"in_{name}", a.shape, mybir.dt.from_np(a.dtype), kind="ExternalInput").ap()
          for name, a in arrays.items()}
    io["out"] = nc.dram_tensor("out_0", (N + DUMMY, C), F32, kind="ExternalOutput").ap()
    for name, (shape, dt) in SCRATCH.items():
        io[name] = nc.dram_tensor(name, shape, dt, kind="Internal").ap()
    build(nc, io)
    r = _run(nc, [{f"in_{name}": a for name, a in arrays.items()}], core_ids=[0])
    return r.results[0]["out_0"][:N].reshape(B, T, C)
```
